# Optimizing a Trainium2 kernel written in Bass

```python
import numpy as np
import jax
import jax.numpy as jnp

def _softmax(x, axis=-1):
    return jax.nn.softmax(x, axis=axis)

def _gelu(x):
    return jax.nn.gelu(x, approximate=True)

def _silu(x):
    return jax.nn.silu(x)

def _sigmoid(x):
    return jax.nn.sigmoid(x)

def _layernorm(x, axis=-1, eps=1e-05):
    m = jnp.mean(x, axis=axis, keepdims=True)
    v = jnp.var(x, axis=axis, keepdims=True)
    return (x - m) / jnp.sqrt(v + eps)

def _scatter_add(tgt, idx, src, axis=0):
    return tgt.at[idx].add(src)

def _segment_sum(src, seg, n):
    return jax.ops.segment_sum(src, seg, n)
kernel_name = 'mk_macaron_d2_jaxref_r8_3252b5'

def setup_inputs(seed: int=0):
    np.random.seed(seed)
    _w = jnp.asarray

    def _L0_attn_setup():
        import jax, jax.numpy as jnp
        import numpy as np
        B, T, C = (2, 256, 128)
        NHEADS = 16
        HEAD_DIM = C // NHEADS
        THETA = 10000.0
        SCALE_BASE = 512.0
        GN_EPS = 1e-05

        def _rotate_half(x):
            x1 = x[..., 0::2]
            x2 = x[..., 1::2]
            return jnp.stack([-x2, x1], axis=-1).reshape(x.shape)

        def _rope_xpos(q, k, T):
            d = q.shape[-1]
            half = jnp.arange(0, d, 2, dtype=jnp.float32)
            inv_freq = 1.0 / THETA ** (half / d)
            t = jnp.arange(T, dtype=jnp.float32)
            freqs = t[:, None] * inv_freq[None, :]
            freqs = jnp.repeat(freqs, 2, axis=-1)
            scale_vec = (half + 0.4 * d) / (1.4 * d)
            power = (t - T // 2) / SCALE_BASE
            scale = scale_vec[None, :] ** power[:, None]
            scale = jnp.repeat(scale, 2, axis=-1)
            cos, sin = (jnp.cos(freqs), jnp.sin(freqs))
            q = q * (cos * scale) + _rotate_half(q) * (sin * scale)
            k = k * (cos / scale) + _rotate_half(k) * (sin / scale)
            return (q, k)

        def _decay_mask(T):
            gamma = 1.0 - 2.0 ** (-5.0 - jnp.arange(NHEADS, dtype=jnp.float32))
            idx = jnp.arange(T)
            diff = idx[:, None] - idx[None, :]
            causal = diff >= 0
            expn = jnp.where(causal, diff, 0).astype(jnp.float32)
            return jnp.where(causal[None], gamma[:, None, None] ** expn[None], 0.0)
        key = jax.random.key(seed)
        ks = jax.random.split(key, 4)
        s = 0.02
        return {'x': jax.random.normal(ks[0], (B, T, C), jnp.float32), 'w_qkv': jax.random.normal(ks[1], (3 * C, C), jnp.float32) * s, 'w_gated': jax.random.normal(ks[2], (C, C), jnp.float32) * s, 'w_proj': jax.random.normal(ks[3], (C, C), jnp.float32) * s, 'gn_weight': jnp.ones((C,), jnp.float32), 'gn_bias': jnp.zeros((C,), jnp.float32)}
    _L0_attn_in = _L0_attn_setup()

    def _L0_ffn_setup():
        import jax, jax.numpy as jnp
        import numpy as np
        N_EMBD = 128
        N_EXPERTS = 8
        TOP_K = 2
        CAPACITY_FACTOR = 1.25
        key = jax.random.key(seed)
        ks = jax.random.split(key, 8)
        B, T, C, E, H = (8, 256, N_EMBD, N_EXPERTS, 4 * N_EMBD)
        w = lambda k, shape: jax.random.normal(k, shape, jnp.float32) * 0.02
        return {'x': jax.random.normal(ks[0], (B, T, C), jnp.float32), 'rW1': w(ks[1], (C, H)), 'rb1': jnp.zeros((H,), jnp.float32), 'rW2': w(ks[2], (H, H)), 'rb2': jnp.zeros((H,), jnp.float32), 'rW3': w(ks[3], (H, E)), 'rb3': jnp.zeros((E,), jnp.float32), 'eW1': w(ks[4], (E, C, H)), 'eb1': jnp.zeros((E, H), jnp.float32), 'eW2': w(ks[5], (E, H, C)), 'eb2': jnp.zeros((E, C), jnp.float32)}
    _L0_ffn_in = _L0_ffn_setup()

    def _L1_attn_setup():
        import jax, jax.numpy as jnp
        import numpy as np
        DIM = 128
        HEADS = 16
        HEAD_DIM = DIM // HEADS
        key = jax.random.key(seed)
        k1, k2, k3 = jax.random.split(key, 3)
        B, N = (4, 256)
        x = jax.random.normal(k1, (B, N, DIM), dtype=jnp.float32)
        w_qkv = jax.random.normal(k2, (3 * DIM, DIM), dtype=jnp.float32) / np.sqrt(DIM)
        w_proj = jax.random.normal(k3, (DIM, DIM), dtype=jnp.float32) / np.sqrt(DIM)
        b_proj = jnp.zeros((DIM,), dtype=jnp.float32)
        return {'x': x, 'w_qkv': w_qkv, 'w_proj': w_proj, 'b_proj': b_proj}
    _L1_attn_in = _L1_attn_setup()

    def _L1_ffn_setup():
        import jax, jax.numpy as jnp
        import numpy as np
        D = 128
        H = 16
        HD = D // H
        E = 32
        ES = 128
        K = 4
        B, S = (2, 128)
        ROPE_BASE = 10000.0

        def _layernorm(x, g, b):
            m = x.mean(-1, keepdims=True)
            v = ((x - m) ** 2).mean(-1, keepdims=True)
            return (x - m) * jax.lax.rsqrt(v + 1e-05) * g + b

        def _forward(src, wq, wk, wv, wp, wo, ln1_g, ln1_b, ln2_g, ln2_b, sel_w, keys, values):
            Bs, Ss, Ds = src.shape
            scale = 1.0 / jnp.sqrt(jnp.array(HD, dtype=src.dtype))
            x = _layernorm(src, ln1_g, ln1_b)
            q = (x @ wq).reshape(Bs, Ss, H, HD)
            k = (x @ wk).reshape(Bs, Ss, H, HD)
            v = (x @ wv).reshape(Bs, Ss, H, HD)
            pos = jnp.arange(Ss - 1, -Ss, -1, dtype=src.dtype)
            inv_freq = 1.0 / ROPE_BASE ** (jnp.arange(0, Ds, 2, dtype=src.dtype) / Ds)
            ang = pos[:, None] * inv_freq[None, :]
            pe = jnp.concatenate([jnp.sin(ang), jnp.cos(ang)], axis=-1)
            p = (pe @ wp).reshape(2 * Ss - 1, H, HD)
            ac = jnp.einsum('bihd,bjhd->bhij', q, k)
            bd_full = jnp.einsum('bihd,phd->bhip', q, p)
            rel = jnp.arange(Ss)[:, None] - jnp.arange(Ss)[None, :] + (Ss - 1)
            bd = bd_full[:, :, jnp.arange(Ss)[:, None], rel]
            att = jax.nn.softmax((ac + bd) * scale, axis=-1)
            attn_out = jnp.einsum('bhij,bjhd->bihd', att, v).reshape(Bs, Ss, Ds) @ wo
            src = src + attn_out
            x2 = _layernorm(src, ln2_g, ln2_b)
            sel = jax.nn.sigmoid(x2 @ sel_w)
            scores, idx = jax.lax.top_k(sel, K)
            gate = (jax.nn.one_hot(idx, E, dtype=sel.dtype) * scores[..., None]).sum(-2)
            h = jax.nn.relu(jnp.einsum('bsd,edh->bseh', x2, keys))
            moe_out = jnp.einsum('bseh,ehd,bse->bsd', h, values, gate)
            return src + moe_out
        key = jax.random.key(seed)
        ks = jax.random.split(key, 10)
        std_scale = np.sqrt(2.0 / 18)
        w_std = std_scale / np.sqrt(D)
        return {'src': jax.random.normal(ks[0], (B, S, D), jnp.float32), 'wq': jax.random.normal(ks[1], (D, H * HD), jnp.float32) * w_std, 'wk': jax.random.normal(ks[2], (D, H * HD), jnp.float32) * w_std, 'wv': jax.random.normal(ks[3], (D, H * HD), jnp.float32) * w_std, 'wp': jax.random.normal(ks[4], (D, H * HD), jnp.float32) * w_std, 'wo': jax.random.normal(ks[5], (H * HD, D), jnp.float32) * w_std, 'ln1_g': jnp.ones((D,), jnp.float32), 'ln1_b': jnp.zeros((D,), jnp.float32), 'ln2_g': jnp.ones((D,), jnp.float32), 'ln2_b': jnp.zeros((D,), jnp.float32), 'sel_w': jax.random.normal(ks[6], (D, E), jnp.float32) / np.sqrt(D), 'keys': jax.random.normal(ks[7], (E, D, ES), jnp.float32) * w_std, 'values': jax.random.normal(ks[8], (E, ES, D), jnp.float32) * (std_scale / np.sqrt(ES))}
    _L1_ffn_in = _L1_ffn_setup()
    _d = {'L0_attn_x': _L0_attn_in['x'], 'L0_attn_w_qkv': _L0_attn_in['w_qkv'], 'L0_attn_w_gated': _L0_attn_in['w_gated'], 'L0_attn_w_proj': _L0_attn_in['w_proj'], 'L0_attn_gn_weight': _L0_attn_in['gn_weight'], 'L0_attn_gn_bias': _L0_attn_in['gn_bias'], 'L0_ffn_rW1': _L0_ffn_in['rW1'], 'L0_ffn_rb1': _L0_ffn_in['rb1'], 'L0_ffn_rW2': _L0_ffn_in['rW2'], 'L0_ffn_rb2': _L0_ffn_in['rb2'], 'L0_ffn_rW3': _L0_ffn_in['rW3'], 'L0_ffn_rb3': _L0_ffn_in['rb3'], 'L0_ffn_eW1': _L0_ffn_in['eW1'], 'L0_ffn_eb1': _L0_ffn_in['eb1'], 'L0_ffn_eW2': _L0_ffn_in['eW2'], 'L0_ffn_eb2': _L0_ffn_in['eb2'], 'L1_attn_w_qkv': _L1_attn_in['w_qkv'], 'L1_attn_w_proj': _L1_attn_in['w_proj'], 'L1_attn_b_proj': _L1_attn_in['b_proj'], 'L1_ffn_wq': _L1_ffn_in['wq'], 'L1_ffn_wk': _L1_ffn_in['wk'], 'L1_ffn_wv': _L1_ffn_in['wv'], 'L1_ffn_wp': _L1_ffn_in['wp'], 'L1_ffn_wo': _L1_ffn_in['wo'], 'L1_ffn_ln1_g': _L1_ffn_in['ln1_g'], 'L1_ffn_ln1_b': _L1_ffn_in['ln1_b'], 'L1_ffn_ln2_g': _L1_ffn_in['ln2_g'], 'L1_ffn_ln2_b': _L1_ffn_in['ln2_b'], 'L1_ffn_sel_w': _L1_ffn_in['sel_w'], 'L1_ffn_keys': _L1_ffn_in['keys'], 'L1_ffn_values': _L1_ffn_in['values']}
    _x0 = _d['L0_attn_x']
    _d['L0_attn_x'] = jax.random.normal(jax.random.fold_in(jax.random.key(seed), 1), (16, 256, 128), dtype=_x0.dtype)
    del _x0
    return _d

def reference(L0_attn_x, L0_attn_w_qkv, L0_attn_w_gated, L0_attn_w_proj, L0_attn_gn_weight, L0_attn_gn_bias, L0_ffn_rW1, L0_ffn_rb1, L0_ffn_rW2, L0_ffn_rb2, L0_ffn_rW3, L0_ffn_rb3, L0_ffn_eW1, L0_ffn_eb1, L0_ffn_eW2, L0_ffn_eb2, L1_attn_w_qkv, L1_attn_w_proj, L1_attn_b_proj, L1_ffn_wq, L1_ffn_wk, L1_ffn_wv, L1_ffn_wp, L1_ffn_wo, L1_ffn_ln1_g, L1_ffn_ln1_b, L1_ffn_ln2_g, L1_ffn_ln2_b, L1_ffn_sel_w, L1_ffn_keys, L1_ffn_values):

    def _L0_attn_ref(x, w_qkv, w_gated, w_proj, gn_weight, gn_bias):
        import jax, jax.numpy as jnp
        import numpy as np
        B, T, C = (2, 256, 128)
        NHEADS = 16
        HEAD_DIM = C // NHEADS
        THETA = 10000.0
        SCALE_BASE = 512.0
        GN_EPS = 1e-05

        def _rotate_half(x):
            x1 = x[..., 0::2]
            x2 = x[..., 1::2]
            return jnp.stack([-x2, x1], axis=-1).reshape(x.shape)

        def _rope_xpos(q, k, T):
            d = q.shape[-1]
            half = jnp.arange(0, d, 2, dtype=jnp.float32)
            inv_freq = 1.0 / THETA ** (half / d)
            t = jnp.arange(T, dtype=jnp.float32)
            freqs = t[:, None] * inv_freq[None, :]
            freqs = jnp.repeat(freqs, 2, axis=-1)
            scale_vec = (half + 0.4 * d) / (1.4 * d)
            power = (t - T // 2) / SCALE_BASE
            scale = scale_vec[None, :] ** power[:, None]
            scale = jnp.repeat(scale, 2, axis=-1)
            cos, sin = (jnp.cos(freqs), jnp.sin(freqs))
            q = q * (cos * scale) + _rotate_half(q) * (sin * scale)
            k = k * (cos / scale) + _rotate_half(k) * (sin / scale)
            return (q, k)

        def _decay_mask(T):
            gamma = 1.0 - 2.0 ** (-5.0 - jnp.arange(NHEADS, dtype=jnp.float32))
            idx = jnp.arange(T)
            diff = idx[:, None] - idx[None, :]
            causal = diff >= 0
            expn = jnp.where(causal, diff, 0).astype(jnp.float32)
            return jnp.where(causal[None], gamma[:, None, None] ** expn[None], 0.0)
        Bx, Tx, Cx = x.shape
        qkv = x @ w_qkv.T
        q, k, v = jnp.split(qkv, 3, axis=-1)

        def to_heads(u):
            return u.reshape(Bx, Tx, NHEADS, HEAD_DIM).transpose(0, 2, 1, 3)
        q, k, v = (to_heads(q), to_heads(k), to_heads(v))
        q, k = _rope_xpos(q, k, Tx)
        mask = _decay_mask(Tx)
        scores = jnp.einsum('bhtd,bhsd->bhts', q, k) * HEAD_DIM ** (-0.5)
        scores = scores * mask[None]
        y = jnp.einsum('bhts,bhsd->bhtd', scores, v)
        y = y.transpose(0, 2, 1, 3).reshape(Bx, Tx, Cx)
        yt = y.transpose(0, 2, 1).reshape(Bx, NHEADS, HEAD_DIM, Tx)
        mean = yt.mean(axis=(2, 3), keepdims=True)
        var = yt.var(axis=(2, 3), keepdims=True)
        yn = (yt - mean) / jnp.sqrt(var + GN_EPS)
        yn = yn.reshape(Bx, Cx, Tx)
        yn = yn * gn_weight[None, :, None] + gn_bias[None, :, None]
        yn = yn.transpose(0, 2, 1)
        out = jax.nn.silu(x @ w_gated.T) * yn
        return out @ w_proj.T

    def _L0_ffn_ref(x, rW1, rb1, rW2, rb2, rW3, rb3, eW1, eb1, eW2, eb2):
        import jax, jax.numpy as jnp
        import numpy as np
        N_EMBD = 128
        N_EXPERTS = 8
        TOP_K = 2
        CAPACITY_FACTOR = 1.25
        B, T, C = x.shape
        E = rb3.shape[0]
        k = TOP_K
        capacity = int(T / E * CAPACITY_FACTOR)
        h = jax.nn.relu(x @ rW1 + rb1)
        h = jax.nn.relu(h @ rW2 + rb2)
        scales = jax.nn.softmax(h @ rW3 + rb3, axis=-1)
        topk_scales, topk_experts = jax.lax.top_k(scales, k)
        e_flat = topk_experts.reshape(B, T * k)
        onehot = jax.nn.one_hot(e_flat, E, dtype=jnp.int32)
        pos_excl = jnp.cumsum(onehot, axis=1) - onehot
        pos = jnp.take_along_axis(pos_excl, e_flat[..., None], axis=-1)[..., 0]
        keep = pos < capacity
        pos_c = jnp.where(keep, pos, capacity)
        b_idx = jnp.broadcast_to(jnp.arange(B)[:, None], (B, T * k))
        x_rep = jnp.repeat(x, k, axis=1)
        dispatched = jnp.zeros((E, B, capacity, C), x.dtype)
        dispatched = dispatched.at[e_flat, b_idx, pos_c].set(jnp.where(keep[..., None], x_rep, 0.0), mode='drop')
        hh = jax.nn.relu(jnp.einsum('ebnc,ech->ebnh', dispatched, eW1) + eb1[:, None, None, :])
        eout = jnp.einsum('ebnh,ehc->ebnc', hh, eW2) + eb2[:, None, None, :]
        gathered = eout[e_flat, b_idx, pos_c]
        gathered = jnp.where(keep[..., None], gathered, 0.0).reshape(B, T, k, C)
        out = jnp.sum(topk_scales[..., None] * gathered, axis=2)
        return out

    def _L1_attn_ref(x, w_qkv, w_proj, b_proj):
        import jax, jax.numpy as jnp
        import numpy as np
        DIM = 128
        HEADS = 16
        HEAD_DIM = DIM // HEADS
        B, N, C = x.shape
        scale = HEAD_DIM ** (-0.5)
        qkv = x @ w_qkv.T
        qkv = qkv.reshape(B, N, 3, HEADS, HEAD_DIM)
        q, k, v = (qkv[:, :, 0], qkv[:, :, 1], qkv[:, :, 2])
        q = q * scale
        attn = jnp.einsum('bnhd,bmhd->bhnm', q, k)
        attn = jax.nn.softmax(attn, axis=-1)
        out = jnp.einsum('bhnm,bmhd->bnhd', attn, v)
        out = out.reshape(B, N, C)
        return out @ w_proj.T + b_proj

    def _L1_ffn_ref(src, wq, wk, wv, wp, wo, ln1_g, ln1_b, ln2_g, ln2_b, sel_w, keys, values):
        import jax, jax.numpy as jnp
        import numpy as np
        D = 128
        H = 16
        HD = D // H
        E = 32
        ES = 128
        K = 4
        B, S = (2, 128)
        ROPE_BASE = 10000.0

        def _layernorm(x, g, b):
            m = x.mean(-1, keepdims=True)
            v = ((x - m) ** 2).mean(-1, keepdims=True)
            return (x - m) * jax.lax.rsqrt(v + 1e-05) * g + b

        def _forward(src, wq, wk, wv, wp, wo, ln1_g, ln1_b, ln2_g, ln2_b, sel_w, keys, values):
            Bs, Ss, Ds = src.shape
            scale = 1.0 / jnp.sqrt(jnp.array(HD, dtype=src.dtype))
            x = _layernorm(src, ln1_g, ln1_b)
            q = (x @ wq).reshape(Bs, Ss, H, HD)
            k = (x @ wk).reshape(Bs, Ss, H, HD)
            v = (x @ wv).reshape(Bs, Ss, H, HD)
            pos = jnp.arange(Ss - 1, -Ss, -1, dtype=src.dtype)
            inv_freq = 1.0 / ROPE_BASE ** (jnp.arange(0, Ds, 2, dtype=src.dtype) / Ds)
            ang = pos[:, None] * inv_freq[None, :]
            pe = jnp.concatenate([jnp.sin(ang), jnp.cos(ang)], axis=-1)
            p = (pe @ wp).reshape(2 * Ss - 1, H, HD)
            ac = jnp.einsum('bihd,bjhd->bhij', q, k)
            bd_full = jnp.einsum('bihd,phd->bhip', q, p)
            rel = jnp.arange(Ss)[:, None] - jnp.arange(Ss)[None, :] + (Ss - 1)
            bd = bd_full[:, :, jnp.arange(Ss)[:, None], rel]
            att = jax.nn.softmax((ac + bd) * scale, axis=-1)
            attn_out = jnp.einsum('bhij,bjhd->bihd', att, v).reshape(Bs, Ss, Ds) @ wo
            src = src + attn_out
            x2 = _layernorm(src, ln2_g, ln2_b)
            sel = jax.nn.sigmoid(x2 @ sel_w)
            scores, idx = jax.lax.top_k(sel, K)
            gate = (jax.nn.one_hot(idx, E, dtype=sel.dtype) * scores[..., None]).sum(-2)
            h = jax.nn.relu(jnp.einsum('bsd,edh->bseh', x2, keys))
            moe_out = jnp.einsum('bseh,ehd,bse->bsd', h, values, gate)
            return src + moe_out
        return _forward(src, wq, wk, wv, wp, wo, ln1_g, ln1_b, ln2_g, ln2_b, sel_w, keys, values)
    x = L0_attn_x
    x = x + 0.5 * _L0_ffn_ref(_layernorm(x, axis=-1), L0_ffn_rW1, L0_ffn_rb1, L0_ffn_rW2, L0_ffn_rb2, L0_ffn_rW3, L0_ffn_rb3, L0_ffn_eW1, L0_ffn_eb1, L0_ffn_eW2, L0_ffn_eb2)
    x = x + _L0_attn_ref(_layernorm(x, axis=-1), L0_attn_w_qkv, L0_attn_w_gated, L0_attn_w_proj, L0_attn_gn_weight, L0_attn_gn_bias)
    x = x + 0.5 * _L0_ffn_ref(_layernorm(x, axis=-1), L0_ffn_rW1, L0_ffn_rb1, L0_ffn_rW2, L0_ffn_rb2, L0_ffn_rW3, L0_ffn_rb3, L0_ffn_eW1, L0_ffn_eb1, L0_ffn_eW2, L0_ffn_eb2)
    x = x + 0.5 * _L1_ffn_ref(_layernorm(x, axis=-1), L1_ffn_wq, L1_ffn_wk, L1_ffn_wv, L1_ffn_wp, L1_ffn_wo, L1_ffn_ln1_g, L1_ffn_ln1_b, L1_ffn_ln2_g, L1_ffn_ln2_b, L1_ffn_sel_w, L1_ffn_keys, L1_ffn_values)
    x = x + _L1_attn_ref(_layernorm(x, axis=-1), L1_attn_w_qkv, L1_attn_w_proj, L1_attn_b_proj)
    x = x + 0.5 * _L1_ffn_ref(_layernorm(x, axis=-1), L1_ffn_wq, L1_ffn_wk, L1_ffn_wv, L1_ffn_wp, L1_ffn_wo, L1_ffn_ln1_g, L1_ffn_ln1_b, L1_ffn_ln2_g, L1_ffn_ln2_b, L1_ffn_sel_w, L1_ffn_keys, L1_ffn_values)
    return x

_drawn_inputs = setup_inputs


def setup_inputs(seed=0):
    import zlib

    import numpy as np

    out = dict(_drawn_inputs(seed))
    spreads = {'L0_attn_gn_weight': (1.0, 0.6),
     'L0_attn_gn_bias': (0.0, 0.8),
     'L0_ffn_rb1': (0.0, 0.8),
     'L0_ffn_rb2': (0.0, 0.64),
     'L0_ffn_rb3': (0.0, 0.444),
     'L0_ffn_eb1': (0.0, 0.8),
     'L0_ffn_eb2': (0.0, 0.68),
     'L1_attn_b_proj': (0.0, 0.1),
     'L1_ffn_ln1_g': (1.0, 0.6),
     'L1_ffn_ln1_b': (0.0, 0.764),
     'L1_ffn_ln2_g': (1.0, 0.6),
     'L1_ffn_ln2_b': (0.0, 0.833)}
    factors = {'L0_ffn_rW1': 6.618,
     'L0_ffn_rW2': 7.099,
     'L0_ffn_rW3': 5.445,
     'L0_ffn_eW1': 8.0,
     'L0_ffn_eW2': 6.38,
     'L1_ffn_wq': 8.0,
     'L1_ffn_wk': 8.0,
     'L1_ffn_wv': 5.166,
     'L1_ffn_wp': 8.0,
     'L1_ffn_wo': 5.029}
    for name, (base, spread) in spreads.items():
        noise = np.random.default_rng([zlib.crc32(name.encode()), seed]).standard_normal(out[name].shape)
        drawn = base * np.exp(spread * noise) if base else spread * noise
        out[name] = jnp.asarray(drawn.astype(out[name].dtype))
    for name, factor in factors.items():
        out[name] = (out[name] * factor).astype(out[name].dtype)
    return out
```

```python
from contextlib import ExitStack

import numpy as np

import concourse.bass as bass
from concourse import mybir

F32 = mybir.dt.float32
BF16 = mybir.dt.bfloat16
U32 = mybir.dt.uint32
ALU = mybir.AluOpType
ACT = mybir.ActivationFunctionType
AX = mybir.AxisListType

P = 128
B, T, C = 16, 256, 128
TT = T // P
H, HD = 16, 8
QUAD = 4
E0, HID, CAP = 8, 512, 40
KH = HID // P
E1, TOPK = 32, 4
EPS = 1e-5
SLOTS = 6
QSLOT = (0, 0, 1, 1, 0, 2)
KSLOT = (0, 1, 0, 1, 2, 0)


class Ring:

    def __init__(self, psum, filled, emptied, per, banks):
        self.psum, self.filled, self.emptied, self.per, self.banks = psum, filled, emptied, per, banks

    def nth(self, item, k):
        return item[0] * self.per + k + 1

    def bank(self, item, k):
        return self.psum[:, (item[1] * self.per + k) % self.banks, :]

    def done(self, item, k):
        return self.nth(item, k) + self.banks


class Pool_:

    def __init__(self, nc, ctx, tag):
        self.nc, self.ctx, self.tag, self.sems = nc, ctx, tag, []
        ctx.callback(self.clear)

    def clear(self):
        if self.sems:
            self.nc.clear_and_free_semaphores(self.sems)
            self.nc.all_engine_barrier()

    def sb(self, name, shape, dt=F32):
        return self.ctx.enter_context(self.nc.sbuf_tensor(f"{self.tag}_{name}", shape, dt))

    def ps(self, name, shape, dt=F32):
        return self.ctx.enter_context(self.nc.psum_tensor(f"{self.tag}_{name}", shape, dt))

    def sem(self, name):
        self.sems.append(self.nc.alloc_semaphore(f"{self.tag}_{name}"))
        return self.sems[-1]


def steps(eng, first, last, step, lead=1, trail=1):
    s = first
    while s < first + lead or (last - trail - s + 1) % 2:
        step((s, s % 2))
        s += 1
    pairs = (last - trail - s + 1) // 2
    base = s
    with eng.Fori(0, pairs) as p:
        for q in (0, 1):
            step((p * 2 + (base + q), (base + q) % 2), inner=True)
    for s in range(base + 2 * pairs, last + 1):
        step((s, s % 2))


def is_first(s, at=0):
    return isinstance(s, int) and s == at


def within(s, first, last):
    return not isinstance(s, int) or first <= s <= last


def before(item, n=1):
    return (item[0] - n, (item[1] + n) % 2)


def after(item):
    return (item[0] + 1, (item[1] + 1) % 2)


def routed_ffn(nc, tag, x_sb, k, w):
    G, GT, NB = B // 2, 4, 2
    S = E0 * CAP
    SW, NW = 2 * CAP, E0 // 2
    W = GT * P
    x_g = x_sb[:, :, :].rearrange("p (g t) c -> p g t c", t=GT)
    with ExitStack() as ctx:
        a = Pool_(nc, ctx, tag)
        xn = a.sb("xn", [P, 2, GT, C])
        stats = a.sb("stats", [P, GT, 6])
        mv = a.sb("mv", [P, GT, 2])
        veps = a.sb("veps", [P, GT])
        rstd = a.sb("rstd", [P, GT])
        xt = a.sb("xt", [P, W])
        h1 = a.sb("h1", [P, KH, W])
        h2 = a.sb("h2", [P, KH, W])
        lg = a.sb("lg", [P, GT, E0])
        top = a.sb("top", [P, GT])
        ex = a.sb("ex", [P, GT, E0])
        den = a.sb("den", [P, GT])
        sc = a.sb("sc", [P, GT, E0])
        best = a.sb("best", [P, GT, 8])
        best_at = a.sb("best_at", [P, GT, 8], U32)
        best_f = a.sb("best_f", [P, GT, 2])
        eq = a.sb("eq", [P, GT, 2, E0])
        mask = a.sb("mask", [P, GT, E0], BF16)
        off = a.sb("off", [P, GT, E0])
        pos = a.sb("pos", [P, GT, E0])
        d = a.sb("d", [P, 2, GT * E0, CAP])
        g = a.sb("g", [P, 2, GT * E0, CAP])
        xd = a.sb("xd", [P, E0, NB, CAP])
        hh = a.sb("hh", [P, E0, KH, NB * CAP])
        eot = a.sb("eot", [P, NB, E0, CAP])
        eos = a.sb("eos", [SW, NB, NW, C])
        gts = a.sb("gts", [SW, GT, NW, P])

        ra = Ring(a.ps("ra", [P, 2, 512]), a.sem("ra_filled"), a.sem("ra_emptied"), 5, 2)
        rv = Ring(a.ps("rv", [P, 2, 512]), a.sem("rv_filled"), a.sem("rv_emptied"), 6, 2)
        ea = Ring(a.ps("ea", [P, 2, 512]), a.sem("ea_filled"), a.sem("ea_emptied"), 9, 2)
        ev = Ring(a.ps("ev", [P, 2, 512]), a.sem("ev_filled"), a.sem("ev_emptied"), 10, 2)
        ln_stats, ln_aggr, ln_veps, ln_rstd, xn_ready = [a.sem(n) for n in (
            "ln_stats", "ln_aggr", "ln_veps", "ln_rstd", "xn_ready")]
        top_ready, lg_ready, ex_ready, den_step, sc_ready, best_step, bestf, mask_step, off_ready, d_ready, g_ready = [
            a.sem(n) for n in ("top_ready", "lg_ready", "ex_ready", "den_step", "sc_ready", "best_step", "bestf",
                               "mask_step", "off_ready", "d_ready", "g_ready")]
        block = ctx.enter_context(nc.Block())

        @block.sync
        def _(sp):
            if w.load is not None:
                w.load(sp)

        @block.tensor
        def _(pe):
            def route(it):
                i = it[0]
                pe.wait_ge(ra.emptied, ra.nth(it, 0))
                pe.wait_ge(xn_ready, i * GT + GT)
                for t in range(GT):
                    mm = nc.tensor.transpose(ra.bank(it, 0)[:, t * P:(t + 1) * P], xn[:, it[1], t, :], k.ident)
                mm.then_inc(ra.filled, 1)
                pe.wait_ge(ra.emptied, ra.done(it, 0))
                if is_first(i):
                    pe.wait_ge(w.router_loaded, w.router_count)
                for m in range(KH):
                    ring, n = (ra, 1 + m // 2) if m % 2 == 0 else (rv, m // 2)
                    pe.wait_ge(ring.emptied, ring.nth(it, n))
                    nc.tensor.matmul(ring.bank(it, n), w.rw1[:, m * P:(m + 1) * P], xt[:, :],
                                     start=True, stop=True).then_inc(ring.filled, 1)
                pe.wait_ge(ra.emptied, ra.done(it, 2))
                pe.wait_ge(rv.emptied, rv.done(it, 1))
                for m in range(KH):
                    ring, n = (ra, 3 + m // 2) if m % 2 == 0 else (rv, 2 + m // 2)
                    pe.wait_ge(ring.emptied, ring.nth(it, n))
                    for j in range(KH):
                        mm = nc.tensor.matmul(ring.bank(it, n), w.rw2[:, j, m * P:(m + 1) * P], h1[:, j, :],
                                              start=(j == 0), stop=(j == KH - 1))
                    mm.then_inc(ring.filled, 1)
                pe.wait_ge(rv.emptied, rv.nth(it, 4))
                pe.wait_ge(ra.emptied, ra.done(it, 4))
                pe.wait_ge(rv.emptied, rv.done(it, 3))
                for t in range(GT):
                    for j in range(KH):
                        mm = nc.tensor.matmul(rv.bank(it, 4)[:, t * E0:(t + 1) * E0],
                                              h2[:, j, t * P:(t + 1) * P], w.rw3[:, j, :],
                                              start=(j == 0), stop=(j == KH - 1))
                mm.then_inc(rv.filled, 1)

            def count(it):
                pe.wait_ge(rv.emptied, rv.nth(it, 5))
                pe.wait_ge(mask_step, it[0] + 1)
                for t in range(GT):
                    out = rv.bank(it, 5)[:, t * E0:(t + 1) * E0]
                    if t % TT:
                        nc.tensor.matmul(out, k.ones_bf, mask[:, t - 1, :], start=True, stop=False)
                    mm = nc.tensor.matmul(out, k.tri_bf, mask[:, t, :], start=(t % TT == 0), stop=True)
                mm.then_inc(rv.filled, 1)

            def experts(it, counted):
                i, par = it
                pe.wait_ge(d_ready, i + 1)
                for b in range(NB):
                    ring = (ea, ev)[b]
                    pe.wait_ge(ring.emptied, ring.nth(it, 0))
                    for t in range(TT):
                        u = b * TT + t
                        mm = nc.tensor.matmul(ring.bank(it, 0)[:, 0:S], xn[:, par, u, :],
                                              d[:, par, u * E0:(u + 1) * E0, :],
                                              start=(t == 0), stop=(t == TT - 1))
                    mm.then_inc(ring.filled, 1)
                pe.wait_ge(ea.emptied, ea.done(it, 0))
                pe.wait_ge(ev.emptied, ev.done(it, 0))
                for e in range(E0):
                    ring, n = (ea, ev)[e % 2], 1 + e // 2
                    pe.wait_ge(ring.emptied, ring.nth(it, n))
                    for j in range(KH):
                        mm = nc.tensor.matmul(ring.bank(it, n)[:, j * SW:(j + 1) * SW],
                                              w.ew1[:, e, j * P:(j + 1) * P], xd[:, e, :, :],
                                              start=True, stop=True)
                    mm.then_inc(ring.filled, 1)
                for e in range(E0):
                    ring = (ea, ev)[e // 4]
                    if e % 4 == 0:
                        pe.wait_ge(ring.emptied, ring.nth(it, 5))
                    source, n = (ea, ev)[e % 2], 1 + e // 2
                    pe.wait_ge(source.emptied, source.done(it, n))
                    for j in range(KH):
                        mm = nc.tensor.matmul(ring.bank(it, 5)[:, (e % 4) * P:(e % 4) * P + SW],
                                              w.ew2[:, e, j, :], hh[:, e, j, :],
                                              start=(j == 0), stop=(j == KH - 1))
                    if e % 4 == 3:
                        mm.then_inc(ring.filled, 1)
                if counted is not None:
                    count(counted)
                pe.wait_ge(ea.emptied, ea.done(it, 5))
                pe.wait_ge(ev.emptied, ev.done(it, 5))
                for b in range(NB):
                    ring = (ea, ev)[b]
                    pe.wait_ge(ring.emptied, ring.nth(it, 6))
                    for v in range(NW):
                        mm = nc.tensor.transpose(ring.bank(it, 6)[0:SW, v * P:(v + 1) * P],
                                                 eot[:, b, 2 * v:2 * v + 2, :], k.ident)
                    mm.then_inc(ring.filled, 1)
                pe.wait_ge(g_ready, i + 1)
                for t in range(GT):
                    ring, n = (ea, ev)[t % 2], 7 + t // 2
                    pe.wait_ge(ring.emptied, ring.nth(it, n))
                    for v in range(NW):
                        mm = nc.tensor.transpose(ring.bank(it, n)[0:SW, v * P:(v + 1) * P],
                                                 g[:, par, t * E0 + 2 * v:t * E0 + 2 * v + 2, :], k.ident)
                    mm.then_inc(ring.filled, 1)
                pe.wait_ge(ev.emptied, ev.nth(it, 9))
                pe.wait_ge(ea.emptied, ea.done(it, 8))
                pe.wait_ge(ev.emptied, ev.done(it, 8))
                for t in range(GT):
                    for v in range(NW):
                        mm = nc.tensor.matmul(ev.bank(it, 9)[:, t * P:(t + 1) * P], gts[:, t, v, :],
                                              eos[:, t // TT, v, :], start=(v == 0), stop=(v == NW - 1))
                mm.then_inc(ev.filled, 1)

            def step(it, inner=False):
                s = it[0]
                if within(s, 0, G - 1):
                    route(it)
                if is_first(s):
                    count(it)
                    pe.wait_ge(w.experts_loaded, w.experts_count)
                if within(s, 1, G):
                    experts(before(it), it if within(s, 0, G - 1) else None)

            pe.wait_ge(k.loaded, k.loaded_count)
            steps(pe, 0, G, step, lead=1, trail=2)

        @block.scalar
        def _(act):
            act.sem_inc(ra.emptied, ra.banks)
            act.sem_inc(ea.emptied, ea.banks)

            def route(it):
                act.wait_ge(ra.filled, ra.nth(it, 0))
                nc.scalar.activation(xt[:, :], ra.bank(it, 0), ACT.Copy).then_inc(ra.emptied, 1)
                if is_first(it[0]):
                    act.wait_ge(w.router_loaded, w.router_count)
                for n, (out, bias) in enumerate(((h1, w.rb1), (h1, w.rb1), (h2, w.rb2), (h2, w.rb2))):
                    m = 2 * (n % 2)
                    act.wait_ge(ra.filled, ra.nth(it, 1 + n))
                    nc.scalar.activation(out[:, m, :], ra.bank(it, 1 + n), ACT.Relu,
                                         bias=bias[:, m:m + 1]).then_inc(ra.emptied, 1)

            def softmax_exp(it):
                act.wait_ge(lg_ready, it[0] + 1)
                nc.scalar.activation(ex[:, :, :], lg[:, :, :], ACT.Exp).then_inc(ex_ready, 1)

            def experts(it, routed):
                act.wait_ge(ea.filled, ea.nth(it, 0))
                nc.scalar.activation(xd[:, :, 0, :], ea.bank(it, 0)[:, 0:S].rearrange("p (e s) -> p e s", e=E0),
                                     ACT.Copy).then_inc(ea.emptied, 1)
                for e in range(0, E0, 2):
                    act.wait_ge(ea.filled, ea.nth(it, 1 + e // 2))
                    for j in range(KH):
                        last = nc.scalar.activation(hh[:, e, j, :], ea.bank(it, 1 + e // 2)[:, j * SW:(j + 1) * SW],
                                                    ACT.Relu, bias=w.eb1[:, e, j:j + 1])
                    last.then_inc(ea.emptied, 1)
                    if e == 2 and routed is not None:
                        softmax_exp(routed)
                act.wait_ge(ea.filled, ea.nth(it, 5))
                for e in range(4):
                    last = nc.scalar.activation(eot[:, :, e, :], ea.bank(it, 5)[:, e * P:e * P + SW]
                                                .rearrange("p (b s) -> p b s", b=NB), ACT.Identity,
                                                bias=w.eb2[:, e:e + 1])
                last.then_inc(ea.emptied, 1)
                act.wait_ge(ea.filled, ea.nth(it, 6))
                nc.scalar.activation(eos[:, 0, :, :].rearrange("p v c -> p (v c)"), ea.bank(it, 6)[0:SW, :],
                                     ACT.Copy).then_inc(ea.emptied, 1)
                for t in (0, 2):
                    act.wait_ge(ea.filled, ea.nth(it, 7 + t // 2))
                    nc.scalar.activation(gts[:, t, :, :].rearrange("p v c -> p (v c)"),
                                         ea.bank(it, 7 + t // 2)[0:SW, :], ACT.Copy).then_inc(ea.emptied, 1)

            def step(it, inner=False):
                s = it[0]
                if within(s, 0, G - 1):
                    route(it)
                    if is_first(s):
                        softmax_exp(it)
                if is_first(s):
                    act.wait_ge(w.experts_loaded, w.experts_count)
                if within(s, 1, G):
                    experts(before(it), it if within(s, 0, G - 1) else None)

            steps(act, 0, G, step, lead=1, trail=2)

        @block.vector
        def _(dve):
            dve.sem_inc(rv.emptied, rv.banks)
            dve.sem_inc(ev.emptied, ev.banks)

            def ln_measure(it):
                i = it[0]
                for t in range(GT):
                    nc.vector.bn_stats(stats[:, t, :], x_g[:, i, t, :]).then_inc(ln_stats, 1)
                dve.wait_ge(ln_stats, i * GT + GT)
                nc.vector.memset(k.idle, 0.0)
                for t in range(GT):
                    last = nc.vector.bn_aggr(mv[:, t, :], stats[:, t, :])
                last.then_inc(ln_aggr, 1)

            def ln_apply(it):
                i = it[0]
                dve.wait_ge(ln_rstd, i + 1)
                for t in range(GT):
                    nc.vector.tensor_scalar(xn[:, it[1], t, :], x_g[:, i, t, :], mv[:, t, 0:1], rstd[:, t:t + 1],
                                            ALU.subtract, ALU.mult).then_inc(xn_ready, 1)

            def route_evacuate(it):
                for n, (out, bias) in enumerate(((h1, w.rb1), (h1, w.rb1), (h2, w.rb2), (h2, w.rb2))):
                    m = 1 + 2 * (n % 2)
                    dve.wait_ge(rv.filled, rv.nth(it, n))
                    nc.vector.tensor_scalar(out[:, m, :], rv.bank(it, n), bias[:, m:m + 1], 0.0,
                                            ALU.add, ALU.max).then_inc(rv.emptied, 1)

            def softmax_shift(it):
                i = it[0]
                dve.wait_ge(rv.filled, rv.nth(it, 4))
                nc.vector.tensor_tensor(lg[:, :, :], rv.bank(it, 4)[:, 0:GT * E0].rearrange("p (t e) -> p t e", t=GT),
                                        w.rb3[:, :].unsqueeze(1).to_broadcast([P, GT, E0]),
                                        ALU.add).then_inc(rv.emptied, 1)
                dve.wait_ge(rv.emptied, rv.done(it, 4))
                nc.vector.tensor_reduce(top[:, :], lg[:, :, :], AX.X, ALU.max).then_inc(top_ready, 1)
                dve.wait_ge(top_ready, i + 1)
                nc.vector.tensor_tensor(lg[:, :, :], lg[:, :, :], top[:, :].unsqueeze(2).to_broadcast([P, GT, E0]),
                                        ALU.subtract).then_inc(lg_ready, 1)

            def softmax_divide(it):
                i = it[0]
                dve.wait_ge(ex_ready, i + 1)
                nc.vector.tensor_reduce(den[:, :], ex[:, :, :], AX.X, ALU.add).then_inc(den_step, 1)
                dve.wait_ge(den_step, i * 2 + 1)
                nc.vector.reciprocal(den[:, :], den[:, :]).then_inc(den_step, 1)
                if not is_first(i):
                    dve.wait_ge(g_ready, i)
                dve.wait_ge(den_step, i * 2 + 2)
                nc.vector.tensor_tensor(sc[:, :, :], ex[:, :, :], den[:, :].unsqueeze(2).to_broadcast([P, GT, E0]),
                                        ALU.mult).then_inc(sc_ready, 1)

            def pick(it):
                i = it[0]
                dve.wait_ge(sc_ready, i + 1)
                nc.vector.memset(k.idle, 0.0)
                for t in range(GT):
                    last = nc.vector.max(best[:, t, :], sc[:, t, :])
                last.then_inc(best_step, 1)
                dve.wait_ge(best_step, i * 2 + 1)
                nc.vector.memset(k.idle, 0.0)
                for t in range(GT):
                    last = nc.vector.max_index(best_at[:, t, :], best[:, t, :], sc[:, t, :])
                last.then_inc(best_step, 1)
                dve.wait_ge(best_step, i * 2 + 2)
                nc.vector.tensor_copy(best_f[:, :, :], best_at[:, :, 0:2]).then_inc(bestf, 1)

            def mark(it):
                i = it[0]
                dve.wait_ge(bestf, i * 2 + 1)
                for n in range(2):
                    last = nc.vector.tensor_tensor(eq[:, :, n, :], k.iota8.unsqueeze(1).to_broadcast([P, GT, E0]),
                                                   best_f[:, :, n:n + 1].to_broadcast([P, GT, E0]), ALU.is_equal)
                last.then_inc(bestf, 1)
                dve.wait_ge(bestf, i * 2 + 2)
                nc.vector.tensor_tensor(mask[:, :, :], eq[:, :, 0, :], eq[:, :, 1, :], ALU.add).then_inc(mask_step, 1)
                dve.wait_ge(mask_step, i + 1)
                nc.vector.tensor_scalar(off[:, :, :], mask[:, :, :], -1000.0, 1000.0, ALU.mult, ALU.add)\
                    .then_inc(off_ready, 1)

            def place(it):
                i = it[0]
                dve.wait_ge(off_ready, i + 1)
                dve.wait_ge(rv.filled, rv.nth(it, 5))
                nc.vector.tensor_tensor(pos[:, :, :], rv.bank(it, 5)[:, 0:GT * E0].rearrange("p (t e) -> p t e", t=GT),
                                        off[:, :, :], ALU.add).then_inc(rv.emptied, 1)
                dve.wait_ge(rv.emptied, rv.done(it, 5))
                nc.vector.tensor_tensor(d[:, it[1], :, :], k.iota40.unsqueeze(1).to_broadcast([P, GT * E0, CAP]),
                                        pos[:, :, :].rearrange("p t e -> p (t e)").unsqueeze(2)
                                        .to_broadcast([P, GT * E0, CAP]), ALU.is_equal).then_inc(d_ready, 1)

            def hidden(it, e):
                dve.wait_ge(ev.filled, ev.nth(it, 1 + e // 2))
                for j in range(KH):
                    last = nc.vector.tensor_scalar(hh[:, e, j, :], ev.bank(it, 1 + e // 2)[:, j * SW:(j + 1) * SW],
                                                   w.eb1[:, e, j:j + 1], 0.0, ALU.add, ALU.max)
                last.then_inc(ev.emptied, 1)

            def experts_first(it, routed):
                dve.wait_ge(ev.filled, ev.nth(it, 0))
                nc.vector.tensor_copy(xd[:, :, 1, :], ev.bank(it, 0)[:, 0:S].rearrange("p (e s) -> p e s", e=E0))\
                    .then_inc(ev.emptied, 1)
                if routed is not None:
                    softmax_shift(routed)
                hidden(it, 1)
                hidden(it, 3)
                if routed is not None:
                    softmax_divide(routed)
                hidden(it, 5)
                if routed is not None:
                    pick(routed)
                hidden(it, 7)
                if routed is not None:
                    mark(routed)

            def experts_last(it):
                dve.wait_ge(ev.filled, ev.nth(it, 5))
                for e in range(4, E0):
                    last = nc.vector.tensor_scalar(eot[:, :, e, :], ev.bank(it, 5)[:, (e - 4) * P:(e - 4) * P + SW]
                                                   .rearrange("p (b s) -> p b s", b=NB), w.eb2[:, e:e + 1], None,
                                                   ALU.add)
                last.then_inc(ev.emptied, 1)

            def combine(it):
                dve.wait_ge(ev.filled, ev.nth(it, 6))
                nc.vector.tensor_copy(eos[:, 1, :, :].rearrange("p v c -> p (v c)"), ev.bank(it, 6)[0:SW, :])\
                    .then_inc(ev.emptied, 1)
                for t in (1, 3):
                    dve.wait_ge(ev.filled, ev.nth(it, 7 + t // 2))
                    nc.vector.tensor_copy(gts[:, t, :, :].rearrange("p v c -> p (v c)"),
                                          ev.bank(it, 7 + t // 2)[0:SW, :]).then_inc(ev.emptied, 1)

            def residual(it):
                dve.wait_ge(ev.filled, ev.nth(it, 9))
                xs = x_g[:, it[0], :, :].rearrange("p t c -> p (t c)")
                nc.vector.scalar_tensor_tensor(xs, ev.bank(it, 9), 0.5, xs, ALU.mult, ALU.add)\
                    .then_inc(ev.emptied, 1)

            def step(it, inner=False):
                s = it[0]
                if is_first(s):
                    ln_measure(it)
                    ln_apply(it)
                    dve.wait_ge(w.router_loaded, w.router_count)
                has_route, has_experts = within(s, 0, G - 1), within(s, 1, G)
                if has_route:
                    route_evacuate(it)
                if has_experts:
                    experts_first(before(it), it if has_route else None)
                else:
                    softmax_shift(it)
                    softmax_divide(it)
                    pick(it)
                    mark(it)
                if within(s, 0, G - 2):
                    ln_measure(after(it))
                if has_experts:
                    experts_last(before(it))
                if has_route:
                    place(it)
                if is_first(s):
                    dve.wait_ge(w.experts_loaded, w.experts_count)
                if within(s, 0, G - 2):
                    ln_apply(after(it))
                if has_experts:
                    combine(before(it))
                    residual(before(it))

            dve.wait_ge(k.loaded, k.loaded_count)
            steps(dve, 0, G, step, lead=1, trail=2)

        @block.gpsimd
        def _(pool):
            def ln_root(it):
                pool.wait_ge(ln_aggr, it[0] + 1)
                nc.gpsimd.tensor_tensor(veps[:, :], mv[:, :, 1], k.eps[:, 0:GT], ALU.add).then_inc(ln_veps, 1)
                pool.wait_ge(ln_veps, it[0] + 1)
                nc.gpsimd.tensor_tensor(rstd[:, :], veps[:, :], k.minus_half[:, 0:GT], ALU.pow).then_inc(ln_rstd, 1)

            def weigh(it):
                pool.wait_ge(d_ready, it[0] + 1)
                nc.gpsimd.tensor_tensor(g[:, it[1], :, :], d[:, it[1], :, :],
                                        sc[:, :, :].rearrange("p t e -> p (t e)").unsqueeze(2)
                                        .to_broadcast([P, GT * E0, CAP]), ALU.mult).then_inc(g_ready, 1)

            def step(it, inner=False):
                s = it[0]
                if is_first(s):
                    ln_root(it)
                if within(s, 0, G - 2):
                    ln_root(after(it))
                if within(s, 0, G - 1):
                    weigh(it)

            pool.wait_ge(k.loaded, k.loaded_count)
            steps(pool, 0, G - 1, step, lead=1, trail=1)


class Desk:

    def __init__(self, psum, filled, emptied, names, late, banks=2):
        self.psum, self.filled, self.emptied, self.banks = psum, filled, emptied, banks
        self.names, self.late = names, late

    def _present(self, s):
        return [n for n in self.names if within(s, *((2, B + 1) if n in self.late else (0, B - 1)))]

    def _before(self, it):
        s, par = it
        if isinstance(s, int):
            n = sum(len(self._present(u)) for u in range(s))
            return n, n % 2
        start = 2 * (len(self.names) - len(self.late))
        return (s - 2) * len(self.names) + start, (start + par * len(self.names)) % 2

    def nth(self, it, name):
        return self._before(it)[0] + self._present(it[0]).index(name) + 1

    def bank(self, it, name):
        return self.psum[:, (self._before(it)[1] + self._present(it[0]).index(name)) % self.banks, :]

    def done(self, it, name):
        return self.nth(it, name) + self.banks


def heads_of(v):
    def at(vm, par, t):
        whole = vm[:, par, t, :, :]
        return bass.AP(whole.tensor, whole.offset, [list(whole.ap[0]), [C + HD, QUAD], [QUAD * HD, H // QUAD], [1, HD]])
    return at(*v)


def stack_parts(sp, parts, scratch, qs, ks, parts_ready, bounced, stacked, passed, sr):
    def step(it, inner=False):
        i, par = it
        if not is_first(i):
            sp.wait_ge(stacked, i * 192)
            sp.sem_inc(passed, 1)
        sp.wait_ge(parts_ready, i + 1)
        sp.dma_start(scratch[par], parts[:, par, :, :, :]).then_inc(bounced, 16)
        if not is_first(i) and not is_first(i, 1):
            sp.wait_ge(sr.filled, (i - 1) * H)
            sp.sem_inc(passed, 1)
        sp.wait_ge(bounced, i * 16 + 16)
        for n in range(SLOTS):
            for dst, which, part in ((qs, 0, QSLOT[n]), (ks, 1, KSLOT[n])):
                sp.dma_start(dst[n * HD:(n + 1) * HD, par, :, :],
                             scratch[par, :, part, which, :].rearrange("(h d) t -> d h t", d=HD))\
                    .then_inc(stacked, 16)

    steps(sp, 0, B - 1, step, lead=2, trail=2)
    sp.wait_ge(stacked, B * 192)


def retention(nc, tag, x_sb, k, io):
    x_b = x_sb[:, :, :].rearrange("p (b t) c -> p b t c", t=TT)
    AB = 4
    LAG = 2
    with ExitStack() as ctx:
        a = Pool_(nc, ctx, tag)
        w0, wp = a.sb("w0", [P, 6, C]), a.sb("wp", [P, C])
        rope, decay, group = a.sb("rope", [P, 4, T]), a.sb("decay", [P, H, T + P]), a.sb("group", [P, P])
        gnw, gnb = a.sb("gnw", [P, 1]), a.sb("gnb", [P, 1])
        stats, mv = a.sb("stats", [P, TT, 6]), a.sb("mv", [P, TT, 2])
        veps, rstd = a.sb("veps", [P, TT]), a.sb("rstd", [P, TT])
        xn = a.sb("xn", [P, TT, C])
        xt = a.sb("xt", [P, T])
        qp, kp = a.sb("qp", [P, 2, T]), a.sb("kp", [P, 2, T])
        qk, rest = a.sb("qk", [P, 2, T]), a.sb("rest", [P, 2, T])
        parts = a.sb("parts", [P, 2, 3, 2, T], BF16)
        qs, ks = a.sb("qs", [SLOTS * HD, 2, H, T], BF16), a.sb("ks", [SLOTS * HD, 2, H, T], BF16)
        scratch = nc.dram_tensor(f"{tag}_scratch", (2, P, 3, 2, T), BF16, kind="Internal").ap()
        vm = a.sb("vm", [P, 2, TT, QUAD, C])
        gate, eg = a.sb("gate", [P, T]), a.sb("eg", [P, T])
        silu = a.sb("silu", [P, 2, T])
        att = a.sb("att", [P, AB, T + P])
        ystats, ymv = a.sb("ystats", [P, 6]), a.sb("ymv", [P, 2])
        mean, dmean, qv, var = [a.sb(n, [P, 1]) for n in ("mean", "dmean", "qv", "var")]
        veps_y, rstd_y, ga, nb = [a.sb(n, [P, 1]) for n in ("veps_y", "rstd_y", "ga", "nb")]
        yn = a.sb("yn", [P, T])
        gated = a.sb("gated", [P, T])
        ob = a.sb("ob", [P, TT, C])

        y_ps = a.ps("y", [P, 2, 512])
        desk = Desk(a.ps("desk", [P, 2, 512]), a.sem("desk_filled"), a.sem("desk_emptied"),
                    ["xt", "gm", "q", "k", "gv", "v", "o", "g"], ["gm", "gv", "o"])
        sr = Ring(a.ps("sr", [P, AB, 512]), a.sem("sr_filled"), a.sem("sr_emptied"), H, AB)
        (loaded, vm_zero, ln_stats, ln_aggr, ln_veps, ln_rstd, xn_ready, qp_turned, kp_turned, qk_ready, part1, rest1,
         part2, parts_ready, bounced, stacked, eg1, eg2, silu_ready, av_done, y_stats, y_aggr, dm_ready, qv_ready,
         y_veps, y_rstd, ga_ready, nb_ready, yn_ready, gated_ready, x_done, passed) = [a.sem(n) for n in (
             "loaded", "vm_zero", "ln_stats", "ln_aggr", "ln_veps", "ln_rstd", "xn_ready", "qp_turned", "kp_turned",
             "qk_ready", "part1", "rest1", "part2", "parts_ready", "bounced", "stacked", "eg1", "eg2", "silu_ready",
             "av_done", "y_stats", "y_aggr", "dm_ready", "qv_ready", "y_veps", "y_rstd", "ga_ready", "nb_ready",
             "yn_ready", "gated_ready", "x_done", "passed")]
        LOADS = 16 * 7
        block = ctx.enter_context(nc.Block())

        def prep(it):
            return within(it[0], 0, B - 1)

        def attend(it):
            return within(it[0], 1, B)

        def finish(it):
            return within(it[0], 2, B + 1)

        @block.sync
        def _(sp):
            for dst, src in ((w0[:, :, :], io["w0"].rearrange("p (n c) -> p n c", c=C)), (rope[:, :, :], io["rope"]),
                             (decay[:, :, :], io["decay"]), (group[:, :], io["group"]), (gnw[:, :], io["gnw"]),
                             (gnb[:, :], io["gnb"]), (wp[:, :], io["w0p"])):
                sp.dma_start(dst, src).then_inc(loaded, 16)

            stack_parts(sp, parts, scratch, qs, ks, parts_ready, bounced, stacked, passed, sr)

        @block.tensor
        def _(pe):
            def fill(it, name):
                pe.wait_ge(desk.emptied, desk.nth(it, name))
                return desk.bank(it, name)

            def attend_scores(it, n):
                h = (n % QUAD) * QUAD + n // QUAD
                pe.wait_ge(sr.emptied, sr.nth(it, n))
                out = sr.bank(it, n)
                nc.tensor.matmul(out[:, 0:T], ks[:, it[1], h, 0:P], qs[:, it[1], h, :], start=True, stop=True)
                nc.tensor.matmul(out[:, T:T + P], ks[:, it[1], h, P:T], qs[:, it[1], h, P:T], start=True,
                                 stop=True).then_inc(sr.filled, 1)

            def attend_values(it, n):
                r, j = n // QUAD, n % QUAD
                q = slice(j * QUAD * HD, (j + 1) * QUAD * HD)
                pe.wait_ge(sr.emptied, sr.done(it, n))
                nc.tensor.matmul(y_ps[q, it[1], 0:T], vm[:, it[1], 0, r, q], att[:, n % AB, 0:T],
                                 start=(r == 0), stop=False, skip_group_check=True)
                nc.tensor.matmul(y_ps[q, it[1], P:T], vm[:, it[1], 1, r, q], att[:, n % AB, T:T + P],
                                 start=False, stop=(r == QUAD - 1), skip_group_check=True).then_inc(av_done, 1)

            def small(it, n):
                i, par = it
                if n == 0 and prep(it):
                    pe.wait_ge(xn_ready, i * TT + TT)
                    out = fill(it, "xt")
                    for t in range(TT):
                        mm = nc.tensor.transpose(out[:, t * P:(t + 1) * P], xn[:, t, :], k.ident)
                    mm.then_inc(desk.filled, 1)
                if n == 1 and finish(it):
                    pe.wait_ge(y_aggr, i - 1)
                    nc.tensor.matmul(fill(it, "gm")[:, 0:1], group[:, :], ymv[:, 0:1], start=True, stop=True)\
                        .then_inc(desk.filled, 1)
                if n in (2, 3) and prep(it):
                    name = "qk"[n - 2]
                    pe.wait_ge(desk.emptied, desk.done(it, "xt"))
                    out = fill(it, name)
                    for u in range(2):
                        mm = nc.tensor.matmul(out[:, u * T:(u + 1) * T], w0[:, 2 * (n - 2) + u, :], xt[:, :],
                                              start=True, stop=True)
                    mm.then_inc(desk.filled, 1)
                if n == 4 and finish(it):
                    pe.wait_ge(qv_ready, i - 1)
                    nc.tensor.matmul(fill(it, "gv")[:, 0:1], group[:, :], qv[:, :], start=True, stop=True)\
                        .then_inc(desk.filled, 1)
                if n == 6 and prep(it):
                    out = fill(it, "v")
                    for t in range(TT):
                        mm = nc.tensor.matmul(out[:, t * P:(t + 1) * P], xt[:, t * P:(t + 1) * P], w0[:, 5, :],
                                              start=True, stop=True)
                    mm.then_inc(desk.filled, 1)
                if n == 10 and finish(it):
                    out = fill(it, "o")
                    pe.wait_ge(gated_ready, i - 1)
                    for t in range(TT):
                        mm = nc.tensor.matmul(out[:, t * P:(t + 1) * P], gated[:, t * P:(t + 1) * P], wp[:, :],
                                              start=True, stop=True)
                    mm.then_inc(desk.filled, 1)
                if n == 12 and prep(it):
                    nc.tensor.matmul(fill(it, "g")[:, 0:T], w0[:, 4, :], xt[:, :], start=True, stop=True)\
                        .then_inc(desk.filled, 1)

            def step(it, inner=False):
                b = before(it)
                if attend(it):
                    pe.wait_ge(stacked, b[0] * 192 + 192)
                    if not is_first(b[0]) and not is_first(b[0], 1):
                        pe.wait_ge(yn_ready, b[0] - 1)
                for n in range(H):
                    small(it, n)
                    if attend(it):
                        attend_scores(b, n)
                        if n >= LAG:
                            attend_values(b, n - LAG)
                if attend(it):
                    for n in range(H - LAG, H):
                        attend_values(b, n)

            pe.wait_ge(k.loaded, k.loaded_count)
            pe.wait_ge(loaded, LOADS)
            pe.wait_ge(vm_zero, 1)
            steps(pe, 0, B + 1, step, lead=2, trail=2)

        @block.scalar
        def _(act):
            act.sem_inc(desk.emptied, 2)

            def taken(it, name):
                act.wait_ge(desk.filled, desk.nth(it, name))
                return desk.bank(it, name)

            def step(it, inner=False):
                i, par = it
                if prep(it):
                    nc_xt = taken(it, "xt")
                    nc.scalar.activation(xt[:, :], nc_xt[:, 0:T], ACT.Copy).then_inc(desk.emptied, 1)
                if finish(it):
                    bank = taken(it, "gm")
                    nc.scalar.activation(mean[:, :], bank[:, 0:1], ACT.Copy).then_inc(desk.emptied, 1)
                if prep(it):
                    for name, dst, turned in (("q", qp, qp_turned), ("k", kp, kp_turned)):
                        bank = taken(it, name)
                        if not is_first(i):
                            act.wait_ge(qk_ready, i * 2)
                        nc.scalar.activation(dst[:, :, :].rearrange("p u t -> p (u t)"), bank, ACT.Copy)\
                            .then_inc(desk.emptied, 1)
                if finish(it):
                    bank = taken(it, "gv")
                    nc.scalar.activation(var[:, :], bank[:, 0:1], ACT.Copy).then_inc(desk.emptied, 1)
                if prep(it):
                    bank = taken(it, "v")
                    for t in range(TT):
                        last = nc.scalar.activation(
                            heads_of((vm, par, t)),
                            bank[:, t * P:(t + 1) * P].rearrange("p (j r d) -> p r j d", r=QUAD, d=HD), ACT.Copy)
                    last.then_inc(desk.emptied, 1)
                if finish(it):
                    bank = taken(it, "o")
                    if not is_first(i, 2):
                        act.wait_ge(x_done, i - 2)
                    nc.scalar.activation(ob[:, :, :].rearrange("p t c -> p (t c)"), bank[:, 0:T], ACT.Copy)\
                        .then_inc(desk.emptied, 1)
                if prep(it):
                    bank = taken(it, "g")
                    if not is_first(i):
                        act.wait_ge(silu_ready, i)
                    nc.scalar.activation(gate[:, :], bank[:, 0:T], ACT.Copy)
                    nc.scalar.activation(eg[:, :], bank[:, 0:T], ACT.Exp, scale=-1.0).then_inc(desk.emptied, 1)

            act.wait_ge(vm_zero, 1)
            steps(act, 0, B + 1, step, lead=2, trail=2)

        @block.vector
        def _(dve):
            dve.sem_inc(sr.emptied, AB)
            nc.vector.memset(vm[:, :, :, :, :].rearrange("p a b c d -> p (a b c d)"), 0.0).then_inc(vm_zero, 1)

            def ln_measure(it):
                i = it[0]
                for t in range(TT):
                    nc.vector.bn_stats(stats[:, t, :], x_b[:, i, t, :]).then_inc(ln_stats, 1)
                dve.wait_ge(ln_stats, i * TT + TT)
                nc.vector.memset(k.idle, 0.0)
                for t in range(TT):
                    last = nc.vector.bn_aggr(mv[:, t, :], stats[:, t, :])
                last.then_inc(ln_aggr, 1)

            def ln_apply(it):
                i = it[0]
                dve.wait_ge(ln_rstd, i + 1)
                for t in range(TT):
                    nc.vector.tensor_scalar(xn[:, t, :], x_b[:, i, t, :], mv[:, t, 0:1], rstd[:, t:t + 1],
                                            ALU.subtract, ALU.mult).then_inc(xn_ready, 1)

            def turn(it, name):
                src, turned, u = (qp, qp_turned, 0) if name == "q" else (kp, kp_turned, 2)
                dve.wait_ge(desk.emptied, desk.done(it, name))
                nc.vector.tensor_tensor(src[:, :, :], src[:, :, :], rope[:, u:u + 2, :], ALU.mult).then_inc(turned, 1)

            def small(it, n):
                i, par = it
                if finish(it):
                    b = i - 2
                    if n == 0:
                        nc.vector.bn_stats(ystats[:, :], y_ps[:, par, 0:T]).then_inc(y_stats, 1)
                        dve.wait_ge(y_stats, b + 1)
                        nc.vector.memset(k.idle, 0.0)
                        nc.vector.bn_aggr(ymv[:, :], ystats[:, :]).then_inc(y_aggr, 1)
                    if n == 3:
                        dve.wait_ge(desk.emptied, desk.done(it, "gm"))
                        nc.vector.tensor_tensor(dmean[:, :], ymv[:, 0:1], mean[:, :], ALU.subtract).then_inc(dm_ready, 1)
                        dve.wait_ge(dm_ready, b + 1)
                        nc.vector.scalar_tensor_tensor(qv[:, :], dmean[:, :], dmean[:, 0:1], ymv[:, 1:2], ALU.mult,
                                                       ALU.add).then_inc(qv_ready, 1)
                    if n == 8:
                        dve.wait_ge(y_rstd, b + 1)
                        nc.vector.tensor_tensor(ga[:, :], rstd_y[:, :], gnw[:, :], ALU.mult).then_inc(ga_ready, 1)
                        dve.wait_ge(ga_ready, b + 1)
                        nc.vector.scalar_tensor_tensor(nb[:, :], mean[:, :], ga[:, 0:1], gnb[:, :], ALU.mult,
                                                       ALU.subtract).then_inc(nb_ready, 1)
                        dve.wait_ge(nb_ready, b + 1)
                        nc.vector.tensor_scalar(yn[:, :], y_ps[:, par, 0:T], ga[:, 0:1], nb[:, 0:1], ALU.mult,
                                                ALU.subtract).then_inc(yn_ready, 1)
                        dve.wait_ge(yn_ready, b + 1)
                        dve.wait_ge(silu_ready, b + 1)
                        nc.vector.tensor_tensor(gated[:, :], yn[:, :], silu[:, par, :], ALU.mult)\
                            .then_inc(gated_ready, 1)
                if prep(it):
                    if n == 2:
                        turn(it, "q")
                    if n == 4:
                        turn(it, "k")
                    if n == 6:
                        if not is_first(i) and not is_first(i, 1):
                            dve.wait_ge(bounced, i * 16 - 16)
                        dve.wait_ge(qk_ready, i * 2 + 2)
                        nc.vector.tensor_copy(parts[:, par, 0, :, :], qk[:, :, :]).then_inc(part1, 1)
                    if n == 9:
                        dve.wait_ge(rest1, i + 1)
                        nc.vector.tensor_copy(parts[:, par, 1, :, :], rest[:, :, :]).then_inc(part2, 1)
                    if n == 15:
                        dve.wait_ge(desk.emptied, desk.done(it, "g"))
                        nc.vector.tensor_scalar(eg[:, :], eg[:, :], 1.0, None, ALU.add).then_inc(eg1, 1)
                        dve.wait_ge(eg1, i + 1)
                        nc.vector.reciprocal(eg[:, :], eg[:, :]).then_inc(eg2, 1)
                        dve.wait_ge(eg2, i + 1)
                        nc.vector.tensor_tensor(silu[:, par, :], eg[:, :], gate[:, :], ALU.mult)\
                            .then_inc(silu_ready, 1)
                if within(i, 0, B - 2):
                    if n == 11:
                        ln_measure(after(it))
                    if n == 13:
                        ln_apply(after(it))

            def decayed(it, n):
                h = (n % QUAD) * QUAD + n // QUAD
                dve.wait_ge(sr.filled, sr.nth(it, n))
                if not (isinstance(it[0], int) and it[0] == 0 and n < AB):
                    dve.wait_ge(av_done, it[0] * H + n - AB + 1)
                nc.vector.tensor_tensor(att[:, n % AB, :], sr.bank(it, n)[:, 0:T + P], decay[:, h, :], ALU.mult)\
                    .then_inc(sr.emptied, 1)

            def step(it, inner=False):
                if finish(it):
                    dve.wait_ge(av_done, (it[0] - 1) * H)
                for n in range(H):
                    if attend(it):
                        decayed(before(it), n)
                    small(it, n)

            dve.wait_ge(k.loaded, k.loaded_count)
            dve.wait_ge(loaded, LOADS)
            ln_measure((0, 0))
            ln_apply((0, 0))
            steps(dve, 0, B + 1, step, lead=2, trail=3)

        @block.gpsimd
        def _(pool):
            def ln_root(it):
                pool.wait_ge(ln_aggr, it[0] + 1)
                nc.gpsimd.tensor_tensor(veps[:, :], mv[:, :, 1], k.eps[:, 0:TT], ALU.add).then_inc(ln_veps, 1)
                pool.wait_ge(ln_veps, it[0] + 1)
                nc.gpsimd.tensor_tensor(rstd[:, :], veps[:, :], k.minus_half[:, 0:TT], ALU.pow).then_inc(ln_rstd, 1)

            def step(it, inner=False):
                i, par = it
                if prep(it):
                    for u, (src, turned) in enumerate(((qp, qp_turned), (kp, kp_turned))):
                        pool.wait_ge(turned, i + 1)
                        nc.gpsimd.tensor_tensor(qk[:, u, :], src[:, 0, :], src[:, 1, :], ALU.add).then_inc(qk_ready, 1)
                    pool.wait_ge(part1, i + 1)
                    nc.gpsimd.tensor_tensor(rest[:, :, :], qk[:, :, :], parts[:, par, 0, :, :], ALU.subtract)\
                        .then_inc(rest1, 1)
                if finish(it):
                    pool.wait_ge(desk.emptied, desk.done(it, "gv"))
                    nc.gpsimd.tensor_tensor(veps_y[:, :], var[:, :], k.eps[:, 0:1], ALU.add).then_inc(y_veps, 1)
                    pool.wait_ge(y_veps, i - 1)
                    nc.gpsimd.tensor_tensor(rstd_y[:, :], veps_y[:, :], k.minus_half[:, 0:1], ALU.pow)\
                        .then_inc(y_rstd, 1)
                if prep(it):
                    pool.wait_ge(part2, i + 1)
                    nc.gpsimd.tensor_tensor(parts[:, par, 2, :, :], rest[:, :, :], parts[:, par, 1, :, :],
                                            ALU.subtract).then_inc(parts_ready, 1)
                if finish(it):
                    b = i - 2
                    pool.wait_ge(desk.emptied, desk.done(it, "o"))
                    nc.gpsimd.tensor_tensor(x_b[:, b, :, :], x_b[:, b, :, :], ob[:, :, :], ALU.add).then_inc(x_done, 1)
                if within(i, 0, B - 2):
                    ln_root(after(it))

            pool.wait_ge(k.loaded, k.loaded_count)
            ln_root((0, 0))
            steps(pool, 0, B + 1, step, lead=2, trail=3)


def head_at(hs):
    return (hs % QUAD) * QUAD + hs // QUAD


def layer1_weights(nc, a, io):
    w = Weights()
    w.keys, w.values = a.sb("keys", [P, E1, P]), a.sb("values", [P, E1, C])
    w.selw, w.ln = a.sb("selw", [P, E1]), a.sb("ln", [P, 4])
    w.ws = a.sb("ws", [SLOTS * HD, 2, H, C], BF16)
    w.experts_loaded, w.experts_count = a.sem("experts_loaded"), 32
    w.small_loaded, w.small_count = a.sem("small_loaded"), 32
    scratch = nc.dram_tensor("l1_scratch", (P, 3, 2, C), BF16, kind="Internal").ap()
    with ExitStack() as ctx:
        b = Pool_(nc, ctx, "wp")
        wp, rest = b.sb("wp", [P, 2, C]), b.sb("rest", [P, 2, C])
        parts = b.sb("parts", [P, 3, 2, C], BF16)
        loaded, part1, rest1, part2, parts_ready, bounced, stacked = [b.sem(n) for n in (
            "loaded", "part1", "rest1", "part2", "parts_ready", "bounced", "stacked")]
        block = ctx.enter_context(nc.Block())

        @block.sync
        def _(sp):
            sp.dma_start(wp[:, :, :], io["wp"]).then_inc(loaded, 16)
            sp.dma_start(w.selw[:, :], io["selw"]).then_inc(w.small_loaded, 16)
            sp.dma_start(w.ln[:, :], io["ln"]).then_inc(w.small_loaded, 16)
            sp.wait_ge(parts_ready, 1)
            sp.dma_start(scratch, parts[:, :, :, :]).then_inc(bounced, 16)
            sp.wait_ge(bounced, 16)
            for n in range(SLOTS):
                for u in range(2):
                    sp.dma_start(w.ws[n * HD:(n + 1) * HD, u, :, :],
                                 scratch[:, KSLOT[n], u, :].rearrange("(h d) f -> d h f", d=HD)).then_inc(stacked, 16)
            sp.dma_start(w.keys[:, :, :], io["keys"]).then_inc(w.experts_loaded, 16)
            sp.dma_start(w.values[:, :, :], io["values"]).then_inc(w.experts_loaded, 16)
            sp.wait_ge(w.small_loaded, w.small_count)
            sp.wait_ge(stacked, 16 * 2 * SLOTS)

        @block.vector
        def _(dve):
            dve.wait_ge(loaded, 16)
            nc.vector.tensor_copy(parts[:, 0, :, :], wp[:, :, :]).then_inc(part1, 1)
            dve.wait_ge(part1, 1)
            nc.vector.tensor_tensor(rest[:, :, :], wp[:, :, :], parts[:, 0, :, :], ALU.subtract).then_inc(rest1, 1)
            dve.wait_ge(rest1, 1)
            nc.vector.tensor_copy(parts[:, 1, :, :], rest[:, :, :]).then_inc(part2, 1)
            dve.wait_ge(part2, 1)
            nc.vector.tensor_tensor(parts[:, 2, :, :], rest[:, :, :], parts[:, 1, :, :], ALU.subtract)\
                .then_inc(parts_ready, 1)

    return w


def relative_ffn(nc, tag, x_sb, k, w, io):
    with ExitStack() as ctx:
        a = Pool_(nc, ctx, tag)
        x2t = a.sb("x2t", [P, B * TT, P])
        gates = a.sb("gates", [P, B * TT, E1])
        softmax_attention(nc, f"{tag}a", x_sb, k, io, w, x2t, gates)
        mixture(nc, f"{tag}m", x_sb, k, w, x2t, gates)


def plain_attention(nc, tag, x_sb, k, io):
    softmax_attention(nc, tag, x_sb, k, io)


def softmax_attention(nc, tag, x_sb, k, io, w=None, x2t_all=None, gates=None):
    rel = w is not None
    x_b = x_sb[:, :, :].rearrange("p (b t) c -> p b t c", t=TT)
    SB = 2 if rel else 4
    NR, RRS, AHEAD = 16, 8, 3
    with ExitStack() as ctx:
        a = Pool_(nc, ctx, tag)
        wq, wo = a.sb("wq", [P, 3, C]), a.sb("wo", [P, C])
        stats, mv = a.sb("stats", [P, TT, 6]), a.sb("mv", [P, TT, 2])
        veps, rstd = a.sb("veps", [P, TT]), a.sb("rstd", [P, TT])
        xn, xt = a.sb("xn", [P, TT, C]), a.sb("xt", [P, T])
        qk, rest = a.sb("qk", [P, 2, T]), a.sb("rest", [P, 2, T])
        parts = a.sb("parts", [P, 2, 3, 2, T], BF16)
        qs, ks = a.sb("qs", [SLOTS * HD, 2, H, T], BF16), a.sb("ks", [SLOTS * HD, 2, H, T], BF16)
        scratch = nc.dram_tensor(f"{tag}_scratch", (2, P, 3, 2, T), BF16, kind="Internal").ap()
        vm = a.sb("vm", [P, 2, TT, QUAD, C])
        nm = a.sb("nm", [P, SB, 2])
        zs = a.sb("zs", [P, 2, TT, H])
        pr = a.sb("pr", [P, 4, 2, T])
        pts = a.sb("pts", [P, 2, TT, QUAD, T])
        rz, rz8, rzb = a.sb("rz", [P, TT, H]), a.sb("rz8", [P, TT, H, HD]), a.sb("rzb", [P, T])
        yn, ob = a.sb("yn", [P, T]), a.sb("ob", [P, TT, C])
        if rel:
            src = a.sb("src", [P, B, TT, C])
            pe_t, turn = a.sb("pe", [P, T]), a.sb("turn", [P, 2, T])
            tmp, rr = a.sb("tmp", [P, 2, 2, T]), a.sb("rr", [P, RRS, T])
            s1, x2 = a.sb("s1", [P, TT, C]), a.sb("x2", [P, TT, C])
            stats2, mv2 = a.sb("stats2", [P, TT, 6]), a.sb("mv2", [P, TT, 2])
            veps2, rstd2 = a.sb("veps2", [P, TT]), a.sb("rstd2", [P, TT])
            x2s = a.sb("x2s", [P, T])
            sel, best = a.sb("sel", [P, TT, E1]), a.sb("best", [P, TT, 8])
            best_at, best_f = a.sb("best_at", [P, TT, 8], U32), a.sb("best_f", [P, TT, TOPK])
            pick, pair = a.sb("pick", [P, TT, TOPK, E1]), a.sb("pair", [P, TT, 2, E1])
        else:
            bp = a.sb("bp", [P, C])

        sr = Ring(a.ps("sr", [P, SB, 512]), a.sem("sr_filled"), a.sem("sr_emptied"), NR, SB)
        tr = [Ring(a.ps(f"tr{e}", [P, 1, 512]), a.sem(f"tr{e}_filled"), a.sem(f"tr{e}_emptied"), NR // 2, 1)
              for e in range(2)]
        y_ps = a.ps("y", [P, 512])
        late = ["rz", "o"] + (["x2t", "sel"] if rel else [])
        desk = Desk(a.ps("desk", [P, 1, 512]), a.sem("desk_filled"), a.sem("desk_emptied"),
                    ["xt", "qk", "rz", "v", "o"] + late[2:], late, 1)
        if rel:
            ur = Ring(a.ps("ur", [P, 2, 512]), a.sem("ur_filled"), a.sem("ur_emptied"), H, 2)
        names = ("loaded wq_scaled vm_zero ln_stats ln_aggr ln_veps ln_rstd xn_ready part1 rest1 part2 parts_ready "
                 "bounced stacked passed nm_ready av_done rz_ready rz8_ready yn_ready bias_added x_done").split()
        (loaded, wq_scaled, vm_zero, ln_stats, ln_aggr, ln_veps, ln_rstd, xn_ready, part1, rest1, part2, parts_ready,
         bounced, stacked, passed, nm_ready, av_done, rz_ready, rz8_ready, yn_ready, bias_added, x_done) = [
             a.sem(n) for n in names]
        if rel:
            names = ("src_ready src_stats src_aggr src_veps src_rstd turned rr_ready s1_ready s1_stats s1_aggr s1_veps "
                     "s1_rstd x2_ready gate_step gates_ready").split()
            (src_ready, src_stats, src_aggr, src_veps, src_rstd, turned, rr_ready, s1_ready, s1_stats, s1_aggr,
             s1_veps, s1_rstd, x2_ready, gate_step, gates_ready) = [a.sem(n) for n in names]
        block = ctx.enter_context(nc.Block())

        def prep(it):
            return within(it[0], 0, B - 1)

        def attend(it):
            return within(it[0], 1, B)

        def finish(it):
            return within(it[0], 2, B + 1)

        def turning(it, n):
            if n >= 2:
                return (before(it), n - 2) if attend(it) else (None, None)
            return (before(it, 2), NR - 2 + n) if finish(it) else (None, None)

        def relating(it, n):
            if n + AHEAD < NR:
                return (before(it), n + AHEAD) if attend(it) else (None, None)
            return (it, n + AHEAD - NR) if prep(it) else (None, None)

        def later_than(b, first):
            return not isinstance(b[0], int) or b[0] >= first

        LOADS = 16 * (4 if rel else 3)

        @block.sync
        def _(sp):
            sp.dma_start(wq[:, :, :], io["w4" if rel else "w5"].rearrange("p (n c) -> p n c", c=C)).then_inc(loaded, 16)
            sp.dma_start(wo[:, :], io["w4p" if rel else "w5p"]).then_inc(loaded, 16)
            if rel:
                sp.dma_start(pe_t[:, :], io["pe"]).then_inc(loaded, 16)
                sp.dma_start(turn[:, :, :], io["turn"]).then_inc(loaded, 16)
            else:
                sp.dma_start(bp[:, :], io["b5p"].partition_broadcast(P)).then_inc(loaded, 16)
            stack_parts(sp, parts, scratch, qs, ks, parts_ready, bounced, stacked, passed, sr)

        @block.tensor
        def _(pe):
            def fill(it, name):
                pe.wait_ge(desk.emptied, desk.nth(it, name))
                return desk.bank(it, name)

            def relate(b, hs):
                if hs == 0:
                    pe.wait_ge(stacked, b[0] * 192 + 192)
                pe.wait_ge(ur.emptied, ur.nth(b, hs))
                out = ur.bank(b, hs)
                h = head_at(hs)
                for u in range(2):
                    mm = nc.tensor.matmul(out[:, u * T:(u + 1) * T], w.ws[:, u, h, :], qs[:, b[1], h, :],
                                          start=True, stop=True)
                mm.then_inc(ur.filled, 1)

            def scores(b, n):
                r, jj, t = n // QUAD, n // 2 % 2, n % 2
                pe.wait_ge(sr.emptied, sr.nth(b, n))
                if rel and t == 0:
                    pe.wait_ge(rr_ready, b[0] * H + n + 2)
                for x in range(2):
                    h = (2 * jj + x) * QUAD + r
                    out = sr.bank(b, n)[:, x * T:(x + 1) * T]
                    mm = nc.tensor.matmul(out, qs[:, b[1], h, t * P:(t + 1) * P], ks[:, b[1], h, :],
                                          start=True, stop=not rel)
                    if rel:
                        mm = nc.tensor.matmul(out, rr[:, (n - t + x) % RRS, t * P:(t + 1) * P], pe_t[:, :],
                                              start=False, stop=True)
                mm.then_inc(sr.filled, 1)

            def turn_round(b, n):
                ring = tr[n % 2]
                pe.wait_ge(ring.emptied, ring.nth(b, n // 2))
                pe.wait_ge(sr.emptied, sr.done(b, n))
                for st in range(TT):
                    for x in range(2):
                        o = (st * 2 + x) * P
                        mm = nc.tensor.transpose(ring.bank(b, n // 2)[:, o:o + P],
                                                 pr[:, n % 4, x, st * P:(st + 1) * P], k.ident)
                mm.then_inc(ring.filled, 1)

            def values(b, r):
                for e in range(2):
                    pe.wait_ge(tr[e].emptied, tr[e].done(b, 2 * r + 1))
                if r == 0 and later_than(b, 1):
                    pe.wait_ge(yn_ready, b[0])
                for st in range(TT):
                    for j in range(QUAD):
                        q = slice(j * QUAD * HD, (j + 1) * QUAD * HD)
                        mm = nc.tensor.matmul(y_ps[q, 0:T], vm[:, b[1], st, r, q], pts[:, r % 2, st, j, :],
                                              start=(r == 0 and st == 0), stop=(r == QUAD - 1 and st == TT - 1),
                                              skip_group_check=True)
                mm.then_inc(av_done, 1)

            def small(it, n):
                i, par = it
                if n == 0 and prep(it):
                    pe.wait_ge(xn_ready, i * TT + TT)
                    out = fill(it, "xt")
                    for t in range(TT):
                        mm = nc.tensor.transpose(out[:, t * P:(t + 1) * P], xn[:, t, :], k.ident)
                    mm.then_inc(desk.filled, 1)
                if n == 1 and prep(it):
                    out = fill(it, "qk")
                    for u in range(2):
                        mm = nc.tensor.matmul(out[:, u * T:(u + 1) * T], wq[:, u, :], xt[:, :], start=True, stop=True)
                    mm.then_inc(desk.filled, 1)
                if n == 3 and finish(it):
                    pe.wait_ge(rz8_ready, i - 1)
                    out = fill(it, "rz")
                    for t in range(TT):
                        mm = nc.tensor.transpose(out[:, t * P:(t + 1) * P],
                                                 rz8[:, t, :, :].rearrange("p h d -> p (h d)"), k.ident)
                    mm.then_inc(desk.filled, 1)
                if n == 4 and prep(it):
                    out = fill(it, "v")
                    for t in range(TT):
                        mm = nc.tensor.matmul(out[:, t * P:(t + 1) * P], xt[:, t * P:(t + 1) * P], wq[:, 2, :],
                                              start=True, stop=True)
                    mm.then_inc(desk.filled, 1)
                if n == 6 and finish(it):
                    out = fill(it, "o")
                    pe.wait_ge(yn_ready, i - 1)
                    for t in range(TT):
                        mm = nc.tensor.matmul(out[:, t * P:(t + 1) * P], yn[:, t * P:(t + 1) * P], wo[:, :],
                                              start=True, stop=True)
                    mm.then_inc(desk.filled, 1)
                if rel and n == 12 and finish(it):
                    out = fill(it, "x2t")
                    pe.wait_ge(x2_ready, (i - 1) * TT)
                    for t in range(TT):
                        mm = nc.tensor.transpose(out[:, t * P:(t + 1) * P], x2[:, t, :], k.ident)
                    mm.then_inc(desk.filled, 1)
                if rel and n == 14 and finish(it):
                    out = fill(it, "sel")
                    for t in range(TT):
                        mm = nc.tensor.matmul(out[:, t * E1:(t + 1) * E1], x2s[:, t * P:(t + 1) * P], w.selw[:, :],
                                              start=True, stop=True)
                    mm.then_inc(desk.filled, 1)

            def step(it, inner=False):
                for n in range(NR):
                    small(it, n)
                    if rel:
                        b, hs = relating(it, n)
                        if b is not None:
                            relate(b, hs)
                    if attend(it):
                        if n == 0 and not rel:
                            pe.wait_ge(stacked, (it[0] - 1) * 192 + 192)
                        scores(before(it), n)
                    b, m = turning(it, n)
                    if b is not None:
                        turn_round(b, m)
                    if n in (7, 11, 15) and attend(it):
                        values(before(it), (n - 7) // 4)
                    if n == 3 and finish(it):
                        values(before(it, 2), 3)

            pe.wait_ge(k.loaded, k.loaded_count)
            pe.wait_ge(loaded, LOADS)
            pe.wait_ge(wq_scaled, 1)
            pe.wait_ge(vm_zero, 1)
            steps(pe, 0, B + 1, step, lead=2, trail=2)

        def take_turned(eng, b, n, copy):
            r, jj, t = n // QUAD, n // 2 % 2, n % 2
            ring = tr[t]
            eng.wait_ge(ring.filled, ring.nth(b, n // 2))
            if n % QUAD < 2 and (r >= 2 or later_than(b, 1)):
                eng.wait_ge(av_done, b[0] * QUAD + r - 1)
            copy(pts[:, r % 2, :, 2 * jj:2 * jj + 2, t * P:(t + 1) * P],
                 ring.bank(b, n // 2).rearrange("p (s x t) -> p s x t", s=TT, x=2)).then_inc(ring.emptied, 1)

        @block.scalar
        def _(act):
            act.sem_inc(desk.emptied, 1)
            act.sem_inc(tr[1].emptied, 1)
            act.sem_inc(sr.emptied, SB)

            def copy(dst, src_):
                return nc.scalar.activation(dst, src_, ACT.Copy)

            def taken(it, name):
                act.wait_ge(desk.filled, desk.nth(it, name))
                return desk.bank(it, name)

            def exponentials(b, n):
                t, hs = n % 2, n - n % 2
                act.wait_ge(nm_ready, b[0] * NR + n + 1)
                if n >= 4 or later_than(b, 1):
                    act.wait_ge(tr[t].filled, b[0] * (NR // 2) + n // 2 - 1)
                if n == 0 and later_than(b, 2):
                    act.wait_ge(rz_ready, b[0] - 1)
                for x in range(2):
                    h = head_at(hs + x)
                    last = nc.scalar.activation(pr[:, n % 4, x, :], sr.bank(b, n)[:, x * T:(x + 1) * T], ACT.Exp,
                                                bias=nm[:, n % SB, x:x + 1], accum_out=zs[:, b[1], t, h:h + 1])
                last.then_inc(sr.emptied, 1)

            def small(it, n):
                i, par = it
                if n == 0 and prep(it):
                    bank = taken(it, "xt")
                    if rel:
                        last = nc.scalar.activation(xt[:, :], bank[:, 0:T], ACT.Identity, scale=w.ln[:, 0:1],
                                                    bias=w.ln[:, 1:2])
                    else:
                        last = copy(xt[:, :], bank[:, 0:T])
                    last.then_inc(desk.emptied, 1)
                if n == 1 and prep(it):
                    bank = taken(it, "qk")
                    if not is_first(i):
                        act.wait_ge(rest1, i)
                    copy(qk[:, :, :].rearrange("p u t -> p (u t)"), bank).then_inc(desk.emptied, 1)
                if n == 3 and finish(it):
                    bank = taken(it, "rz")
                    copy(rzb[:, :], bank[:, 0:T]).then_inc(desk.emptied, 1)
                if n == 4 and prep(it):
                    bank = taken(it, "v")
                    if not is_first(i) and not is_first(i, 1):
                        act.wait_ge(av_done, (i - 1) * QUAD)
                    for t in range(TT):
                        last = copy(heads_of((vm, par, t)),
                                    bank[:, t * P:(t + 1) * P].rearrange("p (j r d) -> p r j d", r=QUAD, d=HD))
                    last.then_inc(desk.emptied, 1)
                if n == 6 and finish(it):
                    bank = taken(it, "o")
                    if not is_first(i, 2):
                        act.wait_ge(s1_ready if rel else x_done, i - 2)
                    copy(ob[:, :, :].rearrange("p t c -> p (t c)"), bank[:, 0:T]).then_inc(desk.emptied, 1)
                if rel and n == 12 and finish(it):
                    bank = taken(it, "x2t")
                    nc.scalar.activation(x2s[:, :], bank[:, 0:T], ACT.Identity, scale=w.ln[:, 2:3], bias=w.ln[:, 3:4])
                    tiles = x2t_all[:, :, :].rearrange("p (b t) c -> p b (t c)", t=TT)
                    nc.scalar.activation(tiles[:, i - 2, :], bank[:, 0:T], ACT.Identity, scale=w.ln[:, 2:3],
                                         bias=w.ln[:, 3:4]).then_inc(desk.emptied, 1)
                if rel and n == 14 and finish(it):
                    bank = taken(it, "sel")
                    if not is_first(i, 2):
                        act.wait_ge(gates_ready, i - 2)
                    nc.scalar.activation(sel[:, :, :].rearrange("p t e -> p (t e)"), bank[:, 0:TT * E1], ACT.Exp,
                                         scale=-1.0).then_inc(desk.emptied, 1)

            def step(it, inner=False):
                for n in range(NR):
                    small(it, n)
                    b, m = turning(it, n)
                    if b is not None and m % 2:
                        take_turned(act, b, m, copy)
                    if attend(it):
                        exponentials(before(it), n)

            act.wait_ge(vm_zero, 1)
            if rel:
                act.wait_ge(w.small_loaded, w.small_count)
            steps(act, 0, B + 1, step, lead=2, trail=3)

        @block.vector
        def _(dve):
            dve.sem_inc(tr[0].emptied, 1)
            if rel:
                dve.sem_inc(ur.emptied, 2)
            nc.vector.memset(vm[:, :, :, :, :].rearrange("p a b c d -> p (a b c d)"), 0.0).then_inc(vm_zero, 1)

            def measure(i, value, stats_, mv_, stats_sem, aggr_sem):
                for t in range(TT):
                    nc.vector.bn_stats(stats_[:, t, :], value(t)).then_inc(stats_sem, 1)
                dve.wait_ge(stats_sem, i * TT + TT)
                nc.vector.memset(k.idle, 0.0)
                for t in range(TT):
                    last = nc.vector.bn_aggr(mv_[:, t, :], stats_[:, t, :])
                last.then_inc(aggr_sem, 1)

            def normalise(dst, value, mv_, rstd_, ready):
                for t in range(TT):
                    nc.vector.tensor_scalar(dst(t), value(t), mv_[:, t, 0:1], rstd_[:, t:t + 1], ALU.subtract,
                                            ALU.mult).then_inc(ready, 1)

            def prepare(it, stage):
                i = it[0]
                x_of = lambda t: x_b[:, i, t, :]
                if stage == 0:
                    if rel:
                        measure(i, x_of, stats, mv, src_stats, src_aggr)
                if stage == 1 and rel:
                    dve.wait_ge(src_rstd, i + 1)
                    normalise(lambda t: src[:, i, t, :], x_of, mv, rstd, src_ready)
                if stage == 2:
                    if rel:
                        dve.wait_ge(src_ready, i * TT + TT)
                        nc.vector.memset(k.idle, 0.0)
                        measure(i, lambda t: src[:, i, t, :], stats2, mv2, ln_stats, ln_aggr)
                    else:
                        measure(i, x_of, stats, mv, ln_stats, ln_aggr)
                if stage == 3:
                    dve.wait_ge(ln_rstd, i + 1)
                    if rel:
                        normalise(lambda t: xn[:, t, :], lambda t: src[:, i, t, :], mv2, rstd2, xn_ready)
                    else:
                        normalise(lambda t: xn[:, t, :], x_of, mv, rstd, xn_ready)

            def maxima(b, n):
                dve.wait_ge(sr.filled, sr.nth(b, n))
                nc.vector.tensor_reduce(nm[:, n % SB, :], sr.bank(b, n).rearrange("p (x s) -> p x s", x=2), AX.X,
                                        ALU.max, negate=True).then_inc(nm_ready, 1)

            def rotate(b, hs):
                dve.wait_ge(ur.filled, ur.nth(b, hs))
                if hs >= 2 or later_than(b, 1):
                    dve.wait_ge(rr_ready, b[0] * H + hs - 1)
                nc.vector.tensor_tensor(tmp[:, hs % 2, :, :], ur.bank(b, hs).rearrange("p (u t) -> p u t", u=2),
                                        turn[:, :, :], ALU.mult).then_inc(ur.emptied, 1)

            def gate(it):
                i = it[0] - 2
                steps_ = [0]

                def stepped(last):
                    last.then_inc(gate_step, 1)
                    steps_[0] += 1
                    dve.wait_ge(gate_step, i * 8 + steps_[0])

                dve.wait_ge(desk.emptied, desk.done(it, "sel"))
                stepped(nc.vector.tensor_scalar(sel[:, :, :], sel[:, :, :], 1.0, None, ALU.add))
                stepped(nc.vector.reciprocal(sel[:, :, :], sel[:, :, :]))
                nc.vector.memset(k.idle, 0.0)
                for t in range(TT):
                    last = nc.vector.max(best[:, t, :], sel[:, t, :])
                stepped(last)
                nc.vector.memset(k.idle, 0.0)
                for t in range(TT):
                    last = nc.vector.max_index(best_at[:, t, :], best[:, t, :], sel[:, t, :])
                stepped(last)
                stepped(nc.vector.tensor_copy(best_f[:, :, :], best_at[:, :, 0:TOPK]))
                for t in range(TT):
                    last = nc.vector.tensor_tensor(pick[:, t, :, :], k.iota32.unsqueeze(1).to_broadcast([P, TOPK, E1]),
                                                   best_f[:, t, :].unsqueeze(2).to_broadcast([P, TOPK, E1]),
                                                   ALU.is_equal)
                stepped(last)
                for t in range(TT):
                    last = nc.vector.tensor_tensor(pick[:, t, :, :], pick[:, t, :, :],
                                                   best[:, t, 0:TOPK].unsqueeze(2).to_broadcast([P, TOPK, E1]),
                                                   ALU.mult)
                stepped(last)
                stepped(nc.vector.tensor_tensor(pair[:, :, :, :], pick[:, :, 0:2, :], pick[:, :, 2:4, :], ALU.add))
                g = gates[:, :, :].rearrange("p (b t) e -> p b t e", t=TT)
                nc.vector.tensor_tensor(g[:, i, :, :], pair[:, :, 0, :], pair[:, :, 1, :], ALU.add)\
                    .then_inc(gates_ready, 1)

            def small(it, n):
                i, par = it
                if finish(it):
                    b = before(it, 2)
                    if n == 1:
                        dve.wait_ge(sr.emptied, sr.done(b, NR - 1))
                        nc.vector.reciprocal(rz[:, :, :], zs[:, par, :, :]).then_inc(rz_ready, 1)
                        dve.wait_ge(rz_ready, i - 1)
                        nc.vector.tensor_copy(rz8[:, :, :, :], rz[:, :, :].unsqueeze(3).to_broadcast([P, TT, H, HD]))\
                            .then_inc(rz8_ready, 1)
                    if n == 4:
                        dve.wait_ge(av_done, (i - 1) * QUAD)
                        dve.wait_ge(desk.emptied, desk.done(it, "rz"))
                        nc.vector.tensor_tensor(yn[:, :], y_ps[:, 0:T], rzb[:, :], ALU.mult).then_inc(yn_ready, 1)
                    if rel and n == 7:
                        dve.wait_ge(desk.emptied, desk.done(it, "o"))
                        nc.vector.tensor_tensor(s1[:, :, :], ob[:, :, :], src[:, i - 2, :, :], ALU.add)\
                            .then_inc(s1_ready, 1)
                        dve.wait_ge(s1_ready, i - 1)
                        nc.vector.scalar_tensor_tensor(x_b[:, i - 2, :, :], s1[:, :, :], 0.5, x_b[:, i - 2, :, :],
                                                       ALU.mult, ALU.add)
                        measure(i - 2, lambda t: s1[:, t, :], stats2, mv2, s1_stats, s1_aggr)
                    if rel and n == 9:
                        dve.wait_ge(s1_rstd, i - 1)
                        normalise(lambda t: x2[:, t, :], lambda t: s1[:, t, :], mv2, rstd2, x2_ready)
                    if rel and n == 15:
                        gate(it)
                if prep(it):
                    if n == 2:
                        if not is_first(i) and not is_first(i, 1):
                            dve.wait_ge(bounced, i * 16 - 16)
                        dve.wait_ge(desk.emptied, desk.done(it, "qk"))
                        nc.vector.tensor_copy(parts[:, par, 0, :, :], qk[:, :, :]).then_inc(part1, 1)
                    if n == 3:
                        dve.wait_ge(rest1, i + 1)
                        nc.vector.tensor_copy(parts[:, par, 1, :, :], rest[:, :, :]).then_inc(part2, 1)
                if within(i, 0, B - 2) and n in (10, 11, 12, 14):
                    prepare(after(it), (10, 11, 12, 14).index(n))

            def step(it, inner=False):
                for n in range(NR):
                    if rel:
                        b, hs = relating(it, n)
                        if b is not None:
                            rotate(b, hs)
                    if attend(it):
                        maxima(before(it), n)
                    b, m = turning(it, n)
                    if b is not None and m % 2 == 0:
                        take_turned(dve, b, m, nc.vector.tensor_copy)
                    small(it, n)

            dve.wait_ge(k.loaded, k.loaded_count)
            dve.wait_ge(loaded, LOADS)
            nc.vector.tensor_scalar(wq[:, 0, :], wq[:, 0, :], float(np.float32(HD ** -0.5)), None, ALU.mult)\
                .then_inc(wq_scaled, 1)
            for stage in range(4):
                prepare((0, 0), stage)
            steps(dve, 0, B + 1, step, lead=2, trail=3)

        @block.gpsimd
        def _(pool):
            def root(i, mv_, veps_, rstd_, aggr_sem, veps_sem, rstd_sem):
                pool.wait_ge(aggr_sem, i + 1)
                nc.gpsimd.tensor_tensor(veps_[:, :], mv_[:, :, 1], k.eps[:, 0:TT], ALU.add).then_inc(veps_sem, 1)
                pool.wait_ge(veps_sem, i + 1)
                nc.gpsimd.tensor_tensor(rstd_[:, :], veps_[:, :], k.minus_half[:, 0:TT], ALU.pow).then_inc(rstd_sem, 1)

            def prepare(it, stage):
                i = it[0]
                if rel and stage == 0:
                    root(i, mv, veps, rstd, src_aggr, src_veps, src_rstd)
                if rel and stage == 2:
                    root(i, mv2, veps2, rstd2, ln_aggr, ln_veps, ln_rstd)
                if not rel and stage == 2:
                    root(i, mv, veps, rstd, ln_aggr, ln_veps, ln_rstd)

            def add_forms(b, hs):
                if hs % 2 == 0 and (hs >= RRS or later_than(b, 1)):
                    pool.wait_ge(sr.filled, b[0] * NR + hs + 2 - RRS)
                pool.wait_ge(ur.emptied, ur.done(b, hs))
                nc.gpsimd.tensor_tensor(rr[:, hs % RRS, :], tmp[:, hs % 2, 0, :], tmp[:, hs % 2, 1, :], ALU.add)\
                    .then_inc(rr_ready, 1)

            def small(it, n):
                i, par = it
                if prep(it):
                    if n == 2:
                        pool.wait_ge(part1, i + 1)
                        nc.gpsimd.tensor_tensor(rest[:, :, :], qk[:, :, :], parts[:, par, 0, :, :], ALU.subtract)\
                            .then_inc(rest1, 1)
                    if n == 3:
                        pool.wait_ge(part2, i + 1)
                        nc.gpsimd.tensor_tensor(parts[:, par, 2, :, :], rest[:, :, :], parts[:, par, 1, :, :],
                                                ALU.subtract).then_inc(parts_ready, 1)
                if finish(it):
                    if rel and n == 7:
                        root(i - 2, mv2, veps2, rstd2, s1_aggr, s1_veps, s1_rstd)
                    if not rel and n == 7:
                        pool.wait_ge(desk.emptied, desk.done(it, "o"))
                        nc.gpsimd.tensor_tensor(ob[:, :, :], ob[:, :, :], bp[:, :].unsqueeze(1)
                                                .to_broadcast([P, TT, C]), ALU.add).then_inc(bias_added, 1)
                        pool.wait_ge(bias_added, i - 1)
                        nc.gpsimd.tensor_tensor(x_b[:, i - 2, :, :], x_b[:, i - 2, :, :], ob[:, :, :], ALU.add)\
                            .then_inc(x_done, 1)
                if within(i, 0, B - 2) and n in (10, 11, 12, 14):
                    prepare(after(it), (10, 11, 12, 14).index(n))

            def step(it, inner=False):
                for n in range(NR):
                    if rel:
                        b, hs = relating(it, n)
                        if b is not None:
                            add_forms(b, hs)
                    small(it, n)

            pool.wait_ge(k.loaded, k.loaded_count)
            pool.wait_ge(loaded, LOADS)
            for stage in range(4):
                prepare((0, 0), stage)
            steps(pool, 0, B + 1, step, lead=2, trail=3)


def mixture(nc, tag, x_sb, k, w, x2t, gates):
    G, GT = 8, 4
    HB, OB = 4, 4
    LAG = 2
    with ExitStack() as ctx:
        a = Pool_(nc, ctx, tag)
        ht = a.sb("ht", [P, HB, GT * P])
        gg = a.sb("gg", [P, GT, E1])
        acc = a.sb("acc", [P, GT, C])
        hr = Ring(a.ps("hr", [P, HB, 512]), a.sem("hr_filled"), a.sem("hr_emptied"), E1, HB)
        our = Ring(a.ps("our", [P, OB, 512]), a.sem("our_filled"), a.sem("our_emptied"), E1, OB)
        gg_ready = a.sem("gg_ready")
        block = ctx.enter_context(nc.Block())
        x_g = x_sb[:, :, :].rearrange("p (g t) c -> p g t c", t=GT)
        x2_g = x2t[:, :, :].rearrange("p (g t) c -> p g (t c)", t=GT)
        gates_g = gates[:, :, :].rearrange("p (g t) e -> p g t e", t=GT)

        @block.tensor
        def _(pe):
            def hidden(it, e):
                pe.wait_ge(hr.emptied, hr.nth(it, e))
                nc.tensor.matmul(hr.bank(it, e), w.keys[:, e, :], x2_g[:, it[0], :], start=True, stop=True)\
                    .then_inc(hr.filled, 1)

            def output(it, e):
                pe.wait_ge(our.emptied, our.nth(it, e))
                pe.wait_ge(hr.emptied, hr.done(it, e))
                for t in range(GT):
                    mm = nc.tensor.matmul(our.bank(it, e)[:, t * P:(t + 1) * P], ht[:, e % HB, t * P:(t + 1) * P],
                                          w.values[:, e, :], start=True, stop=True)
                mm.then_inc(our.filled, 1)

            pe.wait_ge(w.experts_loaded, w.experts_count)
            with pe.Fori(0, G) as g:
                it = (g, 0)
                for e in range(E1 + LAG):
                    if e < E1:
                        hidden(it, e)
                    if e >= LAG:
                        output(it, e - LAG)

        @block.scalar
        def _(act):
            act.sem_inc(hr.emptied, HB)
            with act.Fori(0, G) as g:
                it = (g, 0)
                for e in range(E1):
                    act.wait_ge(hr.filled, hr.nth(it, e))
                    nc.scalar.activation(ht[:, e % HB, :], hr.bank(it, e), ACT.Relu).then_inc(hr.emptied, 1)

        @block.vector
        def _(dve):
            dve.sem_inc(our.emptied, OB)
            with dve.Fori(0, G) as g:
                it = (g, 0)
                nc.vector.tensor_copy(gg[:, :, :], gates_g[:, g, :, :]).then_inc(gg_ready, 1)
                dve.wait_ge(gg_ready, g + 1)
                for e in range(E1):
                    dve.wait_ge(our.filled, our.nth(it, e))
                    for t in range(GT):
                        out = our.bank(it, e)[:, t * P:(t + 1) * P]
                        if e == 0:
                            last = nc.vector.tensor_scalar(acc[:, t, :], out, gg[:, t, e:e + 1], None, ALU.mult)
                        else:
                            if t == 0:
                                dve.wait_ge(our.emptied, our.done(it, e - 1))
                            last = nc.vector.scalar_tensor_tensor(acc[:, t, :], out, gg[:, t, e:e + 1], acc[:, t, :],
                                                                  ALU.mult, ALU.add)
                    last.then_inc(our.emptied, 1)
                dve.wait_ge(our.emptied, our.done(it, E1 - 1))
                nc.vector.scalar_tensor_tensor(x_g[:, g, :, :], acc[:, :, :], 0.5, x_g[:, g, :, :], ALU.mult, ALU.add)


class Constants:
    pass


class Weights:
    pass


def constants(nc, a, cst):
    k = Constants()
    table = a.sb("table", [P, cst.shape[1]])
    bf = a.sb("bf", [P, 2 * P], BF16)
    half = a.sb("half", [P, 16])
    k.idle = a.sb("idle", [P, 1])[:, :]
    k.ident = table[:, 0:P]
    k.iota40 = table[:, 2 * P:2 * P + CAP]
    k.iota8 = table[:, 2 * P + CAP:2 * P + CAP + E0]
    k.iota32 = table[:, 2 * P + CAP + E0:2 * P + CAP + E0 + E1]
    k.tri_bf, k.ones_bf = bf[:, 0:P], bf[:, P:2 * P]
    k.eps, k.minus_half = half[:, 0:8], half[:, 8:16]
    k.table, k.bf, k.half, k.source = table, bf, half, cst
    k.loaded, k.loaded_count = a.sem("loaded"), 5
    return k


def load_x(nc, k, x, x_sb):
    with ExitStack() as ctx:
        a = Pool_(nc, ctx, "load")
        x_in, table_in = a.sem("x_in"), a.sem("table_in")
        block = ctx.enter_context(nc.Block())

        @block.sync
        def _(sp):
            sp.dma_start(k.table[:, :], k.source).then_inc(table_in, 16)
            sp.dma_start(x_sb[:, :, :], x.rearrange("b (t p) c -> p (b t) c", p=P)).then_inc(x_in, 16)
            sp.wait_ge(x_in, 16)

        @block.vector
        def _(dve):
            nc.vector.memset(k.ones_bf, 1.0).then_inc(k.loaded, 1)
            nc.vector.memset(k.eps, EPS).then_inc(k.loaded, 1)
            nc.vector.memset(k.minus_half, -0.5).then_inc(k.loaded, 1)
            dve.wait_ge(table_in, 16)
            nc.vector.tensor_copy(k.tri_bf, k.table[:, P:2 * P]).then_inc(k.loaded, 1)
            dve.sem_inc(k.loaded, 1)


def store_x(nc, x_sb, out):
    with ExitStack() as ctx:
        a = Pool_(nc, ctx, "store")
        stored = a.sem("stored")
        block = ctx.enter_context(nc.Block())

        @block.sync
        def _(sp):
            sp.dma_start(out.rearrange("b (t p) c -> p (b t) c", p=P), x_sb[:, :, :]).then_inc(stored, 16)
            sp.wait_ge(stored, 16)


def layer0_weights(nc, a, io):
    w = Weights()
    w.rw1, w.rw2, w.rw3 = a.sb("rw1", [P, HID]), a.sb("rw2", [P, KH, HID]), a.sb("rw3", [P, KH, E0])
    w.rb1, w.rb2, w.rb3 = a.sb("rb1", [P, KH]), a.sb("rb2", [P, KH]), a.sb("rb3", [P, E0])
    w.ew1, w.ew2 = a.sb("ew1", [P, E0, HID]), a.sb("ew2", [P, E0, KH, C])
    w.eb1, w.eb2 = a.sb("eb1", [P, E0, KH]), a.sb("eb2", [P, E0])
    w.router_loaded, w.router_count = a.sem("router_loaded"), 16 * 6
    w.experts_loaded, w.experts_count = a.sem("experts_loaded"), 16 * 4

    def load(sp):
        for dst, src in ((w.rw1[:, :], io["rW1"]), (w.rb1[:, :], io["rb1"]), (w.rw2[:, :, :], io["rW2"]),
                         (w.rb2[:, :], io["rb2"]), (w.rw3[:, :, :], io["rW3"]),
                         (w.rb3[:, :], io["rb3"].partition_broadcast(P))):
            sp.dma_start(dst, src).then_inc(w.router_loaded, 16)
        for dst, src in ((w.ew1[:, :, :], io["eW1"]), (w.eb1[:, :, :], io["eb1"]), (w.eb2[:, :], io["eb2"]),
                         (w.ew2[:, :, :, :], io["eW2"])):
            sp.dma_start(dst, src).then_inc(w.experts_loaded, 16)
        sp.wait_ge(w.router_loaded, w.router_count)
        sp.wait_ge(w.experts_loaded, w.experts_count)

    w.load = load
    return w


def program(nc, io, stages=(1, 2, 3, 4, 5, 6)):
    with ExitStack() as ctx:
        a = Pool_(nc, ctx, "all")
        x_sb = a.sb("x", [P, B * TT, C])
        k = constants(nc, a, io["cst"])
        load_x(nc, k, io["x"], x_sb)
        with ExitStack() as layer:
            w = layer0_weights(nc, Pool_(nc, layer, "l0"), io)
            if 1 in stages:
                routed_ffn(nc, "f1", x_sb, k, w)
                w.load = None
            if 2 in stages:
                retention(nc, "r2", x_sb, k, io)
            if 3 in stages:
                routed_ffn(nc, "f3", x_sb, k, w)
        if 4 in stages or 5 in stages or 6 in stages:
            with ExitStack() as layer:
                w = layer1_weights(nc, Pool_(nc, layer, "l1"), io)
                if 4 in stages:
                    relative_ffn(nc, "f4", x_sb, k, w, io)
                if 5 in stages:
                    plain_attention(nc, "a5", x_sb, k, io)
                if 6 in stages:
                    relative_ffn(nc, "f6", x_sb, k, w, io)
        store_x(nc, x_sb, io["out"])



def shape_tables():
    i = np.arange(P)
    cst = np.concatenate([np.eye(P), (i[:, None] < i[None, :]).astype(float), np.tile(np.arange(CAP), (P, 1)),
                          np.tile(np.arange(E0), (P, 1)), np.tile(np.arange(E1), (P, 1))], 1)
    half = np.arange(0, HD, 2)
    freq = np.repeat(1.0 / 10000.0 ** (half / HD), 2)[None, :] * np.arange(T)[:, None]
    scale = np.repeat((half + 0.4 * HD) / (1.4 * HD), 2)[None, :] ** ((np.arange(T) - T // 2) / 512.0)[:, None]
    sign = np.tile([-1.0, 1.0], HD // 2)[None, :]
    rope = np.stack([np.cos(freq) * scale, np.sin(freq) * scale * sign, np.cos(freq) / scale,
                     np.sin(freq) / scale * sign])
    rope = np.tile(rope.transpose(2, 0, 1), (H, 1, 1))
    gamma = 1.0 - 2.0 ** (-5.0 - np.arange(H))
    diff = np.arange(T)[None, :] - np.arange(P)[:, None]
    decay = np.where(diff[:, None, :] >= 0, gamma[None, :, None] ** np.maximum(diff, 0)[:, None, :], 0.0)
    decay = np.concatenate([decay, decay[:, :, 0:P]], 2) * HD ** -0.5
    group = np.kron(np.eye(H), np.full((HD, HD), 1.0 / HD))
    w = 1.0 / 10000.0 ** (np.arange(0, C, 2) / C)
    ang = w[:, None] * np.arange(T)[None, :]
    pe = np.concatenate([np.sin(ang), np.cos(ang)], 0)
    turn = np.stack([np.tile(np.cos(ang), (2, 1)), np.concatenate([np.sin(ang), -np.sin(ang)], 0)], 1)
    f = lambda v: np.ascontiguousarray(v, np.float32)
    return {"cst": f(cst), "rope": f(rope), "decay": f(decay), "group": f(group), "pe": f(pe), "turn": f(turn)}


def layouts(v):
    v = {n: np.asarray(a) for n, a in v.items()}
    swap = np.arange(C) ^ 1
    qkv0 = v["L0_attn_w_qkv"].reshape(3, C, C)
    qkv1 = v["L1_attn_w_qkv"].reshape(3, C, C)
    col = lambda a: a.reshape(-1, P).T
    out = {
        "x": v["L0_attn_x"],
        "rW1": v["L0_ffn_rW1"], "rb1": col(v["L0_ffn_rb1"]),
        "rW2": v["L0_ffn_rW2"].reshape(KH, P, HID).transpose(1, 0, 2), "rb2": col(v["L0_ffn_rb2"]),
        "rW3": v["L0_ffn_rW3"].reshape(KH, P, E0).transpose(1, 0, 2), "rb3": v["L0_ffn_rb3"],
        "eW1": v["L0_ffn_eW1"].transpose(1, 0, 2),
        "eb1": v["L0_ffn_eb1"].reshape(E0, KH, P).transpose(2, 0, 1),
        "eW2": v["L0_ffn_eW2"].reshape(E0, KH, P, C).transpose(2, 0, 1, 3), "eb2": v["L0_ffn_eb2"].T,
        "w0": np.concatenate([qkv0[0].T, qkv0[0][swap].T, qkv0[1].T, qkv0[1][swap].T, v["L0_attn_w_gated"].T,
                              qkv0[2].T], 1),
        "w0p": v["L0_attn_w_proj"].T, "gnw": col(v["L0_attn_gn_weight"]), "gnb": col(v["L0_attn_gn_bias"]),
        "w5": np.concatenate([qkv1[0].T, qkv1[1].T, qkv1[2].T], 1), "w5p": v["L1_attn_w_proj"].T,
        "b5p": v["L1_attn_b_proj"],
        "w4": np.concatenate([v["L1_ffn_wq"], v["L1_ffn_wk"], v["L1_ffn_wv"]], 1), "w4p": v["L1_ffn_wo"],
        "wp": np.stack([v["L1_ffn_wp"].T, np.roll(v["L1_ffn_wp"], C // 2, 0).T], 1),
        "ln": np.stack([v["L1_ffn_ln1_g"], v["L1_ffn_ln1_b"], v["L1_ffn_ln2_g"], v["L1_ffn_ln2_b"]], 1),
        "selw": v["L1_ffn_sel_w"], "keys": v["L1_ffn_keys"].transpose(1, 0, 2),
        "values": v["L1_ffn_values"].transpose(1, 0, 2),
    }
    return out


def kernel(**inputs):
    import concourse.bacc as _bacc
    from concourse.bass_utils import run_bass_kernel_spmd as _run

    nc = _bacc.Bacc("TRN2", target_bir_lowering=False, num_devices=1)
    arrays, io = {}, {}
    for name, a in {**layouts(inputs), **shape_tables()}.items():
        arrays[f"in_{name}"] = np.ascontiguousarray(a)
        io[name] = nc.dram_tensor(f"in_{name}", a.shape, mybir.dt.from_np(a.dtype), kind="ExternalInput").ap()
    io["out"] = nc.dram_tensor("out", (B, T, C), F32, kind="ExternalOutput").ap()
    program(nc, io)
    return _run(nc, [arrays], core_ids=[0]).results[0]["out"]
```

```python
from contextlib import ExitStack

import numpy as np

import concourse.bass as bass
from concourse import mybir

F32 = mybir.dt.float32
BF16 = mybir.dt.bfloat16
U32 = mybir.dt.uint32
ALU = mybir.AluOpType
ACT = mybir.ActivationFunctionType
AX = mybir.AxisListType

P = 128
B, T, C = 16, 256, 128
TT = T // P
H, HD = 16, 8
QUAD = 4
E0, HID, CAP = 8, 512, 40
KH = HID // P
E1, TOPK = 32, 4
EPS = 1e-5
SLOTS = 6
ROWS = 96
QSLOT = (0, 0, 0, 1, 1, 2)
KSLOT = (0, 1, 2, 0, 1, 0)
RUNS = ((0, 3), (3, 2), (5, 1))


class Ring:

    def __init__(self, psum, filled, emptied, per, banks):
        self.psum, self.filled, self.emptied, self.per, self.banks = psum, filled, emptied, per, banks

    def nth(self, item, k):
        return item[0] * self.per + k + 1

    def bank(self, item, k):
        return self.psum[:, (item[1] * self.per + k) % self.banks, :]

    def done(self, item, k):
        return self.nth(item, k) + self.banks


class Pool_:

    def __init__(self, nc, ctx, tag):
        self.nc, self.ctx, self.tag, self.sems = nc, ctx, tag, []
        ctx.callback(self.clear)

    def clear(self):
        if self.sems:
            self.nc.clear_and_free_semaphores(self.sems)
            self.nc.all_engine_barrier()

    def sb(self, name, shape, dt=F32):
        return self.ctx.enter_context(self.nc.sbuf_tensor(f"{self.tag}_{name}", shape, dt))

    def ps(self, name, shape, dt=F32):
        return self.ctx.enter_context(self.nc.psum_tensor(f"{self.tag}_{name}", shape, dt))

    def sem(self, name):
        self.sems.append(self.nc.alloc_semaphore(f"{self.tag}_{name}"))
        return self.sems[-1]


def steps(eng, first, last, step, lead=1, trail=1):
    s = first
    while s < first + lead or (last - trail - s + 1) % 2:
        step((s, s % 2))
        s += 1
    pairs = (last - trail - s + 1) // 2
    base = s
    with eng.Fori(0, pairs) as p:
        for q in (0, 1):
            step((p * 2 + (base + q), (base + q) % 2), inner=True)
    for s in range(base + 2 * pairs, last + 1):
        step((s, s % 2))


def is_first(s, at=0):
    return isinstance(s, int) and s == at


def within(s, first, last):
    return not isinstance(s, int) or first <= s <= last


def before(item, n=1):
    return (item[0] - n, (item[1] + n) % 2)


def after(item):
    return (item[0] + 1, (item[1] + 1) % 2)


def routed_ffn(nc, tag, x_sb, k, w):
    G, GT, NB = B // 2, 4, 2
    S = E0 * CAP
    SW, NW = 2 * CAP, E0 // 2
    W = GT * P
    x_g = x_sb[:, :, :].rearrange("p (g t) c -> p g t c", t=GT)
    with ExitStack() as ctx:
        a = Pool_(nc, ctx, tag)
        xn = a.sb("xn", [P, 2, GT, C])
        stats = a.sb("stats", [P, GT, 6])
        mv = a.sb("mv", [P, GT, 2])
        veps = a.sb("veps", [P, GT])
        rstd = a.sb("rstd", [P, GT])
        xt = a.sb("xt", [P, W])
        h1 = a.sb("h1", [P, KH, W])
        h2 = a.sb("h2", [P, KH, W])
        lg = a.sb("lg", [P, GT, E0])
        top = a.sb("top", [P, GT])
        ex = a.sb("ex", [P, GT, E0])
        den = a.sb("den", [P, GT])
        sc = a.sb("sc", [P, GT, E0])
        best = a.sb("best", [P, GT, 8])
        best_at = a.sb("best_at", [P, GT, 8], U32)
        best_f = a.sb("best_f", [P, GT, 2])
        eq = a.sb("eq", [P, GT, 2, E0])
        mask = a.sb("mask", [P, GT, E0], BF16)
        off = a.sb("off", [P, GT, E0])
        pos = a.sb("pos", [P, GT, E0])
        d = a.sb("d", [P, 2, GT * E0, CAP])
        g = a.sb("g", [P, 2, GT * E0, CAP])
        xd = a.sb("xd", [P, E0, NB, CAP])
        hh = a.sb("hh", [P, E0, KH, NB * CAP])
        eot = a.sb("eot", [P, NB, E0, CAP])
        eos = a.sb("eos", [ROWS, NB, NW, C])
        gts = a.sb("gts", [ROWS, GT, NW, P])

        ra = Ring(a.ps("ra", [P, 2, 512]), a.sem("ra_filled"), a.sem("ra_emptied"), 5, 2)
        rv = Ring(a.ps("rv", [P, 2, 512]), a.sem("rv_filled"), a.sem("rv_emptied"), 6, 2)
        ea = Ring(a.ps("ea", [P, 2, 512]), a.sem("ea_filled"), a.sem("ea_emptied"), 9, 2)
        ev = Ring(a.ps("ev", [P, 2, 512]), a.sem("ev_filled"), a.sem("ev_emptied"), 10, 2)
        ln_stats, ln_aggr, ln_veps, ln_rstd, xn_ready = [a.sem(n) for n in (
            "ln_stats", "ln_aggr", "ln_veps", "ln_rstd", "xn_ready")]
        top_ready, lg_ready, ex_ready, den_step, sc_ready, best_step, bestf, mask_step, off_ready, d_ready, g_ready, padded = [
            a.sem(n) for n in ("top_ready", "lg_ready", "ex_ready", "den_step", "sc_ready", "best_step", "bestf",
                               "mask_step", "off_ready", "d_ready", "g_ready", "padded")]
        block = ctx.enter_context(nc.Block())

        @block.sync
        def _(sp):
            if w.load is not None:
                w.load(sp)

        ROUTE_H1 = ((ra, 1), (rv, 0), (ra, 2), (rv, 1))
        ROUTE_H2 = ((ra, 3), (rv, 2), (ra, 4), (rv, 3))

        @block.tensor
        def _(pe):
            def turn_x(it):
                pe.wait_ge(ra.emptied, ra.nth(it, 0))
                pe.wait_ge(xn_ready, it[0] * GT + GT)
                for t in range(GT):
                    mm = nc.tensor.transpose(ra.bank(it, 0)[:, t * P:(t + 1) * P], xn[:, it[1], t, :], k.ident)
                mm.then_inc(ra.filled, 1)

            def layer1(it, m):
                ring, n = ROUTE_H1[m]
                if m == 0:
                    pe.wait_ge(ra.emptied, ra.done(it, 0))
                    if is_first(it[0]):
                        pe.wait_ge(w.router_loaded, w.router_count)
                pe.wait_ge(ring.emptied, ring.nth(it, n))
                nc.tensor.matmul(ring.bank(it, n), w.rw1[:, m * P:(m + 1) * P], xt[:, :], start=True,
                                 stop=True).then_inc(ring.filled, 1)

            def layer2(it, m):
                ring, n = ROUTE_H2[m]
                if m == 0:
                    pe.wait_ge(ra.emptied, ra.done(it, 2))
                    pe.wait_ge(rv.emptied, rv.done(it, 1))
                pe.wait_ge(ring.emptied, ring.nth(it, n))
                for j in range(KH):
                    mm = nc.tensor.matmul(ring.bank(it, n), w.rw2[:, j, m * P:(m + 1) * P], h1[:, j, :],
                                          start=(j == 0), stop=(j == KH - 1))
                mm.then_inc(ring.filled, 1)

            def logits(it, t):
                if t == 0:
                    pe.wait_ge(rv.emptied, rv.nth(it, 4))
                    pe.wait_ge(ra.emptied, ra.done(it, 4))
                    pe.wait_ge(rv.emptied, rv.done(it, 3))
                for j in range(KH):
                    mm = nc.tensor.matmul(rv.bank(it, 4)[:, t * E0:(t + 1) * E0],
                                          h2[:, j, t * P:(t + 1) * P], w.rw3[:, j, :],
                                          start=(j == 0), stop=(j == KH - 1))
                if t == GT - 1:
                    mm.then_inc(rv.filled, 1)

            def count(it):
                pe.wait_ge(rv.emptied, rv.nth(it, 5))
                pe.wait_ge(mask_step, it[0] + 1)
                for t in range(GT):
                    out = rv.bank(it, 5)[:, t * E0:(t + 1) * E0]
                    if t % TT:
                        nc.tensor.matmul(out, k.ones_bf, mask[:, t - 1, :], start=True, stop=False)
                    mm = nc.tensor.matmul(out, k.tri_bf, mask[:, t, :], start=(t % TT == 0), stop=True)
                mm.then_inc(rv.filled, 1)

            def slots(it):
                pe.wait_ge(d_ready, it[0] + 1)
                for b, ring in enumerate((ea, ev)):
                    pe.wait_ge(ring.emptied, ring.nth(it, 0))
                    for t in range(TT):
                        u = b * TT + t
                        mm = nc.tensor.matmul(ring.bank(it, 0)[:, 0:S], xn[:, it[1], u, :],
                                              d[:, it[1], u * E0:(u + 1) * E0, :],
                                              start=(t == 0), stop=(t == TT - 1))
                    mm.then_inc(ring.filled, 1)

            def hidden(it, e):
                ring, n = (ea, ev)[e % 2], 1 + e // 2
                if e == 0:
                    pe.wait_ge(ea.emptied, ea.done(it, 0))
                    pe.wait_ge(ev.emptied, ev.done(it, 0))
                pe.wait_ge(ring.emptied, ring.nth(it, n))
                for j in range(KH):
                    mm = nc.tensor.matmul(ring.bank(it, n)[:, j * SW:(j + 1) * SW],
                                          w.ew1[:, e, j * P:(j + 1) * P], xd[:, e, :, :],
                                          start=True, stop=True)
                mm.then_inc(ring.filled, 1)

            def output(it, e):
                ring = (ea, ev)[e // 4]
                if e % 4 == 0:
                    pe.wait_ge(ring.emptied, ring.nth(it, 5))
                source, n = (ea, ev)[e % 2], 1 + e // 2
                pe.wait_ge(source.emptied, source.done(it, n))
                for j in range(KH):
                    mm = nc.tensor.matmul(ring.bank(it, 5)[:, (e % 4) * P:(e % 4) * P + SW],
                                          w.ew2[:, e, j, :], hh[:, e, j, :],
                                          start=(j == 0), stop=(j == KH - 1))
                if e % 4 == 3:
                    mm.then_inc(ring.filled, 1)

            def turn_slots(it):
                pe.wait_ge(ea.emptied, ea.done(it, 5))
                pe.wait_ge(ev.emptied, ev.done(it, 5))
                for b, ring in enumerate((ea, ev)):
                    pe.wait_ge(ring.emptied, ring.nth(it, 6))
                    for v in range(NW):
                        mm = nc.tensor.transpose(ring.bank(it, 6)[0:SW, v * P:(v + 1) * P],
                                                 eot[:, b, 2 * v:2 * v + 2, :], k.ident)
                    mm.then_inc(ring.filled, 1)

            def turn_weights(it):
                pe.wait_ge(g_ready, it[0] + 1)
                for t in range(GT):
                    ring, n = (ea, ev)[t % 2], 7 + t // 2
                    pe.wait_ge(ring.emptied, ring.nth(it, n))
                    for v in range(NW):
                        mm = nc.tensor.transpose(ring.bank(it, n)[0:SW, v * P:(v + 1) * P],
                                                 g[:, it[1], t * E0 + 2 * v:t * E0 + 2 * v + 2, :], k.ident)
                    mm.then_inc(ring.filled, 1)

            def back(it):
                pe.wait_ge(ev.emptied, ev.nth(it, 9))
                pe.wait_ge(ea.emptied, ea.done(it, 8))
                pe.wait_ge(ev.emptied, ev.done(it, 8))
                for t in range(GT):
                    for v in range(NW):
                        mm = nc.tensor.matmul(ev.bank(it, 9)[:, t * P:(t + 1) * P], gts[:, t, v, :],
                                              eos[:, t // TT, v, :], start=(v == 0), stop=(v == NW - 1))
                mm.then_inc(ev.filled, 1)

            def step(it, inner=False):
                r = it if within(it[0], 0, G - 1) else None
                e = before(it) if within(it[0], 1, G) else None
                if r:
                    turn_x(r)
                if e:
                    count(e)
                if r:
                    for m in range(3):
                        layer1(r, m)
                if e:
                    slots(e)
                if r:
                    layer1(r, 3)
                for m in range(KH):
                    for n in ((0, 1, 2, 3), (4, 5), (6, 7), ())[m]:
                        if e:
                            hidden(e, n)
                    if m == 3 and e:
                        output(e, 0)
                        output(e, 1)
                    if r:
                        layer2(r, m)
                if e:
                    output(e, 2)
                    output(e, 3)
                for t in range(GT):
                    if e:
                        output(e, 4 + t)
                    if r:
                        logits(r, t)
                if e:
                    turn_slots(e)
                    turn_weights(e)
                    back(e)
                if is_first(it[0]):
                    pe.wait_ge(w.experts_loaded, w.experts_count)

            pe.wait_ge(k.loaded, k.loaded_count)
            steps(pe, 0, G, step, lead=1, trail=2)

        @block.scalar
        def _(act):
            act.sem_inc(ra.emptied, ra.banks)
            act.sem_inc(ea.emptied, ea.banks)

            def route_hidden(it, n):
                out, bias = ((h1, w.rb1), (h2, w.rb2))[n // 2]
                m = 2 * (n % 2)
                act.wait_ge(ra.filled, ra.nth(it, 1 + n))
                nc.scalar.activation(out[:, m, :], ra.bank(it, 1 + n), ACT.Relu,
                                     bias=bias[:, m:m + 1]).then_inc(ra.emptied, 1)

            def hidden(it, e):
                act.wait_ge(ea.filled, ea.nth(it, 1 + e // 2))
                for j in range(KH):
                    last = nc.scalar.activation(hh[:, e, j, :], ea.bank(it, 1 + e // 2)[:, j * SW:(j + 1) * SW],
                                                ACT.Relu, bias=w.eb1[:, e, j:j + 1])
                last.then_inc(ea.emptied, 1)

            def step(it, inner=False):
                r = it if within(it[0], 0, G - 1) else None
                e = before(it) if within(it[0], 1, G) else None
                if r:
                    act.wait_ge(ra.filled, ra.nth(r, 0))
                    nc.scalar.activation(xt[:, :], ra.bank(r, 0), ACT.Copy).then_inc(ra.emptied, 1)
                    if is_first(r[0]):
                        act.wait_ge(w.router_loaded, w.router_count)
                    route_hidden(r, 0)
                    route_hidden(r, 1)
                if e:
                    act.wait_ge(ea.filled, ea.nth(e, 0))
                    nc.scalar.activation(xd[:, :, 0, :], ea.bank(e, 0)[:, 0:S].rearrange("p (e s) -> p e s", e=E0),
                                         ACT.Copy).then_inc(ea.emptied, 1)
                    hidden(e, 0)
                    hidden(e, 2)
                if r:
                    route_hidden(r, 2)
                if e:
                    hidden(e, 4)
                    hidden(e, 6)
                if r:
                    route_hidden(r, 3)
                if e:
                    act.wait_ge(ea.filled, ea.nth(e, 5))
                    for n in range(4):
                        last = nc.scalar.activation(eot[:, :, n, :], ea.bank(e, 5)[:, n * P:n * P + SW]
                                                    .rearrange("p (b s) -> p b s", b=NB), ACT.Identity,
                                                    bias=w.eb2[:, n:n + 1])
                    last.then_inc(ea.emptied, 1)
                if r and e:
                    softmax_exp(r)
                if e:
                    act.wait_ge(ea.filled, ea.nth(e, 6))
                    nc.scalar.activation(eos[0:SW, 0, :, :].rearrange("p v c -> p (v c)"), ea.bank(e, 6)[0:SW, :],
                                         ACT.Copy).then_inc(ea.emptied, 1)
                    for t in (0, 2):
                        act.wait_ge(ea.filled, ea.nth(e, 7 + t // 2))
                        nc.scalar.activation(gts[0:SW, t, :, :].rearrange("p v c -> p (v c)"),
                                             ea.bank(e, 7 + t // 2)[0:SW, :], ACT.Copy).then_inc(ea.emptied, 1)
                if r and not e:
                    softmax_exp(r)
                if is_first(it[0]):
                    act.wait_ge(padded, 2)
                    act.wait_ge(w.experts_loaded, w.experts_count)

            def softmax_exp(it):
                act.wait_ge(lg_ready, it[0] + 1)
                nc.scalar.activation(ex[:, :, :], lg[:, :, :], ACT.Exp).then_inc(ex_ready, 1)

            steps(act, 0, G, step, lead=1, trail=2)

        @block.vector
        def _(dve):
            nc.vector.memset(eos[64:ROWS, :, :, :].rearrange("p b v c -> p (b v c)"), 0.0).then_inc(padded, 1)
            nc.vector.memset(gts[64:ROWS, :, :, :].rearrange("p t v c -> p (t v c)"), 0.0).then_inc(padded, 1)
            dve.sem_inc(rv.emptied, rv.banks)
            dve.sem_inc(ev.emptied, ev.banks)

            def ln_measure(it):
                i = it[0]
                for t in range(GT):
                    nc.vector.bn_stats(stats[:, t, :], x_g[:, i, t, :]).then_inc(ln_stats, 1)
                dve.wait_ge(ln_stats, i * GT + GT)
                nc.vector.memset(k.idle, 0.0)
                for t in range(GT):
                    last = nc.vector.bn_aggr(mv[:, t, :], stats[:, t, :])
                last.then_inc(ln_aggr, 1)

            def ln_apply(it):
                i = it[0]
                dve.wait_ge(ln_rstd, i + 1)
                for t in range(GT):
                    nc.vector.tensor_scalar(xn[:, it[1], t, :], x_g[:, i, t, :], mv[:, t, 0:1], rstd[:, t:t + 1],
                                            ALU.subtract, ALU.mult).then_inc(xn_ready, 1)

            def route_hidden(it, n):
                out, bias = ((h1, w.rb1), (h2, w.rb2))[n // 2]
                m = 1 + 2 * (n % 2)
                dve.wait_ge(rv.filled, rv.nth(it, n))
                nc.vector.tensor_scalar(out[:, m, :], rv.bank(it, n), bias[:, m:m + 1], 0.0,
                                        ALU.add, ALU.max).then_inc(rv.emptied, 1)

            def softmax_shift(it):
                i = it[0]
                dve.wait_ge(rv.filled, rv.nth(it, 4))
                nc.vector.tensor_tensor(lg[:, :, :], rv.bank(it, 4)[:, 0:GT * E0].rearrange("p (t e) -> p t e", t=GT),
                                        w.rb3[:, :].unsqueeze(1).to_broadcast([P, GT, E0]),
                                        ALU.add).then_inc(rv.emptied, 1)
                dve.wait_ge(rv.emptied, rv.done(it, 4))
                nc.vector.tensor_reduce(top[:, :], lg[:, :, :], AX.X, ALU.max).then_inc(top_ready, 1)
                dve.wait_ge(top_ready, i + 1)
                nc.vector.tensor_tensor(lg[:, :, :], lg[:, :, :], top[:, :].unsqueeze(2).to_broadcast([P, GT, E0]),
                                        ALU.subtract).then_inc(lg_ready, 1)

            def softmax_divide(it):
                i = it[0]
                dve.wait_ge(ex_ready, i + 1)
                nc.vector.tensor_reduce(den[:, :], ex[:, :, :], AX.X, ALU.add).then_inc(den_step, 1)
                dve.wait_ge(den_step, i * 2 + 1)
                nc.vector.reciprocal(den[:, :], den[:, :]).then_inc(den_step, 1)
                if not is_first(i):
                    dve.wait_ge(g_ready, i)
                dve.wait_ge(den_step, i * 2 + 2)
                nc.vector.tensor_tensor(sc[:, :, :], ex[:, :, :], den[:, :].unsqueeze(2).to_broadcast([P, GT, E0]),
                                        ALU.mult).then_inc(sc_ready, 1)

            def pick(it):
                i = it[0]
                dve.wait_ge(sc_ready, i + 1)
                nc.vector.memset(k.idle, 0.0)
                for t in range(GT):
                    last = nc.vector.max(best[:, t, :], sc[:, t, :])
                last.then_inc(best_step, 1)
                dve.wait_ge(best_step, i * 2 + 1)
                nc.vector.memset(k.idle, 0.0)
                for t in range(GT):
                    last = nc.vector.max_index(best_at[:, t, :], best[:, t, :], sc[:, t, :])
                last.then_inc(best_step, 1)
                dve.wait_ge(best_step, i * 2 + 2)
                nc.vector.tensor_copy(best_f[:, :, :], best_at[:, :, 0:2]).then_inc(bestf, 1)

            def mark(it):
                i = it[0]
                dve.wait_ge(bestf, i * 2 + 1)
                for n in range(2):
                    last = nc.vector.tensor_tensor(eq[:, :, n, :], k.iota8.unsqueeze(1).to_broadcast([P, GT, E0]),
                                                   best_f[:, :, n:n + 1].to_broadcast([P, GT, E0]), ALU.is_equal)
                last.then_inc(bestf, 1)
                dve.wait_ge(bestf, i * 2 + 2)
                nc.vector.tensor_tensor(mask[:, :, :], eq[:, :, 0, :], eq[:, :, 1, :], ALU.add).then_inc(mask_step, 1)
                dve.wait_ge(mask_step, i + 1)
                nc.vector.tensor_scalar(off[:, :, :], mask[:, :, :], -1000.0, 1000.0, ALU.mult, ALU.add)\
                    .then_inc(off_ready, 1)

            def place(it):
                i = it[0]
                dve.wait_ge(off_ready, i + 1)
                dve.wait_ge(rv.filled, rv.nth(it, 5))
                nc.vector.tensor_tensor(pos[:, :, :], rv.bank(it, 5)[:, 0:GT * E0].rearrange("p (t e) -> p t e", t=GT),
                                        off[:, :, :], ALU.add).then_inc(rv.emptied, 1)
                dve.wait_ge(rv.emptied, rv.done(it, 5))
                nc.vector.tensor_tensor(d[:, it[1], :, :], k.iota40.unsqueeze(1).to_broadcast([P, GT * E0, CAP]),
                                        pos[:, :, :].rearrange("p t e -> p (t e)").unsqueeze(2)
                                        .to_broadcast([P, GT * E0, CAP]), ALU.is_equal).then_inc(d_ready, 1)

            def hidden(it, e):
                dve.wait_ge(ev.filled, ev.nth(it, 1 + e // 2))
                for j in range(KH):
                    last = nc.vector.tensor_scalar(hh[:, e, j, :], ev.bank(it, 1 + e // 2)[:, j * SW:(j + 1) * SW],
                                                   w.eb1[:, e, j:j + 1], 0.0, ALU.add, ALU.max)
                last.then_inc(ev.emptied, 1)

            def slots(it):
                dve.wait_ge(ev.filled, ev.nth(it, 0))
                nc.vector.tensor_copy(xd[:, :, 1, :], ev.bank(it, 0)[:, 0:S].rearrange("p (e s) -> p e s", e=E0))\
                    .then_inc(ev.emptied, 1)

            def experts_last(it):
                dve.wait_ge(ev.filled, ev.nth(it, 5))
                for e in range(4, E0):
                    last = nc.vector.tensor_scalar(eot[:, :, e, :], ev.bank(it, 5)[:, (e - 4) * P:(e - 4) * P + SW]
                                                   .rearrange("p (b s) -> p b s", b=NB), w.eb2[:, e:e + 1], None,
                                                   ALU.add)
                last.then_inc(ev.emptied, 1)

            def turned(it, n):
                dve.wait_ge(ev.filled, ev.nth(it, 6 + n))
                out = (eos[0:SW, 1], gts[0:SW, 1], gts[0:SW, 3])[n]
                nc.vector.tensor_copy(out.rearrange("p v c -> p (v c)"), ev.bank(it, 6 + n)[0:SW, :])\
                    .then_inc(ev.emptied, 1)

            def residual(it):
                dve.wait_ge(ev.filled, ev.nth(it, 9))
                xs = x_g[:, it[0], :, :].rearrange("p t c -> p (t c)")
                nc.vector.scalar_tensor_tensor(xs, ev.bank(it, 9), 0.5, xs, ALU.mult, ALU.add)\
                    .then_inc(ev.emptied, 1)

            def step(it, inner=False):
                r = it if within(it[0], 0, G - 1) else None
                e = before(it) if within(it[0], 1, G) else None
                following = after(it) if within(it[0], 0, G - 2) else None
                if is_first(it[0]):
                    ln_measure(it)
                    ln_apply(it)
                    dve.wait_ge(w.router_loaded, w.router_count)
                if e:
                    place(e)
                if r:
                    route_hidden(r, 0)
                if e:
                    slots(e)
                if r:
                    route_hidden(r, 1)
                if e:
                    hidden(e, 1)
                    hidden(e, 3)
                if following:
                    ln_measure(following)
                if e:
                    hidden(e, 5)
                if r:
                    route_hidden(r, 2)
                if e:
                    hidden(e, 7)
                if following:
                    ln_apply(following)
                if r:
                    route_hidden(r, 3)
                if e:
                    experts_last(e)
                if r:
                    softmax_shift(r)
                if e:
                    turned(e, 0)
                if r:
                    softmax_divide(r)
                if e:
                    turned(e, 1)
                if r:
                    pick(r)
                if e:
                    turned(e, 2)
                if r:
                    mark(r)
                if e:
                    residual(e)
                if is_first(it[0]):
                    dve.wait_ge(w.experts_loaded, w.experts_count)

            dve.wait_ge(k.loaded, k.loaded_count)
            steps(dve, 0, G, step, lead=1, trail=2)

        @block.gpsimd
        def _(pool):
            def ln_root(it):
                pool.wait_ge(ln_aggr, it[0] + 1)
                nc.gpsimd.tensor_tensor(veps[:, :], mv[:, :, 1], k.eps[:, 0:GT], ALU.add).then_inc(ln_veps, 1)
                pool.wait_ge(ln_veps, it[0] + 1)
                nc.gpsimd.tensor_tensor(rstd[:, :], veps[:, :], k.minus_half[:, 0:GT], ALU.pow).then_inc(ln_rstd, 1)

            def weigh(it):
                pool.wait_ge(d_ready, it[0] + 1)
                nc.gpsimd.tensor_tensor(g[:, it[1], :, :], d[:, it[1], :, :],
                                        sc[:, :, :].rearrange("p t e -> p (t e)").unsqueeze(2)
                                        .to_broadcast([P, GT * E0, CAP]), ALU.mult).then_inc(g_ready, 1)

            def step(it, inner=False):
                s = it[0]
                if is_first(s):
                    ln_root(it)
                if within(s, 1, G):
                    weigh(before(it))
                if within(s, 0, G - 2):
                    ln_root(after(it))

            pool.wait_ge(k.loaded, k.loaded_count)
            steps(pool, 0, G, step, lead=1, trail=2)


class Desk:

    def __init__(self, psum, filled, emptied, fills, banks):
        self.psum, self.filled, self.emptied, self.banks = psum, filled, emptied, banks
        self.fills = fills

    def _place(self, it, name):
        s, par = it
        present = [n for n, first in self.fills if within(s, first, first + B - 1)]
        if isinstance(s, int):
            n = sum(1 for u in range(s) for _, first in self.fills if within(u, first, first + B - 1))
            return n + present.index(name), n + present.index(name)
        all_, late = len(self.fills), sum(first for _, first in self.fills)
        at = present.index(name)
        return s * all_ - late + at, (par + 4) * all_ - late + at

    def nth(self, it, name):
        return self._place(it, name)[0] + 1

    def bank(self, it, name):
        return self.psum[:, self._place(it, name)[1] % self.banks, :]

    def done(self, it, name):
        return self.nth(it, name) + self.banks


class Pipeline:
    LAST = B + 2

    @staticmethod
    def start(it):
        return it if within(it[0], 0, B - 1) else None

    @staticmethod
    def prepare(it):
        return before(it) if within(it[0], 1, B) else None

    @staticmethod
    def attend(it):
        return before(it, 2) if within(it[0], 2, B + 1) else None

    @staticmethod
    def finish(it):
        return before(it, 3) if within(it[0], 3, B + 2) else None

    @staticmethod
    def run(eng, step):
        steps(eng, 0, Pipeline.LAST, step, lead=3, trail=3)


def heads_of(v):
    def at(vm, par, t):
        whole = vm[:, par, t, :, :]
        return bass.AP(whole.tensor, whole.offset, [list(whole.ap[0]), [C + HD, QUAD], [QUAD * HD, H // QUAD], [1, HD]])
    return at(*v)


STACKED = 16 * 2 * len(RUNS)


def slots_of(part, run, each, n):
    return bass.AP(part.tensor, part.offset, [[each, run], [H * n, HD], [1, H * n]])


def pad_rows(eng, tile, padded):
    for rows in (slice(32, 64), slice(64, ROWS)):
        eng.memset(tile[rows, :, :, :].rearrange("p a h t -> p (a h t)"), 0.0).then_inc(padded, 1)


def stack_parts(sp, parts, scratch, qs, ks, parts_ready, bounced, stacked, passed, sr, padded):
    def step(it, inner=False):
        i, par = it
        if not is_first(i):
            sp.wait_ge(stacked, i * STACKED)
            sp.sem_inc(passed, 1)
        sp.wait_ge(parts_ready, i + 1)
        sp.dma_start(scratch[par].rearrange("n c t -> c n t"), parts[:, par, :, :, :].rearrange("c n u t -> c (n u) t"))\
            .then_inc(bounced, 16)
        if not is_first(i) and not is_first(i, 1):
            sp.wait_ge(sr.filled, (i - 1) * H)
            sp.sem_inc(passed, 1)
        sp.wait_ge(bounced, i * 16 + 16)
        for first, run in RUNS:
            for dst, which, part, each in ((qs, 0, QSLOT[first], 0), (ks, 1, 0, 2 * P * T)):
                slots = slots_of(scratch[par, 2 * part + which], run, each, T)
                sp.dma_start(dst[first * HD:(first + run) * HD, par, :, :].rearrange("s h t -> s (h t)"), slots)\
                    .then_inc(stacked, 16)

    sp.wait_ge(padded, 4)
    steps(sp, 0, B - 1, step, lead=2, trail=2)
    sp.wait_ge(stacked, B * STACKED)


def retention(nc, tag, x_sb, k, io):
    x_b = x_sb[:, :, :].rearrange("p (b t) c -> p b t c", t=TT)
    AB = 4
    LAG = 2
    with ExitStack() as ctx:
        a = Pool_(nc, ctx, tag)
        w0, wp = a.sb("w0", [P, 6, C]), a.sb("wp", [P, C])
        rope, decay, group = a.sb("rope", [P, 4, T]), a.sb("decay", [P, H, T + P]), a.sb("group", [P, P])
        gnw, gnb = a.sb("gnw", [P, 1]), a.sb("gnb", [P, 1])
        stats, mv = a.sb("stats", [P, TT, 6]), a.sb("mv", [P, TT, 2])
        veps, rstd = a.sb("veps", [P, TT]), a.sb("rstd", [P, TT])
        xn = a.sb("xn", [P, TT, C])
        xt = a.sb("xt", [P, T])
        qp, kp = a.sb("qp", [P, 2, T]), a.sb("kp", [P, 2, T])
        qk, rest = a.sb("qk", [P, 2, T]), a.sb("rest", [P, 2, T])
        parts = a.sb("parts", [P, 2, 3, 2, T], BF16)
        qs, ks = a.sb("qs", [ROWS, 2, H, T], BF16), a.sb("ks", [ROWS, 2, H, T], BF16)
        scratch = nc.dram_tensor(f"{tag}_scratch", (2, 6, P, T), BF16, kind="Internal").ap()
        vm = a.sb("vm", [P, 2, TT, QUAD, C])
        one = a.sb("one", [P, 1])
        gate, eg = a.sb("gate", [P, T]), a.sb("eg", [P, T])
        silu = a.sb("silu", [P, 2, T])
        att = a.sb("att", [P, AB, T + P])
        ystats, ymv = a.sb("ystats", [P, 6]), a.sb("ymv", [P, 2])
        mean, dmean, qv, var = [a.sb(n, [P, 1]) for n in ("mean", "dmean", "qv", "var")]
        veps_y, rstd_y, ga, nb = [a.sb(n, [P, 1]) for n in ("veps_y", "rstd_y", "ga", "nb")]
        yn = a.sb("yn", [P, T])
        gated = a.sb("gated", [P, T])
        ob = a.sb("ob", [P, TT, C])

        y_ps = a.ps("y", [P, 2, 512])
        desk = Desk(a.ps("desk", [P, 2, 512]), a.sem("desk_filled"), a.sem("desk_emptied"),
                    [("gm", 3), ("v", 1), ("gv", 3), ("g", 1), ("o", 3), ("xt", 0), ("q", 0), ("k", 0)], 2)
        sr = Ring(a.ps("sr", [P, AB, 512]), a.sem("sr_filled"), a.sem("sr_emptied"), H, AB)
        (loaded, vm_zero, ln_stats, ln_aggr, ln_veps, ln_rstd, xn_ready, qp_turned, kp_turned, qk_ready, part1, rest1,
         part2, parts_ready, bounced, stacked, eg1, eg2, one_ready, silu_ready, av_done, y_stats, y_aggr, dm_ready, qv_ready,
         y_veps, y_rstd, ga_ready, nb_ready, yn_ready, gated_ready, x_done, passed, padded) = [a.sem(n) for n in (
             "loaded", "vm_zero", "ln_stats", "ln_aggr", "ln_veps", "ln_rstd", "xn_ready", "qp_turned", "kp_turned",
             "qk_ready", "part1", "rest1", "part2", "parts_ready", "bounced", "stacked", "eg1", "eg2", "one_ready", "silu_ready",
             "av_done", "y_stats", "y_aggr", "dm_ready", "qv_ready", "y_veps", "y_rstd", "ga_ready", "nb_ready",
             "yn_ready", "gated_ready", "x_done", "passed", "padded")]
        LOADS = 16 * 7
        block = ctx.enter_context(nc.Block())

        @block.sync
        def _(sp):
            for dst, src in ((w0[:, :, :], io["w0"].rearrange("p (n c) -> p n c", c=C)), (rope[:, :, :], io["rope"]),
                             (decay[:, :, :], io["decay"]), (group[:, :], io["group"]), (gnw[:, :], io["gnw"]),
                             (gnb[:, :], io["gnb"]), (wp[:, :], io["w0p"])):
                sp.dma_start(dst, src).then_inc(loaded, 16)

            stack_parts(sp, parts, scratch, qs, ks, parts_ready, bounced, stacked, passed, sr, padded)

        @block.tensor
        def _(pe):
            def fill(it, name):
                pe.wait_ge(desk.emptied, desk.nth(it, name))
                return desk.bank(it, name)

            def attend_scores(it, n):
                h = (n % QUAD) * QUAD + n // QUAD
                pe.wait_ge(sr.emptied, sr.nth(it, n))
                out = sr.bank(it, n)
                nc.tensor.matmul(out[:, 0:T], ks[:, it[1], h, 0:P], qs[:, it[1], h, :], start=True, stop=True)
                nc.tensor.matmul(out[:, T:T + P], ks[:, it[1], h, P:T], qs[:, it[1], h, P:T], start=True,
                                 stop=True).then_inc(sr.filled, 1)

            def attend_values(it, n):
                r, j = n // QUAD, n % QUAD
                q = slice(j * QUAD * HD, (j + 1) * QUAD * HD)
                pe.wait_ge(sr.emptied, sr.done(it, n))
                nc.tensor.matmul(y_ps[q, it[1], 0:T], vm[:, it[1], 0, r, q], att[:, n % AB, 0:T],
                                 start=(r == 0), stop=False, skip_group_check=True)
                nc.tensor.matmul(y_ps[q, it[1], P:T], vm[:, it[1], 1, r, q], att[:, n % AB, T:T + P],
                                 start=False, stop=(r == QUAD - 1), skip_group_check=True).then_inc(av_done, 1)

            def small(it, n):
                new, prep, end = Pipeline.start(it), Pipeline.prepare(it), Pipeline.finish(it)
                if n == 1 and end:
                    pe.wait_ge(y_aggr, end[0] + 1)
                    nc.tensor.matmul(fill(it, "gm")[:, 0:1], group[:, :], ymv[:, 0:1], start=True, stop=True)\
                        .then_inc(desk.filled, 1)
                if n == 2 and prep:
                    out = fill(it, "v")
                    for t in range(TT):
                        mm = nc.tensor.matmul(out[:, t * P:(t + 1) * P], xt[:, t * P:(t + 1) * P], w0[:, 5, :],
                                              start=True, stop=True)
                    mm.then_inc(desk.filled, 1)
                if n == 4 and end:
                    pe.wait_ge(qv_ready, end[0] + 1)
                    nc.tensor.matmul(fill(it, "gv")[:, 0:1], group[:, :], qv[:, :], start=True, stop=True)\
                        .then_inc(desk.filled, 1)
                if n == 6 and prep:
                    nc.tensor.matmul(fill(it, "g")[:, 0:T], w0[:, 4, :], xt[:, :], start=True, stop=True)\
                        .then_inc(desk.filled, 1)
                if n == 9 and end:
                    out = fill(it, "o")
                    pe.wait_ge(gated_ready, end[0] + 1)
                    for t in range(TT):
                        mm = nc.tensor.matmul(out[:, t * P:(t + 1) * P], gated[:, t * P:(t + 1) * P], wp[:, :],
                                              start=True, stop=True)
                    mm.then_inc(desk.filled, 1)
                if n == 11 and new:
                    pe.wait_ge(xn_ready, new[0] * TT + TT)
                    out = fill(it, "xt")
                    for t in range(TT):
                        mm = nc.tensor.transpose(out[:, t * P:(t + 1) * P], xn[:, t, :], k.ident)
                    mm.then_inc(desk.filled, 1)
                if n in (13, 14) and new:
                    pe.wait_ge(desk.emptied, desk.done(it, "xt"))
                    out = fill(it, "qk"[n - 13])
                    for u in range(2):
                        mm = nc.tensor.matmul(out[:, u * T:(u + 1) * T], w0[:, 2 * (n - 13) + u, :], xt[:, :],
                                              start=True, stop=True)
                    mm.then_inc(desk.filled, 1)

            def step(it, inner=False):
                b = Pipeline.attend(it)
                if b:
                    pe.wait_ge(stacked, b[0] * STACKED + STACKED)
                    if not is_first(b[0]) and not is_first(b[0], 1):
                        pe.wait_ge(yn_ready, b[0] - 1)
                for n in range(H):
                    small(it, n)
                    if b:
                        attend_scores(b, n)
                        if n >= LAG:
                            attend_values(b, n - LAG)
                if b:
                    for n in range(H - LAG, H):
                        attend_values(b, n)

            pe.wait_ge(k.loaded, k.loaded_count)
            pe.wait_ge(loaded, LOADS)
            pe.wait_ge(vm_zero, 1)
            Pipeline.run(pe, step)

        @block.scalar
        def _(act):
            act.sem_inc(desk.emptied, 2)

            def taken(it, name):
                act.wait_ge(desk.filled, desk.nth(it, name))
                return desk.bank(it, name)

            def step(it, inner=False):
                new, prep, end = Pipeline.start(it), Pipeline.prepare(it), Pipeline.finish(it)
                if end:
                    bank = taken(it, "gm")
                    nc.scalar.activation(mean[:, :], bank[:, 0:1], ACT.Copy).then_inc(desk.emptied, 1)
                if prep:
                    bank = taken(it, "v")
                    for t in range(TT):
                        last = nc.scalar.activation(
                            heads_of((vm, prep[1], t)),
                            bank[:, t * P:(t + 1) * P].rearrange("p (j r d) -> p r j d", r=QUAD, d=HD), ACT.Copy)
                    last.then_inc(desk.emptied, 1)
                if end:
                    bank = taken(it, "gv")
                    nc.scalar.activation(var[:, :], bank[:, 0:1], ACT.Copy).then_inc(desk.emptied, 1)
                if prep:
                    bank = taken(it, "g")
                    if not is_first(prep[0]):
                        act.wait_ge(silu_ready, prep[0])
                    nc.scalar.activation(gate[:, :], bank[:, 0:T], ACT.Copy)
                    nc.scalar.activation(eg[:, :], bank[:, 0:T], ACT.Exp, scale=-1.0).then_inc(desk.emptied, 1)
                if end:
                    bank = taken(it, "o")
                    if not is_first(end[0]):
                        act.wait_ge(x_done, end[0])
                    nc.scalar.activation(ob[:, :, :].rearrange("p t c -> p (t c)"), bank[:, 0:T], ACT.Copy)\
                        .then_inc(desk.emptied, 1)
                if new:
                    bank = taken(it, "xt")
                    nc.scalar.activation(xt[:, :], bank[:, 0:T], ACT.Copy).then_inc(desk.emptied, 1)
                    for name, dst in (("q", qp), ("k", kp)):
                        bank = taken(it, name)
                        if not is_first(new[0]):
                            act.wait_ge(qk_ready, new[0] * 2)
                        nc.scalar.activation(dst[:, :, :].rearrange("p u t -> p (u t)"), bank, ACT.Copy)\
                            .then_inc(desk.emptied, 1)

            act.wait_ge(vm_zero, 1)
            Pipeline.run(act, step)

        @block.vector
        def _(dve):
            dve.sem_inc(sr.emptied, AB)
            nc.vector.memset(one[:, :], 1.0).then_inc(one_ready, 1)
            nc.vector.memset(vm[:, :, :, :, :].rearrange("p a b c d -> p (a b c d)"), 0.0).then_inc(vm_zero, 1)
            pad_rows(nc.vector, qs, padded)

            def turn(it, new, name):
                src, turned, u = (qp, qp_turned, 0) if name == "q" else (kp, kp_turned, 2)
                dve.wait_ge(desk.emptied, desk.done(it, name))
                nc.vector.tensor_tensor(src[:, :, :], src[:, :, :], rope[:, u:u + 2, :], ALU.mult).then_inc(turned, 1)

            def small(it, n):
                new, prep, end = Pipeline.start(it), Pipeline.prepare(it), Pipeline.finish(it)
                if end:
                    b, par = end
                    if n == 0:
                        nc.vector.bn_stats(ystats[:, :], y_ps[:, par, 0:T]).then_inc(y_stats, 1)
                        dve.wait_ge(y_stats, b + 1)
                        nc.vector.memset(k.idle, 0.0)
                        nc.vector.bn_aggr(ymv[:, :], ystats[:, :]).then_inc(y_aggr, 1)
                    if n == 2:
                        dve.wait_ge(desk.emptied, desk.done(it, "gm"))
                        nc.vector.tensor_tensor(dmean[:, :], ymv[:, 0:1], mean[:, :], ALU.subtract).then_inc(dm_ready, 1)
                        dve.wait_ge(dm_ready, b + 1)
                        nc.vector.scalar_tensor_tensor(qv[:, :], dmean[:, :], dmean[:, 0:1], ymv[:, 1:2], ALU.mult,
                                                       ALU.add).then_inc(qv_ready, 1)
                    if n == 7:
                        dve.wait_ge(y_rstd, b + 1)
                        nc.vector.tensor_tensor(ga[:, :], rstd_y[:, :], gnw[:, :], ALU.mult).then_inc(ga_ready, 1)
                        dve.wait_ge(ga_ready, b + 1)
                        nc.vector.scalar_tensor_tensor(nb[:, :], mean[:, :], ga[:, 0:1], gnb[:, :], ALU.mult,
                                                       ALU.subtract).then_inc(nb_ready, 1)
                        dve.wait_ge(nb_ready, b + 1)
                        nc.vector.tensor_scalar(yn[:, :], y_ps[:, par, 0:T], ga[:, 0:1], nb[:, 0:1], ALU.mult,
                                                ALU.subtract).then_inc(yn_ready, 1)
                        dve.wait_ge(yn_ready, b + 1)
                        dve.wait_ge(silu_ready, b + 1)
                        nc.vector.tensor_tensor(gated[:, :], yn[:, :], silu[:, par, :], ALU.mult)\
                            .then_inc(gated_ready, 1)
                if prep:
                    b, par = prep
                    if n == 1:
                        if not is_first(b) and not is_first(b, 1):
                            dve.wait_ge(bounced, b * 16 - 16)
                        dve.wait_ge(qk_ready, b * 2 + 2)
                        nc.vector.tensor_copy(parts[:, par, 0, :, :], qk[:, :, :]).then_inc(part1, 1)
                    if n == 3:
                        dve.wait_ge(rest1, b + 1)
                        nc.vector.tensor_copy(parts[:, par, 1, :, :], rest[:, :, :]).then_inc(part2, 1)
                    if n == 10:
                        dve.wait_ge(eg1, b + 1)
                        nc.vector.reciprocal(eg[:, :], eg[:, :]).then_inc(eg2, 1)
                if new:
                    b = new[0]
                    if n == 5:
                        for t in range(TT):
                            nc.vector.bn_stats(stats[:, t, :], x_b[:, b, t, :]).then_inc(ln_stats, 1)
                        dve.wait_ge(ln_stats, b * TT + TT)
                        nc.vector.memset(k.idle, 0.0)
                        for t in range(TT):
                            last = nc.vector.bn_aggr(mv[:, t, :], stats[:, t, :])
                        last.then_inc(ln_aggr, 1)
                    if n == 8:
                        dve.wait_ge(ln_rstd, b + 1)
                        for t in range(TT):
                            nc.vector.tensor_scalar(xn[:, t, :], x_b[:, b, t, :], mv[:, t, 0:1], rstd[:, t:t + 1],
                                                    ALU.subtract, ALU.mult).then_inc(xn_ready, 1)
                    if n == 14:
                        turn(it, new, "q")
                    if n == 15:
                        turn(it, new, "k")

            def decayed(b, n):
                h = (n % QUAD) * QUAD + n // QUAD
                dve.wait_ge(sr.filled, sr.nth(b, n))
                if not (is_first(b[0]) and n < AB):
                    dve.wait_ge(av_done, b[0] * H + n - AB + 1)
                nc.vector.tensor_tensor(att[:, n % AB, :], sr.bank(b, n)[:, 0:T + P], decay[:, h, :], ALU.mult)\
                    .then_inc(sr.emptied, 1)

            def step(it, inner=False):
                b, end = Pipeline.attend(it), Pipeline.finish(it)
                if end:
                    dve.wait_ge(av_done, end[0] * H + H)
                for n in range(H):
                    if b:
                        decayed(b, n)
                    small(it, n)

            dve.wait_ge(k.loaded, k.loaded_count)
            dve.wait_ge(loaded, LOADS)
            Pipeline.run(dve, step)

        @block.gpsimd
        def _(pool):
            pad_rows(nc.gpsimd, ks, padded)
            pool.wait_ge(padded, 4)

            def step(it, inner=False):
                new, prep, end = Pipeline.start(it), Pipeline.prepare(it), Pipeline.finish(it)
                if prep:
                    b, par = prep
                    pool.wait_ge(part1, b + 1)
                    nc.gpsimd.tensor_tensor(rest[:, :, :], qk[:, :, :], parts[:, par, 0, :, :], ALU.subtract)\
                        .then_inc(rest1, 1)
                    pool.wait_ge(part2, b + 1)
                    nc.gpsimd.tensor_tensor(parts[:, par, 2, :, :], rest[:, :, :], parts[:, par, 1, :, :],
                                            ALU.subtract).then_inc(parts_ready, 1)
                if end:
                    b = end[0]
                    pool.wait_ge(desk.emptied, desk.done(it, "gv"))
                    nc.gpsimd.tensor_tensor(veps_y[:, :], var[:, :], k.eps[:, 0:1], ALU.add).then_inc(y_veps, 1)
                    pool.wait_ge(y_veps, b + 1)
                    nc.gpsimd.tensor_tensor(rstd_y[:, :], veps_y[:, :], k.minus_half[:, 0:1], ALU.pow)\
                        .then_inc(y_rstd, 1)
                if new:
                    b = new[0]
                    pool.wait_ge(ln_aggr, b + 1)
                    nc.gpsimd.tensor_tensor(veps[:, :], mv[:, :, 1], k.eps[:, 0:TT], ALU.add).then_inc(ln_veps, 1)
                    pool.wait_ge(ln_veps, b + 1)
                    nc.gpsimd.tensor_tensor(rstd[:, :], veps[:, :], k.minus_half[:, 0:TT], ALU.pow).then_inc(ln_rstd, 1)
                if prep:
                    b, par = prep
                    pool.wait_ge(desk.emptied, desk.done(it, "g"))
                    nc.gpsimd.tensor_tensor(eg[:, :], eg[:, :], one[:, :].to_broadcast([P, T]), ALU.add)\
                        .then_inc(eg1, 1)
                if end:
                    b = end[0]
                    pool.wait_ge(desk.emptied, desk.done(it, "o"))
                    nc.gpsimd.tensor_tensor(x_b[:, b, :, :], x_b[:, b, :, :], ob[:, :, :], ALU.add).then_inc(x_done, 1)
                if prep:
                    b, par = prep
                    pool.wait_ge(eg2, b + 1)
                    if not is_first(b) and not is_first(b, 1):
                        pool.wait_ge(gated_ready, b - 1)
                    nc.gpsimd.tensor_tensor(silu[:, par, :], gate[:, :], eg[:, :], ALU.mult).then_inc(silu_ready, 1)
                if new:
                    b = new[0]
                    for u, (src, turned) in enumerate(((qp, qp_turned), (kp, kp_turned))):
                        pool.wait_ge(turned, b + 1)
                        nc.gpsimd.tensor_tensor(qk[:, u, :], src[:, 0, :], src[:, 1, :], ALU.add).then_inc(qk_ready, 1)

            pool.wait_ge(k.loaded, k.loaded_count)
            pool.wait_ge(one_ready, 1)
            Pipeline.run(pool, step)


def head_at(hs):
    return (hs % QUAD) * QUAD + hs // QUAD


def layer1_weights(nc, a, io):
    w = Weights()
    w.keys, w.values = a.sb("keys", [P, E1, P]), a.sb("values", [P, E1, C])
    w.selw, w.ln = a.sb("selw", [P, E1]), a.sb("ln", [P, 4])
    w.ws = a.sb("ws", [ROWS, 2, H, C], BF16)
    w.experts_loaded, w.experts_count = a.sem("experts_loaded"), 32
    w.small_loaded, w.small_count = a.sem("small_loaded"), 32
    scratch = nc.dram_tensor("l1_scratch", (6, P, C), BF16, kind="Internal").ap()
    with ExitStack() as ctx:
        b = Pool_(nc, ctx, "wp")
        wp, rest = b.sb("wp", [P, 2, C]), b.sb("rest", [P, 2, C])
        parts = b.sb("parts", [P, 3, 2, C], BF16)
        loaded, part1, rest1, part2, parts_ready, bounced, stacked, padded = [b.sem(n) for n in (
            "loaded", "part1", "rest1", "part2", "parts_ready", "bounced", "stacked", "padded")]
        block = ctx.enter_context(nc.Block())

        @block.sync
        def _(sp):
            sp.dma_start(wp[:, :, :], io["wp"]).then_inc(loaded, 16)
            sp.dma_start(w.selw[:, :], io["selw"]).then_inc(w.small_loaded, 16)
            sp.dma_start(w.ln[:, :], io["ln"]).then_inc(w.small_loaded, 16)
            sp.wait_ge(parts_ready, 1)
            sp.dma_start(scratch.rearrange("n c f -> c n f"), parts[:, :, :, :].rearrange("c n u f -> c (n u) f")).then_inc(bounced, 16)
            sp.wait_ge(bounced, 16)
            sp.wait_ge(padded, 2)
            for first, run in RUNS:
                for u in range(2):
                    sp.dma_start(w.ws[first * HD:(first + run) * HD, u, :, :].rearrange("s h f -> s (h f)"),
                                 slots_of(scratch[u], run, 2 * P * C, C)).then_inc(stacked, 16)
            sp.dma_start(w.keys[:, :, :], io["keys"]).then_inc(w.experts_loaded, 16)
            sp.dma_start(w.values[:, :, :], io["values"]).then_inc(w.experts_loaded, 16)
            sp.wait_ge(w.small_loaded, w.small_count)
            sp.wait_ge(stacked, STACKED)

        @block.gpsimd
        def _(pool):
            for rows in (slice(32, 64), slice(64, ROWS)):
                nc.gpsimd.memset(w.ws[rows, :, :, :].rearrange("p u h f -> p (u h f)"), 0.0).then_inc(padded, 1)

        @block.vector
        def _(dve):
            dve.wait_ge(loaded, 16)
            nc.vector.tensor_copy(parts[:, 0, :, :], wp[:, :, :]).then_inc(part1, 1)
            dve.wait_ge(part1, 1)
            nc.vector.tensor_tensor(rest[:, :, :], wp[:, :, :], parts[:, 0, :, :], ALU.subtract).then_inc(rest1, 1)
            dve.wait_ge(rest1, 1)
            nc.vector.tensor_copy(parts[:, 1, :, :], rest[:, :, :]).then_inc(part2, 1)
            dve.wait_ge(part2, 1)
            nc.vector.tensor_tensor(parts[:, 2, :, :], rest[:, :, :], parts[:, 1, :, :], ALU.subtract)\
                .then_inc(parts_ready, 1)

    return w


def relative_ffn(nc, tag, x_sb, k, w, io):
    with ExitStack() as ctx:
        a = Pool_(nc, ctx, tag)
        x2t = a.sb("x2t", [P, B * TT, P])
        gates = a.sb("gates", [P, B * TT, E1])
        softmax_attention(nc, f"{tag}a", x_sb, k, io, w, x2t, gates)
        mixture(nc, f"{tag}m", x_sb, k, w, x2t, gates)


def plain_attention(nc, tag, x_sb, k, io):
    softmax_attention(nc, tag, x_sb, k, io)


def softmax_attention(nc, tag, x_sb, k, io, w=None, x2t_all=None, gates=None):
    rel = w is not None
    x_b = x_sb[:, :, :].rearrange("p (b t) c -> p b t c", t=TT)
    SB = 2 if rel else 4
    NR, RRS, AHEAD = 16, 8, 3
    with ExitStack() as ctx:
        a = Pool_(nc, ctx, tag)
        wq, wo = a.sb("wq", [P, 3, C]), a.sb("wo", [P, C])
        stats, mv = a.sb("stats", [P, TT, 6]), a.sb("mv", [P, TT, 2])
        veps, rstd = a.sb("veps", [P, TT]), a.sb("rstd", [P, TT])
        xn, xt = a.sb("xn", [P, TT, C]), a.sb("xt", [P, T])
        qk, rest = a.sb("qk", [P, 2, T]), a.sb("rest", [P, 2, T])
        parts = a.sb("parts", [P, 2, 3, 2, T], BF16)
        qs, ks = a.sb("qs", [ROWS, 2, H, T], BF16), a.sb("ks", [ROWS, 2, H, T], BF16)
        scratch = nc.dram_tensor(f"{tag}_scratch", (2, 6, P, T), BF16, kind="Internal").ap()
        vm = a.sb("vm", [P, 2, TT, QUAD, C])
        nm = a.sb("nm", [P, SB, 2])
        zs = a.sb("zs", [P, 2, TT, H])
        pr = a.sb("pr", [P, 4, 2, T])
        pts = a.sb("pts", [P, 2, TT, QUAD, T])
        rz, rz8, rzb = a.sb("rz", [P, TT, H]), a.sb("rz8", [P, TT, H, HD]), a.sb("rzb", [P, T])
        yn, ob = a.sb("yn", [P, T]), a.sb("ob", [P, TT, C])
        if rel:
            src = a.sb("src", [P, B, TT, C])
            pe_t, turn = a.sb("pe", [P, T]), a.sb("turn", [P, 2, T])
            tmp, rr = a.sb("tmp", [P, 2, 2, T]), a.sb("rr", [P, RRS, T])
            s1, x2 = a.sb("s1", [P, TT, C]), a.sb("x2", [P, TT, C])
            stats2, mv2 = a.sb("stats2", [P, TT, 6]), a.sb("mv2", [P, TT, 2])
            veps2, rstd2 = a.sb("veps2", [P, TT]), a.sb("rstd2", [P, TT])
            stats3, mv3 = a.sb("stats3", [P, TT, 6]), a.sb("mv3", [P, TT, 2])
            veps3, rstd3 = a.sb("veps3", [P, TT]), a.sb("rstd3", [P, TT])
            x2s = a.sb("x2s", [P, T])
            sel, best = a.sb("sel", [P, TT, E1]), a.sb("best", [P, TT, 8])
            best_at, best_f = a.sb("best_at", [P, TT, 8], U32), a.sb("best_f", [P, TT, TOPK])
            pick, pair = a.sb("pick", [P, TT, TOPK, E1]), a.sb("pair", [P, TT, 2, E1])
        else:
            bp = a.sb("bp", [P, C])

        sr = Ring(a.ps("sr", [P, SB, 512]), a.sem("sr_filled"), a.sem("sr_emptied"), NR, SB)
        tr = [Ring(a.ps(f"tr{e}", [P, 1, 512]), a.sem(f"tr{e}_filled"), a.sem(f"tr{e}_emptied"), NR // 2, 1)
              for e in range(2)]
        y_ps = a.ps("y", [P, 512])
        desk = Desk(a.ps("desk", [P, 1, 512]), a.sem("desk_filled"), a.sem("desk_emptied"),
                    [("rz", 3), ("v", 1), ("o", 3)] + ([("x2t", 3), ("sel", 3)] if rel else []) +
                    [("xt", 0), ("qk", 0)], 1)
        if rel:
            ur = Ring(a.ps("ur", [P, 2, 512]), a.sem("ur_filled"), a.sem("ur_emptied"), H, 2)
        names = ("loaded wq_scaled vm_zero ln_stats ln_aggr ln_veps ln_rstd xn_ready part1 rest1 part2 parts_ready "
                 "bounced stacked passed padded nm_ready av_done rz_ready rz8_ready yn_ready bias_added x_done").split()
        (loaded, wq_scaled, vm_zero, ln_stats, ln_aggr, ln_veps, ln_rstd, xn_ready, part1, rest1, part2, parts_ready,
         bounced, stacked, passed, padded, nm_ready, av_done, rz_ready, rz8_ready, yn_ready, bias_added, x_done) = [
             a.sem(n) for n in names]
        if rel:
            names = ("src_ready src_stats src_aggr src_veps src_rstd turned rr_ready s1_ready s1_stats s1_aggr s1_veps "
                     "s1_rstd x2_ready gate_step gates_ready").split()
            (src_ready, src_stats, src_aggr, src_veps, src_rstd, turned, rr_ready, s1_ready, s1_stats, s1_aggr,
             s1_veps, s1_rstd, x2_ready, gate_step, gates_ready) = [a.sem(n) for n in names]
        block = ctx.enter_context(nc.Block())

        attend, finish, prep, new = Pipeline.attend, Pipeline.finish, Pipeline.prepare, Pipeline.start

        def turning(it, n):
            if n >= 2:
                return (attend(it), n - 2)
            return (finish(it), NR - 2 + n)

        def relating(it, n):
            if n + AHEAD < NR:
                return (attend(it), n + AHEAD)
            return (prep(it), n + AHEAD - NR)

        def later_than(b, first):
            return not isinstance(b[0], int) or b[0] >= first

        LOADS = 16 * (4 if rel else 3)

        @block.sync
        def _(sp):
            sp.dma_start(wq[:, :, :], io["w4" if rel else "w5"].rearrange("p (n c) -> p n c", c=C)).then_inc(loaded, 16)
            sp.dma_start(wo[:, :], io["w4p" if rel else "w5p"]).then_inc(loaded, 16)
            if rel:
                sp.dma_start(pe_t[:, :], io["pe"]).then_inc(loaded, 16)
                sp.dma_start(turn[:, :, :], io["turn"]).then_inc(loaded, 16)
            else:
                sp.dma_start(bp[:, :], io["b5p"].partition_broadcast(P)).then_inc(loaded, 16)
            stack_parts(sp, parts, scratch, qs, ks, parts_ready, bounced, stacked, passed, sr, padded)

        @block.tensor
        def _(pe):
            def fill(it, name):
                pe.wait_ge(desk.emptied, desk.nth(it, name))
                return desk.bank(it, name)

            def relate(b, hs):
                if hs == 0:
                    pe.wait_ge(stacked, b[0] * STACKED + STACKED)
                pe.wait_ge(ur.emptied, ur.nth(b, hs))
                out = ur.bank(b, hs)
                h = head_at(hs)
                for u in range(2):
                    mm = nc.tensor.matmul(out[:, u * T:(u + 1) * T], w.ws[:, u, h, :], qs[:, b[1], h, :],
                                          start=True, stop=True)
                mm.then_inc(ur.filled, 1)

            def scores(b, n):
                r, jj, t = n // QUAD, n // 2 % 2, n % 2
                pe.wait_ge(sr.emptied, sr.nth(b, n))
                if rel and t == 0:
                    pe.wait_ge(rr_ready, b[0] * H + n + 2)
                for x in range(2):
                    h = (2 * jj + x) * QUAD + r
                    out = sr.bank(b, n)[:, x * T:(x + 1) * T]
                    mm = nc.tensor.matmul(out, qs[:, b[1], h, t * P:(t + 1) * P], ks[:, b[1], h, :],
                                          start=True, stop=not rel)
                    if rel:
                        mm = nc.tensor.matmul(out, rr[:, (n - t + x) % RRS, t * P:(t + 1) * P], pe_t[:, :],
                                              start=False, stop=True)
                mm.then_inc(sr.filled, 1)

            def turn_round(b, n):
                ring = tr[n % 2]
                pe.wait_ge(ring.emptied, ring.nth(b, n // 2))
                pe.wait_ge(sr.emptied, sr.done(b, n))
                for st in range(TT):
                    for x in range(2):
                        o = (st * 2 + x) * P
                        mm = nc.tensor.transpose(ring.bank(b, n // 2)[:, o:o + P],
                                                 pr[:, n % 4, x, st * P:(st + 1) * P], k.ident)
                mm.then_inc(ring.filled, 1)

            def values(b, r):
                for e in range(2):
                    pe.wait_ge(tr[e].emptied, tr[e].done(b, 2 * r + 1))
                if r == 0 and later_than(b, 1):
                    pe.wait_ge(yn_ready, b[0])
                for st in range(TT):
                    for j in range(QUAD):
                        q = slice(j * QUAD * HD, (j + 1) * QUAD * HD)
                        mm = nc.tensor.matmul(y_ps[q, 0:T], vm[:, b[1], st, r, q], pts[:, r % 2, st, j, :],
                                              start=(r == 0 and st == 0), stop=(r == QUAD - 1 and st == TT - 1),
                                              skip_group_check=True)
                mm.then_inc(av_done, 1)

            def small(it, n):
                b, e = new(it), finish(it)
                if n == 3 and e:
                    pe.wait_ge(rz8_ready, e[0] + 1)
                    out = fill(it, "rz")
                    for t in range(TT):
                        mm = nc.tensor.transpose(out[:, t * P:(t + 1) * P],
                                                 rz8[:, t, :, :].rearrange("p h d -> p (h d)"), k.ident)
                    mm.then_inc(desk.filled, 1)
                if n == 4 and prep(it):
                    out = fill(it, "v")
                    for t in range(TT):
                        mm = nc.tensor.matmul(out[:, t * P:(t + 1) * P], xt[:, t * P:(t + 1) * P], wq[:, 2, :],
                                              start=True, stop=True)
                    mm.then_inc(desk.filled, 1)
                if n == 6 and e:
                    out = fill(it, "o")
                    pe.wait_ge(yn_ready, e[0] + 1)
                    for t in range(TT):
                        mm = nc.tensor.matmul(out[:, t * P:(t + 1) * P], yn[:, t * P:(t + 1) * P], wo[:, :],
                                              start=True, stop=True)
                    mm.then_inc(desk.filled, 1)
                if rel and n == 10 and e:
                    out = fill(it, "x2t")
                    pe.wait_ge(x2_ready, e[0] * TT + TT)
                    for t in range(TT):
                        mm = nc.tensor.transpose(out[:, t * P:(t + 1) * P], x2[:, t, :], k.ident)
                    mm.then_inc(desk.filled, 1)
                if rel and n == 12 and e:
                    out = fill(it, "sel")
                    for t in range(TT):
                        mm = nc.tensor.matmul(out[:, t * E1:(t + 1) * E1], x2s[:, t * P:(t + 1) * P], w.selw[:, :],
                                              start=True, stop=True)
                    mm.then_inc(desk.filled, 1)
                if n == 13 and b:
                    pe.wait_ge(xn_ready, b[0] * TT + TT)
                    out = fill(it, "xt")
                    for t in range(TT):
                        mm = nc.tensor.transpose(out[:, t * P:(t + 1) * P], xn[:, t, :], k.ident)
                    mm.then_inc(desk.filled, 1)
                if n == 14 and b:
                    out = fill(it, "qk")
                    for u in range(2):
                        mm = nc.tensor.matmul(out[:, u * T:(u + 1) * T], wq[:, u, :], xt[:, :], start=True, stop=True)
                    mm.then_inc(desk.filled, 1)

            def step(it, inner=False):
                for n in range(NR):
                    small(it, n)
                    if rel:
                        b, hs = relating(it, n)
                        if b is not None:
                            relate(b, hs)
                    if attend(it):
                        if n == 0 and not rel:
                            pe.wait_ge(stacked, attend(it)[0] * STACKED + STACKED)
                        scores(attend(it), n)
                    b, m = turning(it, n)
                    if b is not None:
                        turn_round(b, m)
                    if n in (7, 11, 15) and attend(it):
                        values(attend(it), (n - 7) // 4)
                    if n == 3 and finish(it):
                        values(finish(it), 3)

            pe.wait_ge(k.loaded, k.loaded_count)
            pe.wait_ge(loaded, LOADS)
            pe.wait_ge(wq_scaled, 1)
            pe.wait_ge(vm_zero, 1)
            Pipeline.run(pe, step)

        def take_turned(eng, b, n, copy):
            r, jj, t = n // QUAD, n // 2 % 2, n % 2
            ring = tr[t]
            eng.wait_ge(ring.filled, ring.nth(b, n // 2))
            if n % QUAD < 2 and (r >= 2 or later_than(b, 1)):
                eng.wait_ge(av_done, b[0] * QUAD + r - 1)
            copy(pts[:, r % 2, :, 2 * jj:2 * jj + 2, t * P:(t + 1) * P],
                 ring.bank(b, n // 2).rearrange("p (s x t) -> p s x t", s=TT, x=2)).then_inc(ring.emptied, 1)

        @block.scalar
        def _(act):
            act.sem_inc(desk.emptied, 1)
            act.sem_inc(tr[1].emptied, 1)
            act.sem_inc(sr.emptied, SB)

            def copy(dst, src_):
                return nc.scalar.activation(dst, src_, ACT.Copy)

            def taken(it, name):
                act.wait_ge(desk.filled, desk.nth(it, name))
                return desk.bank(it, name)

            def exponentials(b, n):
                t, hs = n % 2, n - n % 2
                act.wait_ge(nm_ready, b[0] * NR + n + 1)
                if n >= 4 or later_than(b, 1):
                    act.wait_ge(tr[t].filled, b[0] * (NR // 2) + n // 2 - 1)
                if n == 0 and later_than(b, 2):
                    act.wait_ge(rz_ready, b[0] - 1)
                for x in range(2):
                    h = head_at(hs + x)
                    last = nc.scalar.activation(pr[:, n % 4, x, :], sr.bank(b, n)[:, x * T:(x + 1) * T], ACT.Exp,
                                                bias=nm[:, n % SB, x:x + 1], accum_out=zs[:, b[1], t, h:h + 1])
                last.then_inc(sr.emptied, 1)

            def small(it, n):
                b, p, e = new(it), prep(it), finish(it)
                if n == 3 and e:
                    bank = taken(it, "rz")
                    copy(rzb[:, :], bank[:, 0:T]).then_inc(desk.emptied, 1)
                if n == 4 and p:
                    bank = taken(it, "v")
                    if not is_first(p[0]) and not is_first(p[0], 1):
                        act.wait_ge(av_done, (p[0] - 1) * QUAD)
                    for t in range(TT):
                        last = copy(heads_of((vm, p[1], t)),
                                    bank[:, t * P:(t + 1) * P].rearrange("p (j r d) -> p r j d", r=QUAD, d=HD))
                    last.then_inc(desk.emptied, 1)
                if n == 6 and e:
                    bank = taken(it, "o")
                    if not is_first(e[0]):
                        act.wait_ge(s1_ready if rel else x_done, e[0])
                    copy(ob[:, :, :].rearrange("p t c -> p (t c)"), bank[:, 0:T]).then_inc(desk.emptied, 1)
                if rel and n == 10 and e:
                    bank = taken(it, "x2t")
                    nc.scalar.activation(x2s[:, :], bank[:, 0:T], ACT.Identity, scale=w.ln[:, 2:3], bias=w.ln[:, 3:4])
                    tiles = x2t_all[:, :, :].rearrange("p (b t) c -> p b (t c)", t=TT)
                    nc.scalar.activation(tiles[:, e[0], :], bank[:, 0:T], ACT.Identity, scale=w.ln[:, 2:3],
                                         bias=w.ln[:, 3:4]).then_inc(desk.emptied, 1)
                if rel and n == 12 and e:
                    bank = taken(it, "sel")
                    if not is_first(e[0]):
                        act.wait_ge(gates_ready, e[0])
                    nc.scalar.activation(sel[:, :, :].rearrange("p t e -> p (t e)"), bank[:, 0:TT * E1], ACT.Exp,
                                         scale=-1.0).then_inc(desk.emptied, 1)
                if n == 13 and b:
                    bank = taken(it, "xt")
                    if rel:
                        last = nc.scalar.activation(xt[:, :], bank[:, 0:T], ACT.Identity, scale=w.ln[:, 0:1],
                                                    bias=w.ln[:, 1:2])
                    else:
                        last = copy(xt[:, :], bank[:, 0:T])
                    last.then_inc(desk.emptied, 1)
                if n == 14 and b:
                    bank = taken(it, "qk")
                    if not is_first(b[0]):
                        act.wait_ge(rest1, b[0])
                    copy(qk[:, :, :].rearrange("p u t -> p (u t)"), bank).then_inc(desk.emptied, 1)

            def step(it, inner=False):
                for n in range(NR):
                    small(it, n)
                    b, m = turning(it, n)
                    if b is not None and m % 2:
                        take_turned(act, b, m, copy)
                    if attend(it):
                        exponentials(attend(it), n)

            act.wait_ge(vm_zero, 1)
            if rel:
                act.wait_ge(w.small_loaded, w.small_count)
            Pipeline.run(act, step)

        @block.vector
        def _(dve):
            dve.sem_inc(tr[0].emptied, 1)
            if rel:
                dve.sem_inc(ur.emptied, 2)
            nc.vector.memset(vm[:, :, :, :, :].rearrange("p a b c d -> p (a b c d)"), 0.0).then_inc(vm_zero, 1)
            pad_rows(nc.vector, qs, padded)

            def measure(i, value, stats_, mv_, stats_sem, aggr_sem):
                for t in range(TT):
                    nc.vector.bn_stats(stats_[:, t, :], value(t)).then_inc(stats_sem, 1)
                dve.wait_ge(stats_sem, i * TT + TT)
                nc.vector.memset(k.idle, 0.0)
                for t in range(TT):
                    last = nc.vector.bn_aggr(mv_[:, t, :], stats_[:, t, :])
                last.then_inc(aggr_sem, 1)

            def normalise(dst, value, mv_, rstd_, ready):
                for t in range(TT):
                    nc.vector.tensor_scalar(dst(t), value(t), mv_[:, t, 0:1], rstd_[:, t:t + 1], ALU.subtract,
                                            ALU.mult).then_inc(ready, 1)

            def maxima(b, n):
                dve.wait_ge(sr.filled, sr.nth(b, n))
                nc.vector.tensor_reduce(nm[:, n % SB, :], sr.bank(b, n).rearrange("p (x s) -> p x s", x=2), AX.X,
                                        ALU.max, negate=True).then_inc(nm_ready, 1)

            def rotate(b, hs):
                dve.wait_ge(ur.filled, ur.nth(b, hs))
                if hs >= 2 or later_than(b, 1):
                    dve.wait_ge(rr_ready, b[0] * H + hs - 1)
                nc.vector.tensor_tensor(tmp[:, hs % 2, :, :], ur.bank(b, hs).rearrange("p (u t) -> p u t", u=2),
                                        turn[:, :, :], ALU.mult).then_inc(ur.emptied, 1)

            def gate(it):
                i = finish(it)[0]
                steps_ = [0]

                def stepped(last):
                    last.then_inc(gate_step, 1)
                    steps_[0] += 1
                    dve.wait_ge(gate_step, i * 8 + steps_[0])

                dve.wait_ge(desk.emptied, desk.done(it, "sel"))
                stepped(nc.vector.tensor_scalar(sel[:, :, :], sel[:, :, :], 1.0, None, ALU.add))
                stepped(nc.vector.reciprocal(sel[:, :, :], sel[:, :, :]))
                nc.vector.memset(k.idle, 0.0)
                for t in range(TT):
                    last = nc.vector.max(best[:, t, :], sel[:, t, :])
                stepped(last)
                nc.vector.memset(k.idle, 0.0)
                for t in range(TT):
                    last = nc.vector.max_index(best_at[:, t, :], best[:, t, :], sel[:, t, :])
                stepped(last)
                stepped(nc.vector.tensor_copy(best_f[:, :, :], best_at[:, :, 0:TOPK]))
                for t in range(TT):
                    last = nc.vector.tensor_tensor(pick[:, t, :, :], k.iota32.unsqueeze(1).to_broadcast([P, TOPK, E1]),
                                                   best_f[:, t, :].unsqueeze(2).to_broadcast([P, TOPK, E1]),
                                                   ALU.is_equal)
                stepped(last)
                for t in range(TT):
                    last = nc.vector.tensor_tensor(pick[:, t, :, :], pick[:, t, :, :],
                                                   best[:, t, 0:TOPK].unsqueeze(2).to_broadcast([P, TOPK, E1]),
                                                   ALU.mult)
                stepped(last)
                stepped(nc.vector.tensor_tensor(pair[:, :, :, :], pick[:, :, 0:2, :], pick[:, :, 2:4, :], ALU.add))
                g = gates[:, :, :].rearrange("p (b t) e -> p b t e", t=TT)
                nc.vector.tensor_tensor(g[:, i, :, :], pair[:, :, 0, :], pair[:, :, 1, :], ALU.add)\
                    .then_inc(gates_ready, 1)

            def small(it, n):
                b, p, e = new(it), prep(it), finish(it)
                if e:
                    i, par = e
                    if n == 1:
                        dve.wait_ge(sr.emptied, sr.done(e, NR - 1))
                        nc.vector.reciprocal(rz[:, :, :], zs[:, par, :, :]).then_inc(rz_ready, 1)
                        dve.wait_ge(rz_ready, i + 1)
                        nc.vector.tensor_copy(rz8[:, :, :, :], rz[:, :, :].unsqueeze(3).to_broadcast([P, TT, H, HD]))\
                            .then_inc(rz8_ready, 1)
                    if n == 4:
                        dve.wait_ge(av_done, (i + 1) * QUAD)
                        dve.wait_ge(desk.emptied, desk.done(it, "rz"))
                        nc.vector.tensor_tensor(yn[:, :], y_ps[:, 0:T], rzb[:, :], ALU.mult).then_inc(yn_ready, 1)
                    if rel and n == 7:
                        dve.wait_ge(desk.emptied, desk.done(it, "o"))
                        nc.vector.tensor_tensor(s1[:, :, :], ob[:, :, :], src[:, i, :, :], ALU.add)\
                            .then_inc(s1_ready, 1)
                        dve.wait_ge(s1_ready, i + 1)
                        nc.vector.scalar_tensor_tensor(x_b[:, i, :, :], s1[:, :, :], 0.5, x_b[:, i, :, :],
                                                       ALU.mult, ALU.add)
                        measure(i, lambda t: s1[:, t, :], stats3, mv3, s1_stats, s1_aggr)
                    if rel and n == 8:
                        dve.wait_ge(s1_rstd, i + 1)
                        normalise(lambda t: x2[:, t, :], lambda t: s1[:, t, :], mv3, rstd3, x2_ready)
                    if rel and n == 14:
                        gate(it)
                if p:
                    i, par = p
                    if n == 1:
                        if not is_first(i) and not is_first(i, 1):
                            dve.wait_ge(bounced, i * 16 - 16)
                        dve.wait_ge(desk.emptied, desk.done(before(it), "qk"))
                        nc.vector.tensor_copy(parts[:, par, 0, :, :], qk[:, :, :]).then_inc(part1, 1)
                    if n == 3:
                        dve.wait_ge(rest1, i + 1)
                        nc.vector.tensor_copy(parts[:, par, 1, :, :], rest[:, :, :]).then_inc(part2, 1)
                if b:
                    i = b[0]
                    x_of = lambda t: x_b[:, i, t, :]
                    if rel and n == 5:
                        measure(i, x_of, stats2, mv2, src_stats, src_aggr)
                    if rel and n == 6:
                        dve.wait_ge(src_rstd, i + 1)
                        normalise(lambda t: src[:, i, t, :], x_of, mv2, rstd2, src_ready)
                        dve.wait_ge(src_ready, i * TT + TT)
                        nc.vector.memset(k.idle, 0.0)
                    if n == 9:
                        measure(i, (lambda t: src[:, i, t, :]) if rel else x_of, stats, mv, ln_stats, ln_aggr)
                    if n == 11:
                        dve.wait_ge(ln_rstd, i + 1)
                        normalise(lambda t: xn[:, t, :], (lambda t: src[:, i, t, :]) if rel else x_of, mv, rstd, xn_ready)

            def step(it, inner=False):
                for n in range(NR):
                    if rel:
                        b, hs = relating(it, n)
                        if b is not None:
                            rotate(b, hs)
                    if attend(it):
                        maxima(attend(it), n)
                    b, m = turning(it, n)
                    if b is not None and m % 2 == 0:
                        take_turned(dve, b, m, nc.vector.tensor_copy)
                    small(it, n)

            dve.wait_ge(k.loaded, k.loaded_count)
            dve.wait_ge(loaded, LOADS)
            nc.vector.tensor_scalar(wq[:, 0, :], wq[:, 0, :], float(np.float32(HD ** -0.5)), None, ALU.mult)\
                .then_inc(wq_scaled, 1)
            Pipeline.run(dve, step)

        @block.gpsimd
        def _(pool):
            pad_rows(nc.gpsimd, ks, padded)
            pool.wait_ge(padded, 4)

            def root(i, mv_, veps_, rstd_, aggr_sem, veps_sem, rstd_sem):
                pool.wait_ge(aggr_sem, i + 1)
                nc.gpsimd.tensor_tensor(veps_[:, :], mv_[:, :, 1], k.eps[:, 0:TT], ALU.add).then_inc(veps_sem, 1)
                pool.wait_ge(veps_sem, i + 1)
                nc.gpsimd.tensor_tensor(rstd_[:, :], veps_[:, :], k.minus_half[:, 0:TT], ALU.pow).then_inc(rstd_sem, 1)

            def add_forms(b, hs):
                if hs % 2 == 0 and (hs >= RRS or later_than(b, 1)):
                    pool.wait_ge(sr.filled, b[0] * NR + hs + 2 - RRS)
                pool.wait_ge(ur.emptied, ur.done(b, hs))
                nc.gpsimd.tensor_tensor(rr[:, hs % RRS, :], tmp[:, hs % 2, 0, :], tmp[:, hs % 2, 1, :], ALU.add)\
                    .then_inc(rr_ready, 1)

            def small(it, n):
                b, p, e = new(it), prep(it), finish(it)
                if p:
                    i, par = p
                    if n == 1:
                        pool.wait_ge(part1, i + 1)
                        nc.gpsimd.tensor_tensor(rest[:, :, :], qk[:, :, :], parts[:, par, 0, :, :], ALU.subtract)\
                            .then_inc(rest1, 1)
                    if n == 3:
                        pool.wait_ge(part2, i + 1)
                        nc.gpsimd.tensor_tensor(parts[:, par, 2, :, :], rest[:, :, :], parts[:, par, 1, :, :],
                                                ALU.subtract).then_inc(parts_ready, 1)
                if e:
                    i = e[0]
                    if rel and n == 7:
                        root(i, mv3, veps3, rstd3, s1_aggr, s1_veps, s1_rstd)
                    if not rel and n == 7:
                        pool.wait_ge(desk.emptied, desk.done(it, "o"))
                        nc.gpsimd.tensor_tensor(ob[:, :, :], ob[:, :, :], bp[:, :].unsqueeze(1)
                                                .to_broadcast([P, TT, C]), ALU.add).then_inc(bias_added, 1)
                        pool.wait_ge(bias_added, i + 1)
                        nc.gpsimd.tensor_tensor(x_b[:, i, :, :], x_b[:, i, :, :], ob[:, :, :], ALU.add)\
                            .then_inc(x_done, 1)
                if b:
                    if rel and n == 5:
                        root(b[0], mv2, veps2, rstd2, src_aggr, src_veps, src_rstd)
                    if n == 9:
                        root(b[0], mv, veps, rstd, ln_aggr, ln_veps, ln_rstd)

            def step(it, inner=False):
                for n in range(NR):
                    if rel:
                        b, hs = relating(it, n)
                        if b is not None:
                            add_forms(b, hs)
                    small(it, n)

            pool.wait_ge(k.loaded, k.loaded_count)
            pool.wait_ge(loaded, LOADS)
            Pipeline.run(pool, step)


def mixture(nc, tag, x_sb, k, w, x2t, gates):
    G, GT = 8, 4
    HB, OB = 4, 4
    LAG = 2
    with ExitStack() as ctx:
        a = Pool_(nc, ctx, tag)
        ht = a.sb("ht", [P, HB, GT * P])
        gg = a.sb("gg", [P, GT, E1])
        acc = a.sb("acc", [P, GT, C])
        hr = Ring(a.ps("hr", [P, HB, 512]), a.sem("hr_filled"), a.sem("hr_emptied"), E1, HB)
        our = Ring(a.ps("our", [P, OB, 512]), a.sem("our_filled"), a.sem("our_emptied"), E1, OB)
        gg_ready = a.sem("gg_ready")
        block = ctx.enter_context(nc.Block())
        x_g = x_sb[:, :, :].rearrange("p (g t) c -> p g t c", t=GT)
        x2_g = x2t[:, :, :].rearrange("p (g t) c -> p g (t c)", t=GT)
        gates_g = gates[:, :, :].rearrange("p (g t) e -> p g t e", t=GT)

        @block.tensor
        def _(pe):
            def hidden(it, e):
                pe.wait_ge(hr.emptied, hr.nth(it, e))
                nc.tensor.matmul(hr.bank(it, e), w.keys[:, e, :], x2_g[:, it[0], :], start=True, stop=True)\
                    .then_inc(hr.filled, 1)

            def output(it, e):
                pe.wait_ge(our.emptied, our.nth(it, e))
                pe.wait_ge(hr.emptied, hr.done(it, e))
                for t in range(GT):
                    mm = nc.tensor.matmul(our.bank(it, e)[:, t * P:(t + 1) * P], ht[:, e % HB, t * P:(t + 1) * P],
                                          w.values[:, e, :], start=True, stop=True)
                mm.then_inc(our.filled, 1)

            pe.wait_ge(w.experts_loaded, w.experts_count)
            with pe.Fori(0, G) as g:
                it = (g, 0)
                for e in range(E1 + LAG):
                    if e < E1:
                        hidden(it, e)
                    if e >= LAG:
                        output(it, e - LAG)

        @block.scalar
        def _(act):
            act.sem_inc(hr.emptied, HB)
            with act.Fori(0, G) as g:
                it = (g, 0)
                for e in range(E1):
                    act.wait_ge(hr.filled, hr.nth(it, e))
                    nc.scalar.activation(ht[:, e % HB, :], hr.bank(it, e), ACT.Relu).then_inc(hr.emptied, 1)

        @block.vector
        def _(dve):
            dve.sem_inc(our.emptied, OB)
            with dve.Fori(0, G) as g:
                it = (g, 0)
                nc.vector.tensor_copy(gg[:, :, :], gates_g[:, g, :, :]).then_inc(gg_ready, 1)
                dve.wait_ge(gg_ready, g + 1)
                for e in range(E1):
                    dve.wait_ge(our.filled, our.nth(it, e))
                    for t in range(GT):
                        out = our.bank(it, e)[:, t * P:(t + 1) * P]
                        if e == 0:
                            last = nc.vector.tensor_scalar(acc[:, t, :], out, gg[:, t, e:e + 1], None, ALU.mult)
                        else:
                            if t == 0:
                                dve.wait_ge(our.emptied, our.done(it, e - 1))
                            last = nc.vector.scalar_tensor_tensor(acc[:, t, :], out, gg[:, t, e:e + 1], acc[:, t, :],
                                                                  ALU.mult, ALU.add)
                    last.then_inc(our.emptied, 1)
                dve.wait_ge(our.emptied, our.done(it, E1 - 1))
                nc.vector.scalar_tensor_tensor(x_g[:, g, :, :], acc[:, :, :], 0.5, x_g[:, g, :, :], ALU.mult, ALU.add)


class Constants:
    pass


class Weights:
    pass


def constants(nc, a, cst):
    k = Constants()
    table = a.sb("table", [P, cst.shape[1]])
    bf = a.sb("bf", [P, 2 * P], BF16)
    half = a.sb("half", [P, 16])
    k.idle = a.sb("idle", [P, 1])[:, :]
    k.ident = table[:, 0:P]
    k.iota40 = table[:, 2 * P:2 * P + CAP]
    k.iota8 = table[:, 2 * P + CAP:2 * P + CAP + E0]
    k.iota32 = table[:, 2 * P + CAP + E0:2 * P + CAP + E0 + E1]
    k.tri_bf, k.ones_bf = bf[:, 0:P], bf[:, P:2 * P]
    k.eps, k.minus_half = half[:, 0:8], half[:, 8:16]
    k.table, k.bf, k.half, k.source = table, bf, half, cst
    k.loaded, k.loaded_count = a.sem("loaded"), 5
    return k


def load_x(nc, k, x, x_sb):
    with ExitStack() as ctx:
        a = Pool_(nc, ctx, "load")
        x_in, table_in = a.sem("x_in"), a.sem("table_in")
        block = ctx.enter_context(nc.Block())

        @block.sync
        def _(sp):
            sp.dma_start(k.table[:, :], k.source).then_inc(table_in, 16)
            sp.dma_start(x_sb[:, :, :], x.rearrange("b (t p) c -> p (b t) c", p=P)).then_inc(x_in, 16)
            sp.wait_ge(x_in, 16)

        @block.vector
        def _(dve):
            nc.vector.memset(k.ones_bf, 1.0).then_inc(k.loaded, 1)
            nc.vector.memset(k.eps, EPS).then_inc(k.loaded, 1)
            nc.vector.memset(k.minus_half, -0.5).then_inc(k.loaded, 1)
            dve.wait_ge(table_in, 16)
            nc.vector.tensor_copy(k.tri_bf, k.table[:, P:2 * P]).then_inc(k.loaded, 1)
            dve.sem_inc(k.loaded, 1)


def store_x(nc, x_sb, out):
    with ExitStack() as ctx:
        a = Pool_(nc, ctx, "store")
        stored = a.sem("stored")
        block = ctx.enter_context(nc.Block())

        @block.sync
        def _(sp):
            sp.dma_start(out.rearrange("b (t p) c -> p (b t) c", p=P), x_sb[:, :, :]).then_inc(stored, 16)
            sp.wait_ge(stored, 16)


def layer0_weights(nc, a, io):
    w = Weights()
    w.rw1, w.rw2, w.rw3 = a.sb("rw1", [P, HID]), a.sb("rw2", [P, KH, HID]), a.sb("rw3", [P, KH, E0])
    w.rb1, w.rb2, w.rb3 = a.sb("rb1", [P, KH]), a.sb("rb2", [P, KH]), a.sb("rb3", [P, E0])
    w.ew1, w.ew2 = a.sb("ew1", [P, E0, HID]), a.sb("ew2", [P, E0, KH, C])
    w.eb1, w.eb2 = a.sb("eb1", [P, E0, KH]), a.sb("eb2", [P, E0])
    w.router_loaded, w.router_count = a.sem("router_loaded"), 16 * 6
    w.experts_loaded, w.experts_count = a.sem("experts_loaded"), 16 * 4

    def load(sp):
        for dst, src in ((w.rw1[:, :], io["rW1"]), (w.rb1[:, :], io["rb1"]), (w.rw2[:, :, :], io["rW2"]),
                         (w.rb2[:, :], io["rb2"]), (w.rw3[:, :, :], io["rW3"]),
                         (w.rb3[:, :], io["rb3"].partition_broadcast(P))):
            sp.dma_start(dst, src).then_inc(w.router_loaded, 16)
        for dst, src in ((w.ew1[:, :, :], io["eW1"]), (w.eb1[:, :, :], io["eb1"]), (w.eb2[:, :], io["eb2"]),
                         (w.ew2[:, :, :, :], io["eW2"])):
            sp.dma_start(dst, src).then_inc(w.experts_loaded, 16)
        sp.wait_ge(w.router_loaded, w.router_count)
        sp.wait_ge(w.experts_loaded, w.experts_count)

    w.load = load
    return w


def program(nc, io, stages=(1, 2, 3, 4, 5, 6)):
    with ExitStack() as ctx:
        a = Pool_(nc, ctx, "all")
        x_sb = a.sb("x", [P, B * TT, C])
        k = constants(nc, a, io["cst"])
        load_x(nc, k, io["x"], x_sb)
        with ExitStack() as layer:
            w = layer0_weights(nc, Pool_(nc, layer, "l0"), io)
            if 1 in stages:
                routed_ffn(nc, "f1", x_sb, k, w)
                w.load = None
            if 2 in stages:
                retention(nc, "r2", x_sb, k, io)
            if 3 in stages:
                routed_ffn(nc, "f3", x_sb, k, w)
        if 4 in stages or 5 in stages or 6 in stages:
            with ExitStack() as layer:
                w = layer1_weights(nc, Pool_(nc, layer, "l1"), io)
                if 4 in stages:
                    relative_ffn(nc, "f4", x_sb, k, w, io)
                if 5 in stages:
                    plain_attention(nc, "a5", x_sb, k, io)
                if 6 in stages:
                    relative_ffn(nc, "f6", x_sb, k, w, io)
        store_x(nc, x_sb, io["out"])



def shape_tables():
    i = np.arange(P)
    cst = np.concatenate([np.eye(P), (i[:, None] < i[None, :]).astype(float), np.tile(np.arange(CAP), (P, 1)),
                          np.tile(np.arange(E0), (P, 1)), np.tile(np.arange(E1), (P, 1))], 1)
    half = np.arange(0, HD, 2)
    freq = np.repeat(1.0 / 10000.0 ** (half / HD), 2)[None, :] * np.arange(T)[:, None]
    scale = np.repeat((half + 0.4 * HD) / (1.4 * HD), 2)[None, :] ** ((np.arange(T) - T // 2) / 512.0)[:, None]
    sign = np.tile([-1.0, 1.0], HD // 2)[None, :]
    rope = np.stack([np.cos(freq) * scale, np.sin(freq) * scale * sign, np.cos(freq) / scale,
                     np.sin(freq) / scale * sign])
    rope = np.repeat(rope.transpose(2, 0, 1), H, 0)
    gamma = 1.0 - 2.0 ** (-5.0 - np.arange(H))
    diff = np.arange(T)[None, :] - np.arange(P)[:, None]
    decay = np.where(diff[:, None, :] >= 0, gamma[None, :, None] ** np.maximum(diff, 0)[:, None, :], 0.0)
    decay = np.concatenate([decay, decay[:, :, 0:P]], 2) * HD ** -0.5
    group = np.kron(np.eye(H), np.full((HD, HD), 1.0 / HD))
    w = 1.0 / 10000.0 ** (np.arange(0, C, 2) / C)
    ang = w[:, None] * np.arange(T)[None, :]
    pe = np.concatenate([np.sin(ang), np.cos(ang)], 0)
    turn = np.stack([np.tile(np.cos(ang), (2, 1)), np.concatenate([np.sin(ang), -np.sin(ang)], 0)], 1)
    f = lambda v: np.ascontiguousarray(v, np.float32)
    return {"cst": f(cst), "rope": f(rope), "decay": f(decay), "group": f(group), "pe": f(pe), "turn": f(turn)}


def layouts(v):
    v = {n: np.asarray(a) for n, a in v.items()}
    swap = np.arange(C) ^ 1
    dh = np.arange(C).reshape(H, HD).T.reshape(-1)
    qkv0 = v["L0_attn_w_qkv"].reshape(3, C, C)
    qkv1 = v["L1_attn_w_qkv"].reshape(3, C, C)
    col = lambda a: a.reshape(-1, P).T
    out = {
        "x": v["L0_attn_x"],
        "rW1": v["L0_ffn_rW1"], "rb1": col(v["L0_ffn_rb1"]),
        "rW2": v["L0_ffn_rW2"].reshape(KH, P, HID).transpose(1, 0, 2), "rb2": col(v["L0_ffn_rb2"]),
        "rW3": v["L0_ffn_rW3"].reshape(KH, P, E0).transpose(1, 0, 2), "rb3": v["L0_ffn_rb3"],
        "eW1": v["L0_ffn_eW1"].transpose(1, 0, 2),
        "eb1": v["L0_ffn_eb1"].reshape(E0, KH, P).transpose(2, 0, 1),
        "eW2": v["L0_ffn_eW2"].reshape(E0, KH, P, C).transpose(2, 0, 1, 3), "eb2": v["L0_ffn_eb2"].T,
        "w0": np.concatenate([qkv0[0][dh].T, qkv0[0][swap][dh].T, qkv0[1][dh].T, qkv0[1][swap][dh].T, v["L0_attn_w_gated"].T,
                              qkv0[2].T], 1),
        "w0p": v["L0_attn_w_proj"].T, "gnw": col(v["L0_attn_gn_weight"]), "gnb": col(v["L0_attn_gn_bias"]),
        "w5": np.concatenate([qkv1[0][dh].T, qkv1[1][dh].T, qkv1[2].T], 1), "w5p": v["L1_attn_w_proj"].T,
        "b5p": v["L1_attn_b_proj"],
        "w4": np.concatenate([v["L1_ffn_wq"][:, dh], v["L1_ffn_wk"][:, dh], v["L1_ffn_wv"]], 1), "w4p": v["L1_ffn_wo"],
        "wp": np.stack([v["L1_ffn_wp"].T[dh], np.roll(v["L1_ffn_wp"], C // 2, 0).T[dh]], 1),
        "ln": np.stack([v["L1_ffn_ln1_g"], v["L1_ffn_ln1_b"], v["L1_ffn_ln2_g"], v["L1_ffn_ln2_b"]], 1),
        "selw": v["L1_ffn_sel_w"], "keys": v["L1_ffn_keys"].transpose(1, 0, 2),
        "values": v["L1_ffn_values"].transpose(1, 0, 2),
    }
    return out


def kernel(**inputs):
    import concourse.bacc as _bacc
    from concourse.bass_utils import run_bass_kernel_spmd as _run

    nc = _bacc.Bacc("TRN2", target_bir_lowering=False, num_devices=1)
    arrays, io = {}, {}
    for name, a in {**layouts(inputs), **shape_tables()}.items():
        arrays[f"in_{name}"] = np.ascontiguousarray(a)
        io[name] = nc.dram_tensor(f"in_{name}", a.shape, mybir.dt.from_np(a.dtype), kind="ExternalInput").ap()
    io["out"] = nc.dram_tensor("out", (B, T, C), F32, kind="ExternalOutput").ap()
    program(nc, io)
    return _run(nc, [arrays], core_ids=[0]).results[0]["out"]
```

```python
from contextlib import ExitStack

import numpy as np

import concourse.bass as bass
from concourse import mybir

F32 = mybir.dt.float32
F32R = mybir.dt.float32r
BF16 = mybir.dt.bfloat16
U32 = mybir.dt.uint32
ALU = mybir.AluOpType
ACT = mybir.ActivationFunctionType
AX = mybir.AxisListType

P = 128
B, T, C = 16, 256, 128
TT = T // P
H, HD = 16, 8
QUAD = 4
E0, HID, CAP = 8, 512, 40
KH = HID // P
E1, TOPK = 32, 4
EPS = 1e-5
SLOTS = 6
ROWS = 96
QSLOT = (0, 0, 0, 1, 1, 2)
KSLOT = (0, 1, 2, 0, 1, 0)
RUNS = ((0, 3), (3, 2), (5, 1))


class Ring:

    def __init__(self, psum, filled, emptied, per, banks):
        self.psum, self.filled, self.emptied, self.per, self.banks = psum, filled, emptied, per, banks

    def nth(self, item, k):
        return item[0] * self.per + k + 1

    def bank(self, item, k):
        return self.psum[:, (item[1] * self.per + k) % self.banks, :]

    def done(self, item, k):
        return self.nth(item, k) + self.banks


class Pool_:

    def __init__(self, nc, ctx, tag):
        self.nc, self.ctx, self.tag, self.sems = nc, ctx, tag, []
        ctx.callback(self.clear)

    def clear(self):
        if self.sems:
            self.nc.clear_and_free_semaphores(self.sems)
            self.nc.all_engine_barrier()

    def sb(self, name, shape, dt=F32):
        return self.ctx.enter_context(self.nc.sbuf_tensor(f"{self.tag}_{name}", shape, dt))

    def ps(self, name, shape, dt=F32):
        return self.ctx.enter_context(self.nc.psum_tensor(f"{self.tag}_{name}", shape, dt))

    def sem(self, name):
        self.sems.append(self.nc.alloc_semaphore(f"{self.tag}_{name}"))
        return self.sems[-1]


def steps(eng, first, last, step, lead=1, trail=1):
    s = first
    while s < first + lead or (last - trail - s + 1) % 2:
        step((s, s % 2))
        s += 1
    pairs = (last - trail - s + 1) // 2
    base = s
    with eng.Fori(0, pairs) as p:
        for q in (0, 1):
            step((p * 2 + (base + q), (base + q) % 2), inner=True)
    for s in range(base + 2 * pairs, last + 1):
        step((s, s % 2))


def is_first(s, at=0):
    return isinstance(s, int) and s == at


def within(s, first, last):
    return not isinstance(s, int) or first <= s <= last


def before(item, n=1):
    return (item[0] - n, (item[1] + n) % 2)


def after(item):
    return (item[0] + 1, (item[1] + 1) % 2)


def routed_ffn(nc, tag, x_sb, k, w):
    G, GT, NB = B // 2, 4, 2
    S = E0 * CAP
    SW, NW = 2 * CAP, E0 // 2
    W = GT * P
    x_g = x_sb[:, :, :].rearrange("p (g t) c -> p g t c", t=GT)
    with ExitStack() as ctx:
        a = Pool_(nc, ctx, tag)
        xn = a.sb("xn", [P, 2, GT, C])
        stats = a.sb("stats", [P, GT, 6])
        mv = a.sb("mv", [P, GT, 2])
        veps = a.sb("veps", [P, GT])
        rstd = a.sb("rstd", [P, GT])
        xt = a.sb("xt", [P, W])
        xt_hi, xt_lo = a.sb("xt_hi", [P, W], F32R), a.sb("xt_lo", [P, W], F32R)
        h1 = a.sb("h1", [P, KH, W])
        h1_hi, h1_lo = a.sb("h1_hi", [P, KH, W], F32R), a.sb("h1_lo", [P, KH, W], F32R)
        h2 = a.sb("h2", [P, KH, W])
        lg = a.sb("lg", [P, GT, E0])
        top = a.sb("top", [P, GT])
        ex = a.sb("ex", [P, GT, E0])
        den = a.sb("den", [P, GT])
        sc = a.sb("sc", [P, GT, E0])
        best = a.sb("best", [P, GT, 8])
        best_at = a.sb("best_at", [P, GT, 8], U32)
        best_f = a.sb("best_f", [P, GT, 2])
        eq = a.sb("eq", [P, GT, 2, E0])
        mask = a.sb("mask", [P, GT, E0], BF16)
        off = a.sb("off", [P, GT, E0])
        pos = a.sb("pos", [P, GT, E0])
        d = a.sb("d", [P, 2, GT * E0, CAP])
        g = a.sb("g", [P, 2, GT * E0, CAP])
        xd = a.sb("xd", [P, E0, NB, CAP])
        hh = w.shared[:, 0:E0 * KH * NB * CAP].rearrange("p (e j s) -> p e j s", e=E0, j=KH)
        eot = a.sb("eot", [P, NB, E0, CAP])
        eos = a.sb("eos", [ROWS, NB, NW, C])
        gts = a.sb("gts", [ROWS, GT, NW, P])

        ra = Ring(a.ps("ra", [P, 2, 512]), a.sem("ra_filled"), a.sem("ra_emptied"), 5, 2)
        rv = Ring(a.ps("rv", [P, 2, 512]), a.sem("rv_filled"), a.sem("rv_emptied"), 6, 2)
        ea = Ring(a.ps("ea", [P, 2, 512]), a.sem("ea_filled"), a.sem("ea_emptied"), 9, 2)
        ev = Ring(a.ps("ev", [P, 2, 512]), a.sem("ev_filled"), a.sem("ev_emptied"), 10, 2)
        ln_stats, ln_aggr, ln_veps, ln_rstd, xn_ready = [a.sem(n) for n in (
            "ln_stats", "ln_aggr", "ln_veps", "ln_rstd", "xn_ready")]
        top_ready, lg_ready, ex_ready, den_step, sc_ready, best_step, bestf, mask_step, off_ready, d_ready, g_ready, padded, xt_ready, h1_ready = [
            a.sem(n) for n in ("top_ready", "lg_ready", "ex_ready", "den_step", "sc_ready", "best_step", "bestf",
                               "mask_step", "off_ready", "d_ready", "g_ready", "padded",
                               "xt_ready", "h1_ready")]
        block = ctx.enter_context(nc.Block())

        @block.sync
        def _(sp):
            if w.load is not None:
                w.load(sp)
                w.load_positions(sp)

        ROUTE_H1 = ((ra, 1), (rv, 0), (ra, 2), (rv, 1))
        ROUTE_H2 = ((ra, 3), (rv, 2), (ra, 4), (rv, 3))

        @block.tensor
        def _(pe):
            def turn_x(it):
                pe.wait_ge(ra.emptied, ra.nth(it, 0))
                pe.wait_ge(xn_ready, it[0] * GT + GT)
                for t in range(GT):
                    mm = nc.tensor.transpose(ra.bank(it, 0)[:, t * P:(t + 1) * P], xn[:, it[1], t, :], k.ident)
                mm.then_inc(ra.filled, 1)

            def split_product(out, pairs):
                for j, ((w_hi, w_lo), (v_hi, v_lo)) in enumerate(pairs):
                    nc.tensor.matmul(out, w_hi, v_hi, start=(j == 0), stop=False)
                    nc.tensor.matmul(out, w_hi, v_lo, start=False, stop=False)
                    mm = nc.tensor.matmul(out, w_lo, v_hi, start=False, stop=(j == len(pairs) - 1))
                return mm

            def layer1(it, m):
                ring, n = ROUTE_H1[m]
                if m == 0:
                    pe.wait_ge(xt_ready, it[0] + 1)
                    if is_first(it[0]):
                        pe.wait_ge(w.router_lo_ready, 2)
                pe.wait_ge(ring.emptied, ring.nth(it, n))
                chunk = slice(m * P, (m + 1) * P)
                split_product(ring.bank(it, n), [((w.rw1_hi[:, chunk], w.rw1_lo[:, chunk]),
                                                  (xt_hi[:, :], xt_lo[:, :]))]).then_inc(ring.filled, 1)

            def layer2(it, m):
                ring, n = ROUTE_H2[m]
                if m == 0:
                    pe.wait_ge(h1_ready, it[0] * KH + KH)
                pe.wait_ge(ring.emptied, ring.nth(it, n))
                chunk = slice(m * P, (m + 1) * P)
                split_product(ring.bank(it, n), [((w.rw2_hi[:, j, chunk], w.rw2_lo[:, j, chunk]),
                                                  (h1_hi[:, j, :], h1_lo[:, j, :])) for j in range(KH)])\
                    .then_inc(ring.filled, 1)

            def logits(it, t):
                if t == 0:
                    pe.wait_ge(rv.emptied, rv.nth(it, 4))
                    pe.wait_ge(ra.emptied, ra.done(it, 4))
                    pe.wait_ge(rv.emptied, rv.done(it, 3))
                for j in range(KH):
                    mm = nc.tensor.matmul(rv.bank(it, 4)[:, t * E0:(t + 1) * E0],
                                          h2[:, j, t * P:(t + 1) * P], w.rw3[:, j, :],
                                          start=(j == 0), stop=(j == KH - 1))
                if t == GT - 1:
                    mm.then_inc(rv.filled, 1)

            def count(it):
                pe.wait_ge(rv.emptied, rv.nth(it, 5))
                pe.wait_ge(mask_step, it[0] + 1)
                for t in range(GT):
                    out = rv.bank(it, 5)[:, t * E0:(t + 1) * E0]
                    if t % TT:
                        nc.tensor.matmul(out, k.ones_bf, mask[:, t - 1, :], start=True, stop=False)
                    mm = nc.tensor.matmul(out, k.tri_bf, mask[:, t, :], start=(t % TT == 0), stop=True)
                mm.then_inc(rv.filled, 1)

            def slots(it):
                pe.wait_ge(d_ready, it[0] + 1)
                for b, ring in enumerate((ea, ev)):
                    pe.wait_ge(ring.emptied, ring.nth(it, 0))
                    for t in range(TT):
                        u = b * TT + t
                        mm = nc.tensor.matmul(ring.bank(it, 0)[:, 0:S], xn[:, it[1], u, :],
                                              d[:, it[1], u * E0:(u + 1) * E0, :],
                                              start=(t == 0), stop=(t == TT - 1))
                    mm.then_inc(ring.filled, 1)

            def hidden(it, e):
                ring, n = (ea, ev)[e % 2], 1 + e // 2
                if e == 0:
                    pe.wait_ge(ea.emptied, ea.done(it, 0))
                    pe.wait_ge(ev.emptied, ev.done(it, 0))
                pe.wait_ge(ring.emptied, ring.nth(it, n))
                for j in range(KH):
                    mm = nc.tensor.matmul(ring.bank(it, n)[:, j * SW:(j + 1) * SW],
                                          w.ew1[:, e, j * P:(j + 1) * P], xd[:, e, :, :],
                                          start=True, stop=True)
                mm.then_inc(ring.filled, 1)

            def output(it, e):
                ring = (ea, ev)[e // 4]
                if e % 4 == 0:
                    pe.wait_ge(ring.emptied, ring.nth(it, 5))
                source, n = (ea, ev)[e % 2], 1 + e // 2
                pe.wait_ge(source.emptied, source.done(it, n))
                for j in range(KH):
                    mm = nc.tensor.matmul(ring.bank(it, 5)[:, (e % 4) * P:(e % 4) * P + SW],
                                          w.ew2[:, e, j, :], hh[:, e, j, :],
                                          start=(j == 0), stop=(j == KH - 1))
                if e % 4 == 3:
                    mm.then_inc(ring.filled, 1)

            def turn_slots(it):
                pe.wait_ge(ea.emptied, ea.done(it, 5))
                pe.wait_ge(ev.emptied, ev.done(it, 5))
                for b, ring in enumerate((ea, ev)):
                    pe.wait_ge(ring.emptied, ring.nth(it, 6))
                    for v in range(NW):
                        mm = nc.tensor.transpose(ring.bank(it, 6)[0:SW, v * P:(v + 1) * P],
                                                 eot[:, b, 2 * v:2 * v + 2, :], k.ident)
                    mm.then_inc(ring.filled, 1)

            def turn_weights(it):
                pe.wait_ge(g_ready, it[0] + 1)
                for t in range(GT):
                    ring, n = (ea, ev)[t % 2], 7 + t // 2
                    pe.wait_ge(ring.emptied, ring.nth(it, n))
                    for v in range(NW):
                        mm = nc.tensor.transpose(ring.bank(it, n)[0:SW, v * P:(v + 1) * P],
                                                 g[:, it[1], t * E0 + 2 * v:t * E0 + 2 * v + 2, :], k.ident)
                    mm.then_inc(ring.filled, 1)

            def back(it):
                pe.wait_ge(ev.emptied, ev.nth(it, 9))
                pe.wait_ge(ea.emptied, ea.done(it, 8))
                pe.wait_ge(ev.emptied, ev.done(it, 8))
                for t in range(GT):
                    for v in range(NW):
                        mm = nc.tensor.matmul(ev.bank(it, 9)[:, t * P:(t + 1) * P], gts[:, t, v, :],
                                              eos[:, t // TT, v, :], start=(v == 0), stop=(v == NW - 1))
                mm.then_inc(ev.filled, 1)

            def step(it, inner=False):
                r = it if within(it[0], 0, G - 1) else None
                e = before(it) if within(it[0], 1, G) else None
                if is_first(it[0]):
                    turn_x(it)
                if e:
                    count(e)
                if r:
                    for m in range(KH):
                        layer1(r, m)
                if e:
                    slots(e)
                for m in range(KH):
                    for n in ((0, 1, 2, 3), (4, 5), (6, 7), ())[m]:
                        if e:
                            hidden(e, n)
                    if m == 3 and e:
                        output(e, 0)
                        output(e, 1)
                    if r:
                        layer2(r, m)
                if e:
                    output(e, 2)
                    output(e, 3)
                for t in range(GT):
                    if e:
                        output(e, 4 + t)
                    if r:
                        logits(r, t)
                if within(it[0], 0, G - 2):
                    turn_x(after(it))
                if e:
                    turn_slots(e)
                    turn_weights(e)
                    back(e)
                if is_first(it[0]):
                    pe.wait_ge(w.experts_loaded, w.experts_count)

            pe.wait_ge(k.loaded, k.loaded_count)
            steps(pe, 0, G, step, lead=1, trail=2)

        @block.scalar
        def _(act):
            act.sem_inc(ra.emptied, ra.banks)
            act.sem_inc(ea.emptied, ea.banks)

            def route_hidden(it, n):
                out, bias = ((h1, w.rb1), (h2, w.rb2))[n // 2]
                m = 2 * (n % 2)
                act.wait_ge(ra.filled, ra.nth(it, 1 + n))
                if n < 2:
                    nc.scalar.activation(h1_hi[:, m, :], ra.bank(it, 1 + n), ACT.Relu, bias=bias[:, m:m + 1])
                nc.scalar.activation(out[:, m, :], ra.bank(it, 1 + n), ACT.Relu,
                                     bias=bias[:, m:m + 1]).then_inc(ra.emptied, 1)

            def take_x(it):
                act.wait_ge(ra.filled, ra.nth(it, 0))
                nc.scalar.activation(xt_hi[:, :], ra.bank(it, 0), ACT.Copy)
                nc.scalar.activation(xt[:, :], ra.bank(it, 0), ACT.Copy).then_inc(ra.emptied, 1)

            def hidden(it, e):
                act.wait_ge(ea.filled, ea.nth(it, 1 + e // 2))
                for j in range(KH):
                    last = nc.scalar.activation(hh[:, e, j, :], ea.bank(it, 1 + e // 2)[:, j * SW:(j + 1) * SW],
                                                ACT.Relu, bias=w.eb1[:, e, j:j + 1])
                last.then_inc(ea.emptied, 1)

            def step(it, inner=False):
                r = it if within(it[0], 0, G - 1) else None
                e = before(it) if within(it[0], 1, G) else None
                if is_first(it[0]):
                    take_x(it)
                if r:
                    route_hidden(r, 0)
                    route_hidden(r, 1)
                if e:
                    act.wait_ge(ea.filled, ea.nth(e, 0))
                    nc.scalar.activation(xd[:, :, 0, :], ea.bank(e, 0)[:, 0:S].rearrange("p (e s) -> p e s", e=E0),
                                         ACT.Copy).then_inc(ea.emptied, 1)
                    hidden(e, 0)
                    hidden(e, 2)
                if r:
                    route_hidden(r, 2)
                if e:
                    hidden(e, 4)
                    hidden(e, 6)
                if r:
                    route_hidden(r, 3)
                if e:
                    act.wait_ge(ea.filled, ea.nth(e, 5))
                    for n in range(4):
                        last = nc.scalar.activation(eot[:, :, n, :], ea.bank(e, 5)[:, n * P:n * P + SW]
                                                    .rearrange("p (b s) -> p b s", b=NB), ACT.Identity,
                                                    bias=w.eb2[:, n:n + 1])
                    last.then_inc(ea.emptied, 1)
                if r and e:
                    softmax_exp(r)
                if within(it[0], 0, G - 2):
                    take_x(after(it))
                if e:
                    act.wait_ge(ea.filled, ea.nth(e, 6))
                    nc.scalar.activation(eos[0:SW, 0, :, :].rearrange("p v c -> p (v c)"), ea.bank(e, 6)[0:SW, :],
                                         ACT.Copy).then_inc(ea.emptied, 1)
                    for t in (0, 2):
                        act.wait_ge(ea.filled, ea.nth(e, 7 + t // 2))
                        nc.scalar.activation(gts[0:SW, t, :, :].rearrange("p v c -> p (v c)"),
                                             ea.bank(e, 7 + t // 2)[0:SW, :], ACT.Copy).then_inc(ea.emptied, 1)
                if r and not e:
                    softmax_exp(r)
                if is_first(it[0]):
                    act.wait_ge(padded, 2)
                    act.wait_ge(w.experts_loaded, w.experts_count)

            def softmax_exp(it):
                act.wait_ge(lg_ready, it[0] + 1)
                nc.scalar.activation(ex[:, :, :], lg[:, :, :], ACT.Exp).then_inc(ex_ready, 1)

            act.wait_ge(w.router_loaded, w.router_count)
            if w.load is not None:
                for hi, full in ((w.rw1_hi[:, :], w.rw1[:, :]), (w.rw2_hi[:, :, :], w.rw2[:, :, :])):
                    nc.scalar.activation(hi, full, ACT.Copy).then_inc(w.router_hi_ready, 1)
            steps(act, 0, G, step, lead=1, trail=2)

        @block.vector
        def _(dve):
            dve.sem_inc(rv.emptied, rv.banks)
            dve.sem_inc(ev.emptied, ev.banks)

            def ln_measure(it):
                i = it[0]
                for t in range(GT):
                    nc.vector.bn_stats(stats[:, t, :], x_g[:, i, t, :]).then_inc(ln_stats, 1)
                dve.wait_ge(ln_stats, i * GT + GT)
                nc.vector.memset(k.idle, 0.0)
                for t in range(GT):
                    last = nc.vector.bn_aggr(mv[:, t, :], stats[:, t, :])
                last.then_inc(ln_aggr, 1)

            def ln_apply(it):
                i = it[0]
                dve.wait_ge(ln_rstd, i + 1)
                for t in range(GT):
                    nc.vector.tensor_scalar(xn[:, it[1], t, :], x_g[:, i, t, :], mv[:, t, 0:1], rstd[:, t:t + 1],
                                            ALU.subtract, ALU.mult).then_inc(xn_ready, 1)

            def route_hidden(it, n):
                out, bias = ((h1, w.rb1), (h2, w.rb2))[n // 2]
                m = 1 + 2 * (n % 2)
                dve.wait_ge(rv.filled, rv.nth(it, n))
                if n < 2:
                    nc.vector.tensor_scalar(h1_hi[:, m, :], rv.bank(it, n), bias[:, m:m + 1], 0.0, ALU.add, ALU.max)
                nc.vector.tensor_scalar(out[:, m, :], rv.bank(it, n), bias[:, m:m + 1], 0.0,
                                        ALU.add, ALU.max).then_inc(rv.emptied, 1)

            def softmax_shift(it):
                i = it[0]
                dve.wait_ge(rv.filled, rv.nth(it, 4))
                nc.vector.tensor_tensor(lg[:, :, :], rv.bank(it, 4)[:, 0:GT * E0].rearrange("p (t e) -> p t e", t=GT),
                                        w.rb3[:, :].unsqueeze(1).to_broadcast([P, GT, E0]),
                                        ALU.add).then_inc(rv.emptied, 1)
                dve.wait_ge(rv.emptied, rv.done(it, 4))
                nc.vector.tensor_reduce(top[:, :], lg[:, :, :], AX.X, ALU.max).then_inc(top_ready, 1)
                dve.wait_ge(top_ready, i + 1)
                nc.vector.tensor_tensor(lg[:, :, :], lg[:, :, :], top[:, :].unsqueeze(2).to_broadcast([P, GT, E0]),
                                        ALU.subtract).then_inc(lg_ready, 1)

            def softmax_divide(it):
                i = it[0]
                dve.wait_ge(ex_ready, i + 1)
                nc.vector.tensor_reduce(den[:, :], ex[:, :, :], AX.X, ALU.add).then_inc(den_step, 1)
                dve.wait_ge(den_step, i * 2 + 1)
                nc.vector.reciprocal(den[:, :], den[:, :]).then_inc(den_step, 1)
                if not is_first(i):
                    dve.wait_ge(g_ready, i)
                dve.wait_ge(den_step, i * 2 + 2)
                nc.vector.tensor_tensor(sc[:, :, :], ex[:, :, :], den[:, :].unsqueeze(2).to_broadcast([P, GT, E0]),
                                        ALU.mult).then_inc(sc_ready, 1)

            def pick(it):
                i = it[0]
                dve.wait_ge(sc_ready, i + 1)
                nc.vector.memset(k.idle, 0.0)
                for t in range(GT):
                    last = nc.vector.max(best[:, t, :], sc[:, t, :])
                last.then_inc(best_step, 1)
                dve.wait_ge(best_step, i * 2 + 1)
                nc.vector.memset(k.idle, 0.0)
                for t in range(GT):
                    last = nc.vector.max_index(best_at[:, t, :], best[:, t, :], sc[:, t, :])
                last.then_inc(best_step, 1)
                dve.wait_ge(best_step, i * 2 + 2)
                nc.vector.tensor_copy(best_f[:, :, :], best_at[:, :, 0:2]).then_inc(bestf, 1)

            def mark(it):
                i = it[0]
                dve.wait_ge(bestf, i * 2 + 1)
                for n in range(2):
                    last = nc.vector.tensor_tensor(eq[:, :, n, :], k.iota8.unsqueeze(1).to_broadcast([P, GT, E0]),
                                                   best_f[:, :, n:n + 1].to_broadcast([P, GT, E0]), ALU.is_equal)
                last.then_inc(bestf, 1)
                dve.wait_ge(bestf, i * 2 + 2)
                nc.vector.tensor_tensor(mask[:, :, :], eq[:, :, 0, :], eq[:, :, 1, :], ALU.add).then_inc(mask_step, 1)
                dve.wait_ge(mask_step, i + 1)
                nc.vector.tensor_scalar(off[:, :, :], mask[:, :, :], -1000.0, 1000.0, ALU.mult, ALU.add)\
                    .then_inc(off_ready, 1)

            def place(it):
                i = it[0]
                dve.wait_ge(off_ready, i + 1)
                dve.wait_ge(rv.filled, rv.nth(it, 5))
                nc.vector.tensor_tensor(pos[:, :, :], rv.bank(it, 5)[:, 0:GT * E0].rearrange("p (t e) -> p t e", t=GT),
                                        off[:, :, :], ALU.add).then_inc(rv.emptied, 1)
                dve.wait_ge(rv.emptied, rv.done(it, 5))
                nc.vector.tensor_tensor(d[:, it[1], :, :], k.iota40.unsqueeze(1).to_broadcast([P, GT * E0, CAP]),
                                        pos[:, :, :].rearrange("p t e -> p (t e)").unsqueeze(2)
                                        .to_broadcast([P, GT * E0, CAP]), ALU.is_equal).then_inc(d_ready, 1)

            def hidden(it, e):
                dve.wait_ge(ev.filled, ev.nth(it, 1 + e // 2))
                for j in range(KH):
                    last = nc.vector.tensor_scalar(hh[:, e, j, :], ev.bank(it, 1 + e // 2)[:, j * SW:(j + 1) * SW],
                                                   w.eb1[:, e, j:j + 1], 0.0, ALU.add, ALU.max)
                last.then_inc(ev.emptied, 1)

            def slots(it):
                dve.wait_ge(ev.filled, ev.nth(it, 0))
                nc.vector.tensor_copy(xd[:, :, 1, :], ev.bank(it, 0)[:, 0:S].rearrange("p (e s) -> p e s", e=E0))\
                    .then_inc(ev.emptied, 1)

            def experts_last(it):
                dve.wait_ge(ev.filled, ev.nth(it, 5))
                for e in range(4, E0):
                    last = nc.vector.tensor_scalar(eot[:, :, e, :], ev.bank(it, 5)[:, (e - 4) * P:(e - 4) * P + SW]
                                                   .rearrange("p (b s) -> p b s", b=NB), w.eb2[:, e:e + 1], None,
                                                   ALU.add)
                last.then_inc(ev.emptied, 1)

            def turned(it, n):
                dve.wait_ge(ev.filled, ev.nth(it, 6 + n))
                out = (eos[0:SW, 1], gts[0:SW, 1], gts[0:SW, 3])[n]
                nc.vector.tensor_copy(out.rearrange("p v c -> p (v c)"), ev.bank(it, 6 + n)[0:SW, :])\
                    .then_inc(ev.emptied, 1)

            def residual(it):
                dve.wait_ge(ev.filled, ev.nth(it, 9))
                xs = x_g[:, it[0], :, :].rearrange("p t c -> p (t c)")
                nc.vector.scalar_tensor_tensor(xs, ev.bank(it, 9), 0.5, xs, ALU.mult, ALU.add)\
                    .then_inc(ev.emptied, 1)

            def step(it, inner=False):
                r = it if within(it[0], 0, G - 1) else None
                e = before(it) if within(it[0], 1, G) else None
                following = after(it) if within(it[0], 0, G - 2) else None
                if is_first(it[0]):
                    ln_measure(it)
                    ln_apply(it)
                    nc.vector.memset(eos[64:ROWS, :, :, :].rearrange("p b v c -> p (b v c)"), 0.0).then_inc(padded, 1)
                    nc.vector.memset(gts[64:ROWS, :, :, :].rearrange("p t v c -> p (t v c)"), 0.0).then_inc(padded, 1)
                    dve.wait_ge(w.router_loaded, w.router_count)
                    if w.load is not None:
                        for n, (lo, full, hi) in enumerate(((w.rw1_lo[:, :], w.rw1[:, :], w.rw1_hi[:, :]),
                                                            (w.rw2_lo[:, :, :], w.rw2[:, :, :], w.rw2_hi[:, :, :]))):
                            dve.wait_ge(w.router_hi_ready, n + 1)
                            nc.vector.tensor_tensor(lo, full, hi, ALU.subtract).then_inc(w.router_lo_ready, 1)
                if e:
                    place(e)
                if r:
                    route_hidden(r, 0)
                    route_hidden(r, 1)
                if e:
                    slots(e)
                if e:
                    hidden(e, 1)
                    hidden(e, 3)
                if following:
                    ln_measure(following)
                if e:
                    hidden(e, 5)
                if r:
                    route_hidden(r, 2)
                if e:
                    hidden(e, 7)
                if following:
                    ln_apply(following)
                if r:
                    route_hidden(r, 3)
                if e:
                    experts_last(e)
                if r:
                    softmax_shift(r)
                if e:
                    turned(e, 0)
                if r:
                    softmax_divide(r)
                if e:
                    turned(e, 1)
                if r:
                    pick(r)
                if e:
                    turned(e, 2)
                if r:
                    mark(r)
                if e:
                    residual(e)
                if is_first(it[0]):
                    dve.wait_ge(w.experts_loaded, w.experts_count)
                    if w.load is not None:
                        w.split_positions(dve)

            dve.wait_ge(k.loaded, k.loaded_count)
            steps(dve, 0, G, step, lead=1, trail=2)

        @block.gpsimd
        def _(pool):
            def ln_root(it):
                pool.wait_ge(ln_aggr, it[0] + 1)
                nc.gpsimd.tensor_tensor(veps[:, :], mv[:, :, 1], k.eps[:, 0:GT], ALU.add).then_inc(ln_veps, 1)
                pool.wait_ge(ln_veps, it[0] + 1)
                nc.gpsimd.tensor_tensor(rstd[:, :], veps[:, :], k.minus_half[:, 0:GT], ALU.pow).then_inc(ln_rstd, 1)

            def weigh(it):
                pool.wait_ge(d_ready, it[0] + 1)
                nc.gpsimd.tensor_tensor(g[:, it[1], :, :], d[:, it[1], :, :],
                                        sc[:, :, :].rearrange("p t e -> p (t e)").unsqueeze(2)
                                        .to_broadcast([P, GT * E0, CAP]), ALU.mult).then_inc(g_ready, 1)

            def rest_of_x(it):
                pool.wait_ge(ra.emptied, ra.done(it, 0))
                nc.gpsimd.tensor_tensor(xt_lo[:, :], xt[:, :], xt_hi[:, :], ALU.subtract).then_inc(xt_ready, 1)

            def rest_of_h1(it, m):
                ring, n = ROUTE_H1[m]
                pool.wait_ge(ring.emptied, ring.done(it, n))
                nc.gpsimd.tensor_tensor(h1_lo[:, m, :], h1[:, m, :], h1_hi[:, m, :], ALU.subtract)\
                    .then_inc(h1_ready, 1)

            def step(it, inner=False):
                s = it[0]
                if is_first(s):
                    ln_root(it)
                    rest_of_x(it)
                if within(s, 0, G - 1):
                    rest_of_h1(it, 0)
                if within(s, 1, G):
                    weigh(before(it))
                if within(s, 0, G - 1):
                    for m in range(1, KH):
                        rest_of_h1(it, m)
                if within(s, 0, G - 2):
                    ln_root(after(it))
                    rest_of_x(after(it))

            pool.wait_ge(k.loaded, k.loaded_count)
            steps(pool, 0, G, step, lead=1, trail=2)


class Desk:

    def __init__(self, psum, filled, emptied, fills, banks):
        self.psum, self.filled, self.emptied, self.banks = psum, filled, emptied, banks
        self.fills = fills

    def _place(self, it, name):
        s, par = it
        present = [n for n, first in self.fills if within(s, first, first + B - 1)]
        if isinstance(s, int):
            n = sum(1 for u in range(s) for _, first in self.fills if within(u, first, first + B - 1))
            return n + present.index(name), n + present.index(name)
        all_, late = len(self.fills), sum(first for _, first in self.fills)
        at = present.index(name)
        return s * all_ - late + at, (par + 4) * all_ - late + at

    def nth(self, it, name):
        return self._place(it, name)[0] + 1

    def bank(self, it, name):
        return self.psum[:, self._place(it, name)[1] % self.banks, :]

    def done(self, it, name):
        return self.nth(it, name) + self.banks


class Pipeline:
    LAST = B + 2

    @staticmethod
    def start(it):
        return it if within(it[0], 0, B - 1) else None

    @staticmethod
    def prepare(it):
        return before(it) if within(it[0], 1, B) else None

    @staticmethod
    def attend(it):
        return before(it, 2) if within(it[0], 2, B + 1) else None

    @staticmethod
    def finish(it):
        return before(it, 3) if within(it[0], 3, B + 2) else None

    @staticmethod
    def run(eng, step):
        steps(eng, 0, Pipeline.LAST, step, lead=3, trail=3)


def heads_of(v):
    def at(vm, par, t):
        whole = vm[:, par, t, :, :]
        return bass.AP(whole.tensor, whole.offset, [list(whole.ap[0]), [C + HD, QUAD], [QUAD * HD, H // QUAD], [1, HD]])
    return at(*v)


STACKED = 16 * 2 * len(RUNS)


def slots_of(part, run, each, n):
    return bass.AP(part.tensor, part.offset, [[each, run], [H * n, HD], [1, H * n]])


def stack_parts(sp, parts, scratch, qs, ks, parts_ready, bounced, stacked, passed, sr):
    def step(it, inner=False):
        i, par = it
        if not is_first(i):
            sp.wait_ge(stacked, i * STACKED)
            sp.sem_inc(passed, 1)
        sp.wait_ge(parts_ready, i + 1)
        sp.dma_start(scratch[par].rearrange("n c t -> c n t"), parts[:, par, :, :, :].rearrange("c n u t -> c (n u) t"))\
            .then_inc(bounced, 16)
        if not is_first(i) and not is_first(i, 1):
            sp.wait_ge(sr.filled, (i - 1) * H)
            sp.sem_inc(passed, 1)
        sp.wait_ge(bounced, i * 16 + 16)
        for first, run in RUNS:
            for dst, which, part, each in ((qs, 0, QSLOT[first], 0), (ks, 1, 0, 2 * P * T)):
                slots = slots_of(scratch[par, 2 * part + which], run, each, T)
                sp.dma_start(dst[first * HD:(first + run) * HD, par, :, :].rearrange("s h t -> s (h t)"), slots)\
                    .then_inc(stacked, 16)

    steps(sp, 0, B - 1, step, lead=2, trail=2)
    sp.wait_ge(stacked, B * STACKED)


def retention(nc, tag, x_sb, k, io):
    x_b = x_sb[:, :, :].rearrange("p (b t) c -> p b t c", t=TT)
    AB, DECAYED = 4, 8
    LAG = 3
    with ExitStack() as ctx:
        a = Pool_(nc, ctx, tag)
        w0, wp = a.sb("w0", [P, 6, C]), a.sb("wp", [P, C])
        rope, decay, group = a.sb("rope", [P, 4, T]), a.sb("decay", [P, H, T + P]), a.sb("group", [P, P])
        gnw, gnb = a.sb("gnw", [P, 1]), a.sb("gnb", [P, 1])
        stats, mv = a.sb("stats", [P, TT, 6]), a.sb("mv", [P, TT, 2])
        veps, rstd = a.sb("veps", [P, TT]), a.sb("rstd", [P, TT])
        xn = a.sb("xn", [P, TT, C])
        xt = a.sb("xt", [P, T])
        qp, kp = a.sb("qp", [P, 2, T]), a.sb("kp", [P, 2, T])
        qk, rest = a.sb("qk", [P, 2, T]), a.sb("rest", [P, 2, T])
        parts = a.sb("parts", [P, 2, 3, 2, T], BF16)
        qs, ks = k.qs, k.ks
        scratch = nc.dram_tensor(f"{tag}_scratch", (2, 6, P, T), BF16, kind="Internal").ap()
        vm = a.sb("vm", [P, 2, TT, QUAD, C])
        one = a.sb("one", [P, 1])
        gate, eg = a.sb("gate", [P, T]), a.sb("eg", [P, T])
        silu = a.sb("silu", [P, 2, T])
        att = a.sb("att", [P, DECAYED, T + P])
        ystats, ymv = a.sb("ystats", [P, 6]), a.sb("ymv", [P, 2])
        mean, dmean, qv, var = [a.sb(n, [P, 1]) for n in ("mean", "dmean", "qv", "var")]
        veps_y, rstd_y, ga, nb = [a.sb(n, [P, 1]) for n in ("veps_y", "rstd_y", "ga", "nb")]
        yn = a.sb("yn", [P, T])
        gated = a.sb("gated", [P, T])
        ob = a.sb("ob", [P, TT, C])

        y_ps = a.ps("y", [P, 2, 512])
        desk = Desk(a.ps("desk", [P, 2, 512]), a.sem("desk_filled"), a.sem("desk_emptied"),
                    [("v", 1), ("gm", 3), ("g", 1), ("gv", 3), ("o", 3), ("xt", 0), ("q", 0), ("k", 0)], 2)
        sr = Ring(a.ps("sr", [P, AB, 512]), a.sem("sr_filled"), a.sem("sr_emptied"), H, AB)
        (loaded, vm_zero, ln_stats, ln_aggr, ln_veps, ln_rstd, xn_ready, qp_turned, kp_turned, qk_ready, part1, rest1,
         part2, parts_ready, bounced, stacked, eg1, eg2, one_ready, silu_ready, av_done, y_stats, y_aggr, dm_ready, qv_ready,
         y_veps, y_rstd, ga_ready, nb_ready, yn_ready, gated_ready, x_done, passed, decay_loaded) = [a.sem(n) for n in (
             "loaded", "vm_zero", "ln_stats", "ln_aggr", "ln_veps", "ln_rstd", "xn_ready", "qp_turned", "kp_turned",
             "qk_ready", "part1", "rest1", "part2", "parts_ready", "bounced", "stacked", "eg1", "eg2", "one_ready", "silu_ready",
             "av_done", "y_stats", "y_aggr", "dm_ready", "qv_ready", "y_veps", "y_rstd", "ga_ready", "nb_ready",
             "yn_ready", "gated_ready", "x_done", "passed",
             "decay_loaded")]
        LOADS = 16 * 6
        block = ctx.enter_context(nc.Block())

        @block.sync
        def _(sp):
            for dst, src in ((w0[:, :, :], io["w0"].rearrange("p (n c) -> p n c", c=C)), (rope[:, :, :], io["rope"]),
                             (group[:, :], io["group"]), (gnw[:, :], io["gnw"]),
                             (gnb[:, :], io["gnb"]), (wp[:, :], io["w0p"])):
                sp.dma_start(dst, src).then_inc(loaded, 16)
            sp.dma_start(decay[:, :, :], io["decay"]).then_inc(decay_loaded, 16)
            stack_parts(sp, parts, scratch, qs, ks, parts_ready, bounced, stacked, passed, sr)

        @block.tensor
        def _(pe):
            def fill(it, name):
                pe.wait_ge(desk.emptied, desk.nth(it, name))
                return desk.bank(it, name)

            def attend_scores(it, n):
                h = (n % QUAD) * QUAD + n // QUAD
                pe.wait_ge(sr.emptied, sr.nth(it, n))
                out = sr.bank(it, n)
                nc.tensor.matmul(out[:, 0:T], ks[:, it[1], h, 0:P], qs[:, it[1], h, :], start=True, stop=True)
                nc.tensor.matmul(out[:, T:T + P], ks[:, it[1], h, P:T], qs[:, it[1], h, P:T], start=True,
                                 stop=True).then_inc(sr.filled, 1)

            def attend_values(it, n):
                r, j = n // QUAD, n % QUAD
                q = slice(j * QUAD * HD, (j + 1) * QUAD * HD)
                pe.wait_ge(sr.emptied, sr.done(it, n))
                nc.tensor.matmul(y_ps[q, it[1], 0:T], vm[:, it[1], 0, r, q], att[:, n % DECAYED, 0:T],
                                 start=(r == 0), stop=False, skip_group_check=True)
                nc.tensor.matmul(y_ps[q, it[1], P:T], vm[:, it[1], 1, r, q], att[:, n % DECAYED, T:T + P],
                                 start=False, stop=(r == QUAD - 1), skip_group_check=True).then_inc(av_done, 1)

            def small(it, n):
                new, prep, end = Pipeline.start(it), Pipeline.prepare(it), Pipeline.finish(it)
                if n == 5 and end:
                    pe.wait_ge(y_aggr, end[0] + 1)
                    nc.tensor.matmul(fill(it, "gm")[:, 0:1], group[:, :], ymv[:, 0:1], start=True, stop=True)\
                        .then_inc(desk.filled, 1)
                if n == 4 and prep:
                    out = fill(it, "v")
                    for t in range(TT):
                        mm = nc.tensor.matmul(out[:, t * P:(t + 1) * P], xt[:, t * P:(t + 1) * P], w0[:, 5, :],
                                              start=True, stop=True)
                    mm.then_inc(desk.filled, 1)
                if n == 8 and end:
                    pe.wait_ge(qv_ready, end[0] + 1)
                    nc.tensor.matmul(fill(it, "gv")[:, 0:1], group[:, :], qv[:, :], start=True, stop=True)\
                        .then_inc(desk.filled, 1)
                if n == 7 and prep:
                    nc.tensor.matmul(fill(it, "g")[:, 0:T], w0[:, 4, :], xt[:, :], start=True, stop=True)\
                        .then_inc(desk.filled, 1)
                if n == 12 and end:
                    out = fill(it, "o")
                    pe.wait_ge(gated_ready, end[0] + 1)
                    for t in range(TT):
                        mm = nc.tensor.matmul(out[:, t * P:(t + 1) * P], gated[:, t * P:(t + 1) * P], wp[:, :],
                                              start=True, stop=True)
                    mm.then_inc(desk.filled, 1)
                if n == 13 and new:
                    pe.wait_ge(xn_ready, new[0] * TT + TT)
                    out = fill(it, "xt")
                    for t in range(TT):
                        mm = nc.tensor.transpose(out[:, t * P:(t + 1) * P], xn[:, t, :], k.ident)
                    mm.then_inc(desk.filled, 1)
                if n in (14, 15) and new:
                    if is_first(new[0]):
                        pe.wait_ge(loaded, LOADS)
                    pe.wait_ge(desk.emptied, desk.done(it, "xt"))
                    out = fill(it, "qk"[n - 14])
                    for u in range(2):
                        mm = nc.tensor.matmul(out[:, u * T:(u + 1) * T], w0[:, 2 * (n - 14) + u, :], xt[:, :],
                                              start=True, stop=True)
                    mm.then_inc(desk.filled, 1)

            def step(it, inner=False):
                b, end = Pipeline.attend(it), Pipeline.finish(it)
                if b:
                    if is_first(b[0]):
                        pe.wait_ge(vm_zero, 1)
                    pe.wait_ge(stacked, b[0] * STACKED + STACKED)
                    if not is_first(b[0]) and not is_first(b[0], 1):
                        pe.wait_ge(yn_ready, b[0] - 1)
                for n in range(H):
                    small(it, n)
                    if b:
                        attend_scores(b, n)
                    if n >= LAG and b:
                        attend_values(b, n - LAG)
                    if n < LAG and end:
                        attend_values(end, H + n - LAG)

            pe.wait_ge(k.loaded, k.loaded_count)
            Pipeline.run(pe, step)

        @block.scalar
        def _(act):
            act.sem_inc(desk.emptied, 2)

            def taken(it, name):
                act.wait_ge(desk.filled, desk.nth(it, name))
                return desk.bank(it, name)

            def step(it, inner=False):
                new, prep, end = Pipeline.start(it), Pipeline.prepare(it), Pipeline.finish(it)
                if prep:
                    bank = taken(it, "v")
                    if is_first(prep[0]):
                        act.wait_ge(vm_zero, 1)
                    for t in range(TT):
                        last = nc.scalar.activation(
                            heads_of((vm, prep[1], t)),
                            bank[:, t * P:(t + 1) * P].rearrange("p (j r d) -> p r j d", r=QUAD, d=HD), ACT.Copy)
                    last.then_inc(desk.emptied, 1)
                if end:
                    bank = taken(it, "gm")
                    nc.scalar.activation(mean[:, :], bank[:, 0:1], ACT.Copy).then_inc(desk.emptied, 1)
                if end:
                    bank = taken(it, "gv")
                    nc.scalar.activation(var[:, :], bank[:, 0:1], ACT.Copy).then_inc(desk.emptied, 1)
                if prep:
                    bank = taken(it, "g")
                    if not is_first(prep[0]):
                        act.wait_ge(silu_ready, prep[0])
                    nc.scalar.activation(gate[:, :], bank[:, 0:T], ACT.Copy)
                    nc.scalar.activation(eg[:, :], bank[:, 0:T], ACT.Exp, scale=-1.0).then_inc(desk.emptied, 1)
                if end:
                    bank = taken(it, "o")
                    if not is_first(end[0]):
                        act.wait_ge(x_done, end[0])
                    nc.scalar.activation(ob[:, :, :].rearrange("p t c -> p (t c)"), bank[:, 0:T], ACT.Copy)\
                        .then_inc(desk.emptied, 1)
                if new:
                    bank = taken(it, "xt")
                    nc.scalar.activation(xt[:, :], bank[:, 0:T], ACT.Copy).then_inc(desk.emptied, 1)
                    for name, dst in (("q", qp), ("k", kp)):
                        bank = taken(it, name)
                        if not is_first(new[0]):
                            act.wait_ge(qk_ready, new[0] * 2)
                        nc.scalar.activation(dst[:, :, :].rearrange("p u t -> p (u t)"), bank, ACT.Copy)\
                            .then_inc(desk.emptied, 1)

            Pipeline.run(act, step)

        @block.vector
        def _(dve):
            dve.sem_inc(sr.emptied, AB)
            nc.vector.memset(one[:, :], 1.0).then_inc(one_ready, 1)

            def turn(it, new, name):
                src, turned, u = (qp, qp_turned, 0) if name == "q" else (kp, kp_turned, 2)
                dve.wait_ge(desk.emptied, desk.done(it, name))
                nc.vector.tensor_tensor(src[:, :, :], src[:, :, :], rope[:, u:u + 2, :], ALU.mult).then_inc(turned, 1)

            def small(it, n):
                new, prep, end = Pipeline.start(it), Pipeline.prepare(it), Pipeline.finish(it)
                if end:
                    b, par = end
                    if n == 3:
                        dve.wait_ge(av_done, b * H + H)
                        nc.vector.bn_stats(ystats[:, :], y_ps[:, par, 0:T]).then_inc(y_stats, 1)
                        dve.wait_ge(y_stats, b + 1)
                        nc.vector.memset(k.idle, 0.0)
                        nc.vector.bn_aggr(ymv[:, :], ystats[:, :]).then_inc(y_aggr, 1)
                    if n == 6:
                        dve.wait_ge(desk.emptied, desk.done(it, "gm"))
                        nc.vector.tensor_tensor(dmean[:, :], ymv[:, 0:1], mean[:, :], ALU.subtract).then_inc(dm_ready, 1)
                        dve.wait_ge(dm_ready, b + 1)
                        nc.vector.scalar_tensor_tensor(qv[:, :], dmean[:, :], dmean[:, 0:1], ymv[:, 1:2], ALU.mult,
                                                       ALU.add).then_inc(qv_ready, 1)
                    if n == 10:
                        dve.wait_ge(y_rstd, b + 1)
                        nc.vector.tensor_tensor(ga[:, :], rstd_y[:, :], gnw[:, :], ALU.mult).then_inc(ga_ready, 1)
                        dve.wait_ge(ga_ready, b + 1)
                        nc.vector.scalar_tensor_tensor(nb[:, :], mean[:, :], ga[:, 0:1], gnb[:, :], ALU.mult,
                                                       ALU.subtract).then_inc(nb_ready, 1)
                        dve.wait_ge(nb_ready, b + 1)
                        nc.vector.tensor_scalar(yn[:, :], y_ps[:, par, 0:T], ga[:, 0:1], nb[:, 0:1], ALU.mult,
                                                ALU.subtract).then_inc(yn_ready, 1)
                        dve.wait_ge(yn_ready, b + 1)
                        dve.wait_ge(silu_ready, b + 1)
                        nc.vector.tensor_tensor(gated[:, :], yn[:, :], silu[:, par, :], ALU.mult)\
                            .then_inc(gated_ready, 1)
                if prep:
                    b, par = prep
                    if n == 1:
                        if not is_first(b) and not is_first(b, 1):
                            dve.wait_ge(bounced, b * 16 - 16)
                        dve.wait_ge(qk_ready, b * 2 + 2)
                        nc.vector.tensor_copy(parts[:, par, 0, :, :], qk[:, :, :]).then_inc(part1, 1)
                    if n == 3:
                        dve.wait_ge(rest1, b + 1)
                        nc.vector.tensor_copy(parts[:, par, 1, :, :], rest[:, :, :]).then_inc(part2, 1)
                    if n == 12:
                        dve.wait_ge(eg1, b + 1)
                        nc.vector.reciprocal(eg[:, :], eg[:, :]).then_inc(eg2, 1)
                if new:
                    b = new[0]
                    if n == 6:
                        for t in range(TT):
                            nc.vector.bn_stats(stats[:, t, :], x_b[:, b, t, :]).then_inc(ln_stats, 1)
                        dve.wait_ge(ln_stats, b * TT + TT)
                        nc.vector.memset(k.idle, 0.0)
                        for t in range(TT):
                            last = nc.vector.bn_aggr(mv[:, t, :], stats[:, t, :])
                        last.then_inc(ln_aggr, 1)
                    if n == 11:
                        dve.wait_ge(ln_rstd, b + 1)
                        for t in range(TT):
                            nc.vector.tensor_scalar(xn[:, t, :], x_b[:, b, t, :], mv[:, t, 0:1], rstd[:, t:t + 1],
                                                    ALU.subtract, ALU.mult).then_inc(xn_ready, 1)
                        if is_first(b):
                            nc.vector.memset(vm[:, :, :, :, :].rearrange("p a b c d -> p (a b c d)"), 0.0)\
                                .then_inc(vm_zero, 1)
                            dve.wait_ge(loaded, LOADS)
                    if n == 14:
                        turn(it, new, "q")
                    if n == 15:
                        turn(it, new, "k")

            def decayed(b, n):
                h = (n % QUAD) * QUAD + n // QUAD
                dve.wait_ge(sr.filled, sr.nth(b, n))
                if not (is_first(b[0]) and n < DECAYED):
                    dve.wait_ge(av_done, b[0] * H + n - DECAYED + 1)
                nc.vector.tensor_tensor(att[:, n % DECAYED, :], sr.bank(b, n)[:, 0:T + P], decay[:, h, :], ALU.mult)\
                    .then_inc(sr.emptied, 1)

            def step(it, inner=False):
                b, end = Pipeline.attend(it), Pipeline.finish(it)
                if b and is_first(b[0]):
                    dve.wait_ge(decay_loaded, 16)
                for n in range(H):
                    if b:
                        decayed(b, n)
                    small(it, n)

            dve.wait_ge(k.loaded, k.loaded_count)
            Pipeline.run(dve, step)

        @block.gpsimd
        def _(pool):
            def step(it, inner=False):
                new, prep, end = Pipeline.start(it), Pipeline.prepare(it), Pipeline.finish(it)
                if prep:
                    b, par = prep
                    pool.wait_ge(part1, b + 1)
                    nc.gpsimd.tensor_tensor(rest[:, :, :], qk[:, :, :], parts[:, par, 0, :, :], ALU.subtract)\
                        .then_inc(rest1, 1)
                    pool.wait_ge(part2, b + 1)
                    nc.gpsimd.tensor_tensor(parts[:, par, 2, :, :], rest[:, :, :], parts[:, par, 1, :, :],
                                            ALU.subtract).then_inc(parts_ready, 1)
                if end:
                    b = end[0]
                    pool.wait_ge(desk.emptied, desk.done(it, "gv"))
                    nc.gpsimd.tensor_tensor(veps_y[:, :], var[:, :], k.eps[:, 0:1], ALU.add).then_inc(y_veps, 1)
                    pool.wait_ge(y_veps, b + 1)
                    nc.gpsimd.tensor_tensor(rstd_y[:, :], veps_y[:, :], k.minus_half[:, 0:1], ALU.pow)\
                        .then_inc(y_rstd, 1)
                if new:
                    b = new[0]
                    pool.wait_ge(ln_aggr, b + 1)
                    nc.gpsimd.tensor_tensor(veps[:, :], mv[:, :, 1], k.eps[:, 0:TT], ALU.add).then_inc(ln_veps, 1)
                    pool.wait_ge(ln_veps, b + 1)
                    nc.gpsimd.tensor_tensor(rstd[:, :], veps[:, :], k.minus_half[:, 0:TT], ALU.pow).then_inc(ln_rstd, 1)
                if prep:
                    b, par = prep
                    pool.wait_ge(desk.emptied, desk.done(it, "g"))
                    nc.gpsimd.tensor_tensor(eg[:, :], eg[:, :], one[:, :].to_broadcast([P, T]), ALU.add)\
                        .then_inc(eg1, 1)
                if end:
                    b = end[0]
                    pool.wait_ge(desk.emptied, desk.done(it, "o"))
                    nc.gpsimd.tensor_tensor(x_b[:, b, :, :], x_b[:, b, :, :], ob[:, :, :], ALU.add).then_inc(x_done, 1)
                if prep:
                    b, par = prep
                    pool.wait_ge(eg2, b + 1)
                    if not is_first(b) and not is_first(b, 1):
                        pool.wait_ge(gated_ready, b - 1)
                    nc.gpsimd.tensor_tensor(silu[:, par, :], gate[:, :], eg[:, :], ALU.mult).then_inc(silu_ready, 1)
                if new:
                    b = new[0]
                    for u, (src, turned) in enumerate(((qp, qp_turned), (kp, kp_turned))):
                        pool.wait_ge(turned, b + 1)
                        nc.gpsimd.tensor_tensor(qk[:, u, :], src[:, 0, :], src[:, 1, :], ALU.add).then_inc(qk_ready, 1)

            pool.wait_ge(k.loaded, k.loaded_count)
            pool.wait_ge(one_ready, 1)
            Pipeline.run(pool, step)


def head_at(hs):
    return (hs % QUAD) * QUAD + hs // QUAD


def positions_weights(nc, a, io, w):
    w.selw, w.ln = a.sb("selw", [P, E1]), a.sb("ln", [P, 4])
    w.ws = a.sb("ws", [ROWS, 2, H, C], BF16)
    w.small_loaded, w.small_count = a.sem("small_loaded"), 32
    w.wp_loaded, w.wp_split, w.wp_bounced, w.ws_stacked = [a.sem(n) for n in (
        "wp_loaded", "wp_split", "wp_bounced", "ws_stacked")]
    scratch = nc.dram_tensor("wp_scratch", (6, P, C), BF16, kind="Internal").ap()

    def load(sp):
        sp.dma_start(w.wp[:, :, :], io["wp"]).then_inc(w.wp_loaded, 16)
        sp.dma_start(w.selw[:, :], io["selw"]).then_inc(w.small_loaded, 16)
        sp.dma_start(w.ln[:, :], io["ln"]).then_inc(w.small_loaded, 16)
        sp.wait_ge(w.wp_split, 4)
        sp.dma_start(scratch.rearrange("n c f -> c n f"), w.wp_parts[:, :, :, :].rearrange("c n u f -> c (n u) f"))\
            .then_inc(w.wp_bounced, 16)
        sp.wait_ge(w.wp_bounced, 16)
        for first, run in RUNS:
            for u in range(2):
                sp.dma_start(w.ws[first * HD:(first + run) * HD, u, :, :].rearrange("s h f -> s (h f)"),
                             slots_of(scratch[u], run, 2 * P * C, C)).then_inc(w.ws_stacked, 16)
        sp.wait_ge(w.small_loaded, w.small_count)
        sp.wait_ge(w.ws_stacked, STACKED)

    def split(dve):
        dve.wait_ge(w.wp_loaded, 16)
        nc.vector.tensor_copy(w.wp_parts[:, 0, :, :], w.wp[:, :, :]).then_inc(w.wp_split, 1)
        dve.wait_ge(w.wp_split, 1)
        nc.vector.tensor_tensor(w.wp_rest[:, :, :], w.wp[:, :, :], w.wp_parts[:, 0, :, :], ALU.subtract)\
            .then_inc(w.wp_split, 1)
        dve.wait_ge(w.wp_split, 2)
        nc.vector.tensor_copy(w.wp_parts[:, 1, :, :], w.wp_rest[:, :, :]).then_inc(w.wp_split, 1)
        dve.wait_ge(w.wp_split, 3)
        nc.vector.tensor_tensor(w.wp_parts[:, 2, :, :], w.wp_rest[:, :, :], w.wp_parts[:, 1, :, :], ALU.subtract)\
            .then_inc(w.wp_split, 1)

    w.load_positions, w.split_positions = load, split


def layer1_weights(nc, a, io, w):
    w.keys, w.values = a.sb("keys", [P, E1, P]), a.sb("values", [P, E1, C])
    w.experts_loaded, w.experts_count = a.sem("experts_loaded"), 32

    def load(sp):
        sp.dma_start(w.keys[:, :, :], io["keys"]).then_inc(w.experts_loaded, 16)
        sp.dma_start(w.values[:, :, :], io["values"]).then_inc(w.experts_loaded, 16)
        sp.wait_ge(w.experts_loaded, w.experts_count)

    w.load_experts = load


def relative_ffn(nc, tag, x_sb, k, w, io):
    with ExitStack() as ctx:
        a = Pool_(nc, ctx, tag)
        x2t = a.sb("x2t", [P, B * TT, P])
        gates = a.sb("gates", [P, B * TT, E1])
        softmax_attention(nc, f"{tag}a", x_sb, k, io, w, x2t, gates)
        mixture(nc, f"{tag}m", x_sb, k, w, x2t, gates)


def plain_attention(nc, tag, x_sb, k, io):
    softmax_attention(nc, tag, x_sb, k, io)


def softmax_attention(nc, tag, x_sb, k, io, w=None, x2t_all=None, gates=None):
    rel = w is not None
    x_b = x_sb[:, :, :].rearrange("p (b t) c -> p b t c", t=TT)
    SB = 2 if rel else 4
    NR, RRS, AHEAD, RAW = 16, 8, 5, 4
    TURN = 2 if rel else 3
    VALUES = TURN + 5
    with ExitStack() as ctx:
        a = Pool_(nc, ctx, tag)
        wq, wo = a.sb("wq", [P, 3, C]), a.sb("wo", [P, C])
        stats, mv = a.sb("stats", [P, TT, 6]), a.sb("mv", [P, TT, 2])
        veps, rstd = a.sb("veps", [P, TT]), a.sb("rstd", [P, TT])
        xn, xt = a.sb("xn", [P, TT, C]), a.sb("xt", [P, T])
        qk, rest = a.sb("qk", [P, 2, T]), a.sb("rest", [P, 2, T])
        parts = a.sb("parts", [P, 2, 3, 2, T], BF16)
        qs, ks = k.qs, k.ks
        scratch = nc.dram_tensor(f"{tag}_scratch", (2, 6, P, T), BF16, kind="Internal").ap()
        vm = a.sb("vm", [P, 2, TT, QUAD, C])
        nm = a.sb("nm", [P, SB, 2])
        zs = a.sb("zs", [P, 2, TT, H])
        pr = a.sb("pr", [P, 4, 2, T])
        pts = a.sb("pts", [P, 2, TT, QUAD, T])
        rz, rz8, rzb = a.sb("rz", [P, TT, H]), a.sb("rz8", [P, TT, H, HD]), a.sb("rzb", [P, T])
        yn, ob = a.sb("yn", [P, T]), a.sb("ob", [P, TT, C])
        if rel:
            src = a.sb("src", [P, B, TT, C])
            pe_t, turn = yn, a.sb("turn", [P, 2, T])
            pe_hi, pe_lo = a.sb("pe_hi", [P, T], F32R), a.sb("pe_lo", [P, T], F32R)
            tmp, rr = a.sb("tmp", [P, 2, 2, T]), a.sb("rr", [P, RAW, T])
            rr_hi, rr_lo = a.sb("rr_hi", [P, RRS, T], F32R), a.sb("rr_lo", [P, RRS, T], F32R)
            s1, x2 = a.sb("s1", [P, TT, C]), ob
            stats2, mv2 = a.sb("stats2", [P, TT, 6]), a.sb("mv2", [P, TT, 2])
            veps2, rstd2 = a.sb("veps2", [P, TT]), a.sb("rstd2", [P, TT])
            stats3, mv3 = a.sb("stats3", [P, TT, 6]), a.sb("mv3", [P, TT, 2])
            veps3, rstd3 = a.sb("veps3", [P, TT]), a.sb("rstd3", [P, TT])
            x2s = xt
            sel, best = a.sb("sel", [P, TT, E1]), a.sb("best", [P, TT, 8])
            best_at, best_f = a.sb("best_at", [P, TT, 8], U32), a.sb("best_f", [P, TT, TOPK])
            pick = a.sb("pick", [P, TT, TOPK, E1])
        else:
            bp = a.sb("bp", [P, C])

        sr = Ring(a.ps("sr", [P, SB, 512]), a.sem("sr_filled"), a.sem("sr_emptied"), NR, SB)
        tr = [Ring(a.ps(f"tr{e}", [P, 1, 512]), a.sem(f"tr{e}_filled"), a.sem(f"tr{e}_emptied"), NR // 2, 1)
              for e in range(2)]
        y_ps = a.ps("y", [P, 512])
        desk = Desk(a.ps("desk", [P, 1, 512]), a.sem("desk_filled"), a.sem("desk_emptied"),
                    [("rz", 3), ("v", 1), ("o", 3)] + ([("x2t", 3), ("sel", 3)] if rel else []) +
                    [("xt", 0), ("qk", 0)], 1)
        if rel:
            ur = Ring(a.ps("ur", [P, 2, 512]), a.sem("ur_filled"), a.sem("ur_emptied"), H, 2)
        names = ("loaded wq_scaled vm_zero ln_stats ln_aggr ln_veps ln_rstd xn_ready part1 rest1 part2 parts_ready "
                 "bounced stacked passed nm_ready av_done rz_ready rz8_ready yn_ready bias_added x_done").split()
        (loaded, wq_scaled, vm_zero, ln_stats, ln_aggr, ln_veps, ln_rstd, xn_ready, part1, rest1, part2, parts_ready,
         bounced, stacked, passed, nm_ready, av_done, rz_ready, rz8_ready, yn_ready, bias_added, x_done) = [
             a.sem(n) for n in names]
        if rel:
            names = ("src_ready src_stats src_aggr src_veps src_rstd pe_split rr_ready rr_hi_ready rr_lo_ready s1_ready s1_stats s1_aggr s1_veps "
                     "s1_rstd x2_ready gate_step gates_ready").split()
            (src_ready, src_stats, src_aggr, src_veps, src_rstd, pe_split, rr_ready, rr_hi_ready, rr_lo_ready, s1_ready, s1_stats, s1_aggr,
             s1_veps, s1_rstd, x2_ready, gate_step, gates_ready) = [a.sem(n) for n in names]
        block = ctx.enter_context(nc.Block())

        attend, finish, prep, new = Pipeline.attend, Pipeline.finish, Pipeline.prepare, Pipeline.start

        def turning(it, n):
            if n >= TURN:
                return (attend(it), n - TURN)
            return (finish(it), NR - TURN + n)

        def relating(it, n, ahead=AHEAD):
            if n + ahead < NR:
                return (attend(it), n + ahead)
            return (prep(it), n + ahead - NR)

        def acts(n):
            return rel or n % 2 == 1

        def later_than(b, first):
            return not isinstance(b[0], int) or b[0] >= first

        LOADS = 16 * (4 if rel else 3)

        @block.sync
        def _(sp):
            sp.dma_start(wq[:, :, :], io["w4" if rel else "w5"].rearrange("p (n c) -> p n c", c=C)).then_inc(loaded, 16)
            sp.dma_start(wo[:, :], io["w4p" if rel else "w5p"]).then_inc(loaded, 16)
            if rel:
                sp.dma_start(pe_t[:, :], io["pe"]).then_inc(loaded, 16)
                sp.dma_start(turn[:, :, :], io["turn"]).then_inc(loaded, 16)
            else:
                sp.dma_start(bp[:, :], io["b5p"].partition_broadcast(P)).then_inc(loaded, 16)
            if rel and w.load_experts is not None:
                w.load_experts(sp)
                w.load_experts = None
            stack_parts(sp, parts, scratch, qs, ks, parts_ready, bounced, stacked, passed, sr)

        @block.tensor
        def _(pe):
            def fill(it, name):
                pe.wait_ge(desk.emptied, desk.nth(it, name))
                return desk.bank(it, name)

            def relate(b, hs):
                if hs == 0:
                    pe.wait_ge(stacked, b[0] * STACKED + STACKED)
                pe.wait_ge(ur.emptied, ur.nth(b, hs))
                out = ur.bank(b, hs)
                h = head_at(hs)
                for u in range(2):
                    mm = nc.tensor.matmul(out[:, u * T:(u + 1) * T], w.ws[:, u, h, :], qs[:, b[1], h, :],
                                          start=True, stop=True)
                mm.then_inc(ur.filled, 1)

            def scores(b, n):
                r, jj, t = n // QUAD, n // 2 % 2, n % 2
                pe.wait_ge(sr.emptied, sr.nth(b, n))
                if rel and t == 0:
                    pe.wait_ge(rr_lo_ready, b[0] * H + n + 2)
                for x in range(2):
                    h = (2 * jj + x) * QUAD + r
                    out = sr.bank(b, n)[:, x * T:(x + 1) * T]
                    mm = nc.tensor.matmul(out, qs[:, b[1], h, t * P:(t + 1) * P], ks[:, b[1], h, :],
                                          start=True, stop=not rel)
                    if rel:
                        at = (slice(None), (n - t + x) % RRS, slice(t * P, (t + 1) * P))
                        nc.tensor.matmul(out, rr_hi[at], pe_hi[:, :], start=False, stop=False)
                        nc.tensor.matmul(out, rr_hi[at], pe_lo[:, :], start=False, stop=False)
                        mm = nc.tensor.matmul(out, rr_lo[at], pe_hi[:, :], start=False, stop=True)
                mm.then_inc(sr.filled, 1)

            def turn_round(b, n):
                ring = tr[n % 2]
                pe.wait_ge(ring.emptied, ring.nth(b, n // 2))
                pe.wait_ge(sr.emptied, sr.done(b, n))
                for st in range(TT):
                    for x in range(2):
                        o = (st * 2 + x) * P
                        mm = nc.tensor.transpose(ring.bank(b, n // 2)[:, o:o + P],
                                                 pr[:, n % 4, x, st * P:(st + 1) * P], k.ident)
                mm.then_inc(ring.filled, 1)

            def values(b, r):
                for e in range(2):
                    pe.wait_ge(tr[e].emptied, tr[e].done(b, 2 * r + 1))
                if r == 0 and later_than(b, 1):
                    pe.wait_ge(yn_ready, b[0])
                for st in range(TT):
                    for j in range(QUAD):
                        q = slice(j * QUAD * HD, (j + 1) * QUAD * HD)
                        mm = nc.tensor.matmul(y_ps[q, 0:T], vm[:, b[1], st, r, q], pts[:, r % 2, st, j, :],
                                              start=(r == 0 and st == 0), stop=(r == QUAD - 1 and st == TT - 1),
                                              skip_group_check=True)
                mm.then_inc(av_done, 1)

            def small(it, n):
                b, e = new(it), finish(it)
                if n == 3 and e:
                    pe.wait_ge(rz8_ready, e[0] + 1)
                    out = fill(it, "rz")
                    for t in range(TT):
                        mm = nc.tensor.transpose(out[:, t * P:(t + 1) * P],
                                                 rz8[:, t, :, :].rearrange("p h d -> p (h d)"), k.ident)
                    mm.then_inc(desk.filled, 1)
                if n == VALUES - 3 and prep(it):
                    out = fill(it, "v")
                    for t in range(TT):
                        mm = nc.tensor.matmul(out[:, t * P:(t + 1) * P], xt[:, t * P:(t + 1) * P], wq[:, 2, :],
                                              start=True, stop=True)
                    mm.then_inc(desk.filled, 1)
                if n == VALUES - 1 and e:
                    out = fill(it, "o")
                    pe.wait_ge(yn_ready, e[0] + 1)
                    for t in range(TT):
                        mm = nc.tensor.matmul(out[:, t * P:(t + 1) * P], yn[:, t * P:(t + 1) * P], wo[:, :],
                                              start=True, stop=True)
                    mm.then_inc(desk.filled, 1)
                if rel and n == 10 and e:
                    out = fill(it, "x2t")
                    pe.wait_ge(x2_ready, e[0] * TT + TT)
                    for t in range(TT):
                        mm = nc.tensor.transpose(out[:, t * P:(t + 1) * P], x2[:, t, :], k.ident)
                    mm.then_inc(desk.filled, 1)
                if rel and n == 12 and e:
                    out = fill(it, "sel")
                    for t in range(TT):
                        mm = nc.tensor.matmul(out[:, t * E1:(t + 1) * E1], x2s[:, t * P:(t + 1) * P], w.selw[:, :],
                                              start=True, stop=True)
                    mm.then_inc(desk.filled, 1)
                if n == 13 and b:
                    pe.wait_ge(xn_ready, b[0] * TT + TT)
                    out = fill(it, "xt")
                    for t in range(TT):
                        mm = nc.tensor.transpose(out[:, t * P:(t + 1) * P], xn[:, t, :], k.ident)
                    mm.then_inc(desk.filled, 1)
                if n == 15 and b:
                    if is_first(b[0]):
                        pe.wait_ge(loaded, LOADS)
                        pe.wait_ge(wq_scaled, 1)
                    out = fill(it, "qk")
                    for u in range(2):
                        mm = nc.tensor.matmul(out[:, u * T:(u + 1) * T], wq[:, u, :], xt[:, :], start=True, stop=True)
                    mm.then_inc(desk.filled, 1)

            def step(it, inner=False):
                if attend(it) and is_first(attend(it)[0]):
                    pe.wait_ge(vm_zero, 1)
                    if rel:
                        pe.wait_ge(pe_split, 2)
                for n in range(NR):
                    small(it, n)
                    if rel:
                        b, hs = relating(it, n)
                        if b is not None:
                            relate(b, hs)
                    if attend(it):
                        if n == 0 and not rel:
                            pe.wait_ge(stacked, attend(it)[0] * STACKED + STACKED)
                        scores(attend(it), n)
                    b, m = turning(it, n)
                    if b is not None:
                        turn_round(b, m)
                    for r in range(QUAD):
                        at = VALUES + r * QUAD
                        if n == at and attend(it):
                            values(attend(it), r)
                        if n == at - NR and finish(it):
                            values(finish(it), r)

            pe.wait_ge(k.loaded, k.loaded_count)
            Pipeline.run(pe, step)

        def take_turned(eng, b, n, copy):
            r, jj, t = n // QUAD, n // 2 % 2, n % 2
            ring = tr[t]
            eng.wait_ge(ring.filled, ring.nth(b, n // 2))
            if n % QUAD < 2 and (r >= 2 or later_than(b, 1)):
                eng.wait_ge(av_done, b[0] * QUAD + r - 1)
            copy(pts[:, r % 2, :, 2 * jj:2 * jj + 2, t * P:(t + 1) * P],
                 ring.bank(b, n // 2).rearrange("p (s x t) -> p s x t", s=TT, x=2)).then_inc(ring.emptied, 1)

        @block.scalar
        def _(act):
            act.sem_inc(desk.emptied, 1)
            act.sem_inc(tr[1].emptied, 1)
            act.sem_inc(sr.emptied, SB)

            def copy(dst, src_):
                return nc.scalar.activation(dst, src_, ACT.Copy)

            def taken(it, name):
                act.wait_ge(desk.filled, desk.nth(it, name))
                return desk.bank(it, name)

            def exponentials(b, n):
                t, hs = n % 2, n - n % 2
                act.wait_ge(nm_ready, b[0] * NR + n + 1)
                if n >= 4 or later_than(b, 1):
                    act.wait_ge(tr[t].filled, b[0] * (NR // 2) + n // 2 - 1)
                if n == 0 and later_than(b, 2):
                    act.wait_ge(rz_ready, b[0] - 1)
                for x in range(2):
                    h = head_at(hs + x)
                    last = nc.scalar.activation(pr[:, n % 4, x, :], sr.bank(b, n)[:, x * T:(x + 1) * T], ACT.Exp,
                                                bias=nm[:, n % SB, x:x + 1], accum_out=zs[:, b[1], t, h:h + 1])
                last.then_inc(sr.emptied, 1)

            def small(it, n):
                b, p, e = new(it), prep(it), finish(it)
                if n == 3 and e:
                    bank = taken(it, "rz")
                    copy(rzb[:, :], bank[:, 0:T]).then_inc(desk.emptied, 1)
                if n == VALUES - 3 and p:
                    bank = taken(it, "v")
                    if is_first(p[0]):
                        act.wait_ge(vm_zero, 1)
                    if not is_first(p[0]) and not is_first(p[0], 1):
                        act.wait_ge(av_done, (p[0] - 1) * QUAD)
                    for t in range(TT):
                        last = copy(heads_of((vm, p[1], t)),
                                    bank[:, t * P:(t + 1) * P].rearrange("p (j r d) -> p r j d", r=QUAD, d=HD))
                    last.then_inc(desk.emptied, 1)
                if n == VALUES - 1 and e:
                    bank = taken(it, "o")
                    if not is_first(e[0]):
                        act.wait_ge(s1_ready if rel else x_done, e[0])
                    copy(ob[:, :, :].rearrange("p t c -> p (t c)"), bank[:, 0:T]).then_inc(desk.emptied, 1)
                if rel and n == 10 and e:
                    bank = taken(it, "x2t")
                    nc.scalar.activation(x2s[:, :], bank[:, 0:T], ACT.Identity, scale=w.ln[:, 2:3], bias=w.ln[:, 3:4])
                    tiles = x2t_all[:, :, :].rearrange("p (b t) c -> p b (t c)", t=TT)
                    nc.scalar.activation(tiles[:, e[0], :], bank[:, 0:T], ACT.Identity, scale=w.ln[:, 2:3],
                                         bias=w.ln[:, 3:4]).then_inc(desk.emptied, 1)
                if rel and n == 12 and e:
                    bank = taken(it, "sel")
                    if not is_first(e[0]):
                        act.wait_ge(gates_ready, e[0])
                    nc.scalar.activation(sel[:, :, :].rearrange("p t e -> p (t e)"), bank[:, 0:TT * E1], ACT.Exp,
                                         scale=-1.0).then_inc(desk.emptied, 1)
                if n == 13 and b:
                    bank = taken(it, "xt")
                    if rel:
                        last = nc.scalar.activation(xt[:, :], bank[:, 0:T], ACT.Identity, scale=w.ln[:, 0:1],
                                                    bias=w.ln[:, 1:2])
                    else:
                        last = copy(xt[:, :], bank[:, 0:T])
                    last.then_inc(desk.emptied, 1)
                if n == 15 and b:
                    bank = taken(it, "qk")
                    if not is_first(b[0]):
                        act.wait_ge(rest1, b[0])
                    copy(qk[:, :, :].rearrange("p u t -> p (u t)"), bank).then_inc(desk.emptied, 1)

            def round_terms(b, hs):
                act.wait_ge(rr_ready, b[0] * H + hs + 1)
                if hs % 2 == 0 and (hs >= RRS or later_than(b, 1)):
                    act.wait_ge(sr.filled, b[0] * NR + hs + 2 - RRS)
                nc.scalar.activation(rr_hi[:, hs % RRS, :], rr[:, hs % RAW, :], ACT.Copy).then_inc(rr_hi_ready, 1)

            def step(it, inner=False):
                for n in range(NR):
                    small(it, n)
                    b, m = turning(it, n)
                    if b is not None and acts(m):
                        take_turned(act, b, m, copy)
                    if rel:
                        b, hs = relating(it, n, AHEAD - 1)
                        if b is not None:
                            round_terms(b, hs)
                    if attend(it):
                        exponentials(attend(it), n)

            if rel:
                act.wait_ge(w.small_loaded, w.small_count)
            Pipeline.run(act, step)

        @block.vector
        def _(dve):
            dve.sem_inc(tr[0].emptied, 1)
            if rel:
                dve.sem_inc(ur.emptied, 2)

            def measure(i, value, stats_, mv_, stats_sem, aggr_sem):
                for t in range(TT):
                    nc.vector.bn_stats(stats_[:, t, :], value(t)).then_inc(stats_sem, 1)
                dve.wait_ge(stats_sem, i * TT + TT)
                nc.vector.memset(k.idle, 0.0)
                for t in range(TT):
                    last = nc.vector.bn_aggr(mv_[:, t, :], stats_[:, t, :])
                last.then_inc(aggr_sem, 1)

            def normalise(dst, value, mv_, rstd_, ready):
                for t in range(TT):
                    nc.vector.tensor_scalar(dst(t), value(t), mv_[:, t, 0:1], rstd_[:, t:t + 1], ALU.subtract,
                                            ALU.mult).then_inc(ready, 1)

            def once():
                dve.wait_ge(loaded, LOADS)
                nc.vector.tensor_scalar(wq[:, 0, :], wq[:, 0, :], float(np.float32(HD ** -0.5)), None, ALU.mult)\
                    .then_inc(wq_scaled, 1)
                nc.vector.memset(vm[:, :, :, :, :].rearrange("p a b c d -> p (a b c d)"), 0.0).then_inc(vm_zero, 1)
                if rel:
                    nc.vector.tensor_copy(pe_hi[:, :], pe_t[:, :]).then_inc(pe_split, 1)
                    dve.wait_ge(pe_split, 1)
                    nc.vector.tensor_tensor(pe_lo[:, :], pe_t[:, :], pe_hi[:, :], ALU.subtract).then_inc(pe_split, 1)

            def maxima(b, n):
                dve.wait_ge(sr.filled, sr.nth(b, n))
                nc.vector.tensor_reduce(nm[:, n % SB, :], sr.bank(b, n).rearrange("p (x s) -> p x s", x=2), AX.X,
                                        ALU.max, negate=True).then_inc(nm_ready, 1)

            def rotate(b, hs):
                dve.wait_ge(ur.filled, ur.nth(b, hs))
                if hs >= 2 or later_than(b, 1):
                    dve.wait_ge(rr_ready, b[0] * H + hs - 1)
                nc.vector.tensor_tensor(tmp[:, hs % 2, :, :], ur.bank(b, hs).rearrange("p (u t) -> p u t", u=2),
                                        turn[:, :, :], ALU.mult).then_inc(ur.emptied, 1)

            def gate(it, part):
                i = finish(it)[0]

                def stepped(n, last):
                    last.then_inc(gate_step, 1)
                    dve.wait_ge(gate_step, i * 8 + n)

                if part == 0:
                    dve.wait_ge(desk.emptied, desk.done(it, "sel"))
                    stepped(1, nc.vector.tensor_scalar(sel[:, :, :], sel[:, :, :], 1.0, None, ALU.add))
                    stepped(2, nc.vector.reciprocal(sel[:, :, :], sel[:, :, :]))
                    nc.vector.memset(k.idle, 0.0)
                    for t in range(TT):
                        last = nc.vector.max(best[:, t, :], sel[:, t, :])
                    last.then_inc(gate_step, 1)
                if part == 1:
                    dve.wait_ge(gate_step, i * 8 + 3)
                    nc.vector.memset(k.idle, 0.0)
                    for t in range(TT):
                        last = nc.vector.max_index(best_at[:, t, :], best[:, t, :], sel[:, t, :])
                    stepped(4, last)
                    stepped(5, nc.vector.tensor_copy(best_f[:, :, :], best_at[:, :, 0:TOPK]))
                    for t in range(TT):
                        last = nc.vector.tensor_tensor(pick[:, t, :, :],
                                                       k.iota32.unsqueeze(1).to_broadcast([P, TOPK, E1]),
                                                       best_f[:, t, :].unsqueeze(2).to_broadcast([P, TOPK, E1]),
                                                       ALU.is_equal)
                    last.then_inc(gate_step, 1)
                if part == 2:
                    dve.wait_ge(gate_step, i * 8 + 6)
                    for t in range(TT):
                        last = nc.vector.tensor_tensor(pick[:, t, :, :], pick[:, t, :, :],
                                                       best[:, t, 0:TOPK].unsqueeze(2).to_broadcast([P, TOPK, E1]),
                                                       ALU.mult)
                    stepped(7, last)
                    stepped(8, nc.vector.tensor_tensor(pick[:, :, 0:2, :], pick[:, :, 0:2, :], pick[:, :, 2:4, :],
                                                       ALU.add))
                    g = gates[:, :, :].rearrange("p (b t) e -> p b t e", t=TT)
                    nc.vector.tensor_tensor(g[:, i, :, :], pick[:, :, 0, :], pick[:, :, 1, :], ALU.add)\
                        .then_inc(gates_ready, 1)

            def small(it, n):
                b, p, e = new(it), prep(it), finish(it)
                if e:
                    i, par = e
                    if n == 1:
                        dve.wait_ge(sr.emptied, sr.done(e, NR - 1))
                        nc.vector.reciprocal(rz[:, :, :], zs[:, par, :, :]).then_inc(rz_ready, 1)
                        dve.wait_ge(rz_ready, i + 1)
                        nc.vector.tensor_copy(rz8[:, :, :, :], rz[:, :, :].unsqueeze(3).to_broadcast([P, TT, H, HD]))\
                            .then_inc(rz8_ready, 1)
                    if n == VALUES - 3:
                        dve.wait_ge(av_done, (i + 1) * QUAD)
                        dve.wait_ge(desk.emptied, desk.done(it, "rz"))
                        nc.vector.tensor_tensor(yn[:, :], y_ps[:, 0:T], rzb[:, :], ALU.mult).then_inc(yn_ready, 1)
                    if rel and n == 7:
                        dve.wait_ge(desk.emptied, desk.done(it, "o"))
                        nc.vector.tensor_tensor(s1[:, :, :], ob[:, :, :], src[:, i, :, :], ALU.add)\
                            .then_inc(s1_ready, 1)
                        dve.wait_ge(s1_ready, i + 1)
                        nc.vector.scalar_tensor_tensor(x_b[:, i, :, :], s1[:, :, :], 0.5, x_b[:, i, :, :],
                                                       ALU.mult, ALU.add)
                        measure(i, lambda t: s1[:, t, :], stats3, mv3, s1_stats, s1_aggr)
                    if rel and n == 8:
                        dve.wait_ge(s1_rstd, i + 1)
                        normalise(lambda t: x2[:, t, :], lambda t: s1[:, t, :], mv3, rstd3, x2_ready)
                    if rel and n in (13, 14, 15):
                        gate(it, n - 13)
                if p:
                    i, par = p
                    if n == 1:
                        if not is_first(i) and not is_first(i, 1):
                            dve.wait_ge(bounced, i * 16 - 16)
                        dve.wait_ge(desk.emptied, desk.done(before(it), "qk"))
                        nc.vector.tensor_copy(parts[:, par, 0, :, :], qk[:, :, :]).then_inc(part1, 1)
                    if n == 3:
                        dve.wait_ge(rest1, i + 1)
                        nc.vector.tensor_copy(parts[:, par, 1, :, :], rest[:, :, :]).then_inc(part2, 1)
                if b:
                    i = b[0]
                    x_of = lambda t: x_b[:, i, t, :]
                    if rel and n == 5:
                        measure(i, x_of, stats2, mv2, src_stats, src_aggr)
                    if rel and n == 6:
                        dve.wait_ge(src_rstd, i + 1)
                        normalise(lambda t: src[:, i, t, :], x_of, mv2, rstd2, src_ready)
                        dve.wait_ge(src_ready, i * TT + TT)
                        nc.vector.memset(k.idle, 0.0)
                    if n == (9 if rel else 8):
                        measure(i, (lambda t: src[:, i, t, :]) if rel else x_of, stats, mv, ln_stats, ln_aggr)
                    if n == 10:
                        dve.wait_ge(ln_rstd, i + 1)
                        normalise(lambda t: xn[:, t, :], (lambda t: src[:, i, t, :]) if rel else x_of, mv, rstd, xn_ready)
                        if is_first(i):
                            once()

            def step(it, inner=False):
                for n in range(NR):
                    if rel:
                        b, hs = relating(it, n)
                        if b is not None:
                            rotate(b, hs)
                    if attend(it):
                        maxima(attend(it), n)
                    b, m = turning(it, n)
                    if b is not None and not acts(m):
                        take_turned(dve, b, m, nc.vector.tensor_copy)
                    small(it, n)

            dve.wait_ge(k.loaded, k.loaded_count)
            Pipeline.run(dve, step)

        @block.gpsimd
        def _(pool):
            def root(i, mv_, veps_, rstd_, aggr_sem, veps_sem, rstd_sem):
                pool.wait_ge(aggr_sem, i + 1)
                nc.gpsimd.tensor_tensor(veps_[:, :], mv_[:, :, 1], k.eps[:, 0:TT], ALU.add).then_inc(veps_sem, 1)
                pool.wait_ge(veps_sem, i + 1)
                nc.gpsimd.tensor_tensor(rstd_[:, :], veps_[:, :], k.minus_half[:, 0:TT], ALU.pow).then_inc(rstd_sem, 1)

            def add_forms(b, hs):
                if hs >= RAW or later_than(b, 1):
                    pool.wait_ge(rr_lo_ready, b[0] * H + hs + 1 - RAW)
                pool.wait_ge(ur.emptied, ur.done(b, hs))
                nc.gpsimd.tensor_tensor(rr[:, hs % RAW, :], tmp[:, hs % 2, 0, :], tmp[:, hs % 2, 1, :], ALU.add)\
                    .then_inc(rr_ready, 1)

            def rest_of_terms(b, hs):
                pool.wait_ge(rr_hi_ready, b[0] * H + hs + 1)
                nc.gpsimd.tensor_tensor(rr_lo[:, hs % RRS, :], rr[:, hs % RAW, :], rr_hi[:, hs % RRS, :], ALU.subtract)\
                    .then_inc(rr_lo_ready, 1)

            def small(it, n):
                b, p, e = new(it), prep(it), finish(it)
                if p:
                    i, par = p
                    if n == 1:
                        pool.wait_ge(part1, i + 1)
                        nc.gpsimd.tensor_tensor(rest[:, :, :], qk[:, :, :], parts[:, par, 0, :, :], ALU.subtract)\
                            .then_inc(rest1, 1)
                    if n == 3:
                        pool.wait_ge(part2, i + 1)
                        nc.gpsimd.tensor_tensor(parts[:, par, 2, :, :], rest[:, :, :], parts[:, par, 1, :, :],
                                                ALU.subtract).then_inc(parts_ready, 1)
                if e:
                    i = e[0]
                    if rel and n == 7:
                        root(i, mv3, veps3, rstd3, s1_aggr, s1_veps, s1_rstd)
                    if not rel and n == 7:
                        pool.wait_ge(desk.emptied, desk.done(it, "o"))
                        nc.gpsimd.tensor_tensor(ob[:, :, :], ob[:, :, :], bp[:, :].unsqueeze(1)
                                                .to_broadcast([P, TT, C]), ALU.add).then_inc(bias_added, 1)
                        pool.wait_ge(bias_added, i + 1)
                        nc.gpsimd.tensor_tensor(x_b[:, i, :, :], x_b[:, i, :, :], ob[:, :, :], ALU.add)\
                            .then_inc(x_done, 1)
                if b:
                    if rel and n == 5:
                        root(b[0], mv2, veps2, rstd2, src_aggr, src_veps, src_rstd)
                    if n == (9 if rel else 8):
                        root(b[0], mv, veps, rstd, ln_aggr, ln_veps, ln_rstd)

            def step(it, inner=False):
                for n in range(NR):
                    if rel:
                        b, hs = relating(it, n)
                        if b is not None:
                            add_forms(b, hs)
                        b, hs = relating(it, n, AHEAD - 2)
                        if b is not None:
                            rest_of_terms(b, hs)
                    small(it, n)

            pool.wait_ge(k.loaded, k.loaded_count)
            pool.wait_ge(loaded, LOADS)
            Pipeline.run(pool, step)


def mixture(nc, tag, x_sb, k, w, x2t, gates):
    G, GT = 8, 4
    HB, OB = 4, 4
    LAG = 2
    CHUNK = 8
    with ExitStack() as ctx:
        a = Pool_(nc, ctx, tag)
        keys_hi, keys_lo = a.sb("keys_hi", [P, E1, P], F32R), a.sb("keys_lo", [P, E1, P], F32R)
        x_hi, x_lo = a.sb("x_hi", [P, 2, GT * P], F32R), a.sb("x_lo", [P, 2, GT * P], F32R)
        ht = a.sb("ht", [P, HB, GT * P])
        gg = a.sb("gg", [P, GT, E1])
        acc = a.sb("acc", [P, GT, C])
        hr = Ring(a.ps("hr", [P, HB, 512]), a.sem("hr_filled"), a.sem("hr_emptied"), E1, HB)
        our = Ring(a.ps("our", [P, OB, 512]), a.sem("our_filled"), a.sem("our_emptied"), E1, OB)
        gg_ready, keys_hi_ready, keys_lo_ready, x_hi_ready, x_lo_ready = [a.sem(n) for n in (
            "gg_ready", "keys_hi_ready", "keys_lo_ready", "x_hi_ready", "x_lo_ready")]
        block = ctx.enter_context(nc.Block())
        x_g = x_sb[:, :, :].rearrange("p (g t) c -> p g t c", t=GT)
        x2_g = x2t[:, :, :].rearrange("p (g t) c -> p g (t c)", t=GT)
        gates_g = gates[:, :, :].rearrange("p (g t) e -> p g t e", t=GT)

        @block.tensor
        def _(pe):
            def hidden(it, e):
                g, par = it
                if is_first(g) and e % CHUNK == 0:
                    pe.wait_ge(keys_lo_ready, e // CHUNK + 1)
                if e == 0:
                    pe.wait_ge(x_lo_ready, g + 1)
                pe.wait_ge(hr.emptied, hr.nth(it, e))
                out = hr.bank(it, e)
                nc.tensor.matmul(out, keys_hi[:, e, :], x_hi[:, par, :], start=True, stop=False)
                nc.tensor.matmul(out, keys_hi[:, e, :], x_lo[:, par, :], start=False, stop=False)
                nc.tensor.matmul(out, keys_lo[:, e, :], x_hi[:, par, :], start=False, stop=True)\
                    .then_inc(hr.filled, 1)

            def output(it, e):
                pe.wait_ge(our.emptied, our.nth(it, e))
                pe.wait_ge(hr.emptied, hr.done(it, e))
                for t in range(GT):
                    mm = nc.tensor.matmul(our.bank(it, e)[:, t * P:(t + 1) * P], ht[:, e % HB, t * P:(t + 1) * P],
                                          w.values[:, e, :], start=True, stop=True)
                mm.then_inc(our.filled, 1)

            def step(it, inner=False):
                for e in range(E1 + LAG):
                    if e < E1:
                        hidden(it, e)
                    if e >= LAG:
                        output(it, e - LAG)

            steps(pe, 0, G - 1, step)

        @block.scalar
        def _(act):
            act.sem_inc(hr.emptied, HB)

            def split_x(it):
                nc.scalar.activation(x_hi[:, it[1], :], x2_g[:, it[0], :], ACT.Copy).then_inc(x_hi_ready, 1)

            def step(it, inner=False):
                for e in range(E1):
                    act.wait_ge(hr.filled, hr.nth(it, e))
                    nc.scalar.activation(ht[:, e % HB, :], hr.bank(it, e), ACT.Relu).then_inc(hr.emptied, 1)
                    if e == 8 and within(it[0], 0, G - 2):
                        split_x(after(it))

            act.wait_ge(w.experts_loaded, w.experts_count)
            split_x((0, 0))
            for c in range(0, E1, CHUNK):
                nc.scalar.activation(keys_hi[:, c:c + CHUNK, :], w.keys[:, c:c + CHUNK, :], ACT.Copy)\
                    .then_inc(keys_hi_ready, 1)
            steps(act, 0, G - 1, step)

        @block.vector
        def _(dve):
            dve.sem_inc(our.emptied, OB)

            def step(it, inner=False):
                g = it[0]
                nc.vector.tensor_copy(gg[:, :, :], gates_g[:, g, :, :]).then_inc(gg_ready, 1)
                dve.wait_ge(gg_ready, g + 1)
                for e in range(E1):
                    dve.wait_ge(our.filled, our.nth(it, e))
                    for t in range(GT):
                        out = our.bank(it, e)[:, t * P:(t + 1) * P]
                        if e == 0:
                            last = nc.vector.tensor_scalar(acc[:, t, :], out, gg[:, t, e:e + 1], None, ALU.mult)
                        else:
                            if t == 0:
                                dve.wait_ge(our.emptied, our.done(it, e - 1))
                            last = nc.vector.scalar_tensor_tensor(acc[:, t, :], out, gg[:, t, e:e + 1], acc[:, t, :],
                                                                  ALU.mult, ALU.add)
                    last.then_inc(our.emptied, 1)
                dve.wait_ge(our.emptied, our.done(it, E1 - 1))
                nc.vector.scalar_tensor_tensor(x_g[:, g, :, :], acc[:, :, :], 0.5, x_g[:, g, :, :], ALU.mult, ALU.add)

            dve.wait_ge(w.experts_loaded, w.experts_count)
            for n, c in enumerate(range(0, E1, CHUNK)):
                dve.wait_ge(keys_hi_ready, n + 1)
                nc.vector.tensor_tensor(keys_lo[:, c:c + CHUNK, :], w.keys[:, c:c + CHUNK, :],
                                        keys_hi[:, c:c + CHUNK, :], ALU.subtract).then_inc(keys_lo_ready, 1)
            steps(dve, 0, G - 1, step)

        @block.gpsimd
        def _(pool):
            for g in range(G):
                pool.wait_ge(x_hi_ready, g + 1)
                nc.gpsimd.tensor_tensor(x_lo[:, g % 2, :], x2_g[:, g, :], x_hi[:, g % 2, :], ALU.subtract)\
                    .then_inc(x_lo_ready, 1)


class Constants:
    pass


class Weights:
    pass


def constants(nc, a, cst):
    k = Constants()
    table = a.sb("table", [P, cst.shape[1]])
    bf = a.sb("bf", [P, 2 * P], BF16)
    half = a.sb("half", [P, 16])
    k.idle = a.sb("idle", [P, 1])[:, :]
    k.ident = table[:, 0:P]
    k.iota40 = table[:, 2 * P:2 * P + CAP]
    k.iota8 = table[:, 2 * P + CAP:2 * P + CAP + E0]
    k.iota32 = table[:, 2 * P + CAP + E0:2 * P + CAP + E0 + E1]
    k.tri_bf, k.ones_bf = bf[:, 0:P], bf[:, P:2 * P]
    k.eps, k.minus_half = half[:, 0:8], half[:, 8:16]
    k.table, k.bf, k.half, k.source = table, bf, half, cst
    k.loaded, k.loaded_count = a.sem("loaded"), 5
    k.qs, k.ks = a.sb("qs", [ROWS, 2, H, T], BF16), a.sb("ks", [ROWS, 2, H, T], BF16)
    return k


def load_x(nc, k, x, x_sb, ws):
    with ExitStack() as ctx:
        a = Pool_(nc, ctx, "load")
        x_in, table_in, zeroed = a.sem("x_in"), a.sem("table_in"), a.sem("zeroed")
        block = ctx.enter_context(nc.Block())

        @block.sync
        def _(sp):
            sp.dma_start(k.table[:, :], k.source).then_inc(table_in, 16)
            sp.dma_start(x_sb[:, :, :], x.rearrange("b (t p) c -> p (b t) c", p=P)).then_inc(x_in, 16)
            sp.wait_ge(x_in, 16)

        @block.vector
        def _(dve):
            nc.vector.memset(k.ones_bf, 1.0).then_inc(k.loaded, 1)
            nc.vector.memset(k.eps, EPS).then_inc(k.loaded, 1)
            nc.vector.memset(k.minus_half, -0.5).then_inc(k.loaded, 1)
            dve.wait_ge(table_in, 16)
            nc.vector.tensor_copy(k.tri_bf, k.table[:, P:2 * P]).then_inc(k.loaded, 1)
            dve.sem_inc(k.loaded, 1)
            for tile, rows in ((k.qs, slice(32, 64)), (k.qs, slice(64, ROWS)), (k.ks, slice(32, 64))):
                nc.vector.memset(tile[rows, :, :, :].rearrange("p a h t -> p (a h t)"), 0.0)

        @block.gpsimd
        def _(pool):
            for n, (tile, rows) in enumerate(((ws, slice(32, 64)), (ws, slice(64, ROWS)), (k.ks, slice(64, ROWS)))):
                nc.gpsimd.memset(tile[rows, :, :, :].rearrange("p a h t -> p (a h t)"), 0.0).then_inc(zeroed, 1)
                pool.wait_ge(zeroed, n + 1)


def store_x(nc, x_sb, out):
    with ExitStack() as ctx:
        a = Pool_(nc, ctx, "store")
        stored = a.sem("stored")
        block = ctx.enter_context(nc.Block())

        @block.sync
        def _(sp):
            sp.dma_start(out.rearrange("b (t p) c -> p (b t) c", p=P), x_sb[:, :, :]).then_inc(stored, 16)
            sp.wait_ge(stored, 16)


def layer0_weights(nc, a, io, w):
    w.shared = a.sb("shared", [P, max(HID + KH * HID, E0 * KH * 2 * CAP)])
    w.rw1 = w.shared[:, 0:HID]
    w.rw2 = w.shared[:, HID:HID + KH * HID].rearrange("p (j h) -> p j h", j=KH)
    w.rw3 = a.sb("rw3", [P, KH, E0])
    w.rb1, w.rb2, w.rb3 = a.sb("rb1", [P, KH]), a.sb("rb2", [P, KH]), a.sb("rb3", [P, E0])
    w.ew1, w.ew2 = a.sb("ew1", [P, E0, HID]), a.sb("ew2", [P, E0, KH, C])
    w.eb1, w.eb2 = a.sb("eb1", [P, E0, KH]), a.sb("eb2", [P, E0])
    w.rw1_hi, w.rw1_lo = a.sb("rw1_hi", [P, HID], F32R), a.sb("rw1_lo", [P, HID], F32R)
    w.rw2_hi, w.rw2_lo = a.sb("rw2_hi", [P, KH, HID], F32R), a.sb("rw2_lo", [P, KH, HID], F32R)
    w.wp, w.wp_rest = a.sb("wp", [P, 2, C]), a.sb("wp_rest", [P, 2, C])
    w.wp_parts = a.sb("wp_parts", [P, 3, 2, C], BF16)
    w.router_hi_ready, w.router_lo_ready = a.sem("router_hi_ready"), a.sem("router_lo_ready")
    w.router_loaded, w.router_count = a.sem("router_loaded"), 16 * 6
    w.experts_loaded, w.experts_count = a.sem("experts_loaded"), 16 * 4

    def load(sp):
        for dst, src in ((w.rw1, io["rW1"]), (w.rb1[:, :], io["rb1"]), (w.rw2, io["rW2"]),
                         (w.rb2[:, :], io["rb2"]), (w.rw3[:, :, :], io["rW3"]),
                         (w.rb3[:, :], io["rb3"].partition_broadcast(P))):
            sp.dma_start(dst, src).then_inc(w.router_loaded, 16)
        for dst, src in ((w.ew1[:, :, :], io["eW1"]), (w.eb1[:, :, :], io["eb1"]), (w.eb2[:, :], io["eb2"]),
                         (w.ew2[:, :, :, :], io["eW2"])):
            sp.dma_start(dst, src).then_inc(w.experts_loaded, 16)
        sp.wait_ge(w.router_loaded, w.router_count)
        sp.wait_ge(w.experts_loaded, w.experts_count)

    w.load = load
    return w


def program(nc, io, stages=(1, 2, 3, 4, 5, 6)):
    with ExitStack() as ctx:
        a = Pool_(nc, ctx, "all")
        x_sb = a.sb("x", [P, B * TT, C])
        k = constants(nc, a, io["cst"])
        w = Weights()
        positions_weights(nc, a, io, w)
        load_x(nc, k, io["x"], x_sb, w.ws)
        with ExitStack() as layer:
            layer0_weights(nc, Pool_(nc, layer, "l0"), io, w)
            if 1 in stages:
                routed_ffn(nc, "f1", x_sb, k, w)
                w.load = None
            if 2 in stages:
                retention(nc, "r2", x_sb, k, io)
            if 3 in stages:
                routed_ffn(nc, "f3", x_sb, k, w)
        if 4 in stages or 5 in stages or 6 in stages:
            with ExitStack() as layer:
                layer1_weights(nc, Pool_(nc, layer, "l1"), io, w)
                if 4 in stages:
                    relative_ffn(nc, "f4", x_sb, k, w, io)
                if 5 in stages:
                    plain_attention(nc, "a5", x_sb, k, io)
                if 6 in stages:
                    relative_ffn(nc, "f6", x_sb, k, w, io)
        store_x(nc, x_sb, io["out"])



def shape_tables():
    i = np.arange(P)
    cst = np.concatenate([np.eye(P), (i[:, None] < i[None, :]).astype(float), np.tile(np.arange(CAP), (P, 1)),
                          np.tile(np.arange(E0), (P, 1)), np.tile(np.arange(E1), (P, 1))], 1)
    half = np.arange(0, HD, 2)
    freq = np.repeat(1.0 / 10000.0 ** (half / HD), 2)[None, :] * np.arange(T)[:, None]
    scale = np.repeat((half + 0.4 * HD) / (1.4 * HD), 2)[None, :] ** ((np.arange(T) - T // 2) / 512.0)[:, None]
    sign = np.tile([-1.0, 1.0], HD // 2)[None, :]
    rope = np.stack([np.cos(freq) * scale, np.sin(freq) * scale * sign, np.cos(freq) / scale,
                     np.sin(freq) / scale * sign])
    rope = np.repeat(rope.transpose(2, 0, 1), H, 0)
    gamma = 1.0 - 2.0 ** (-5.0 - np.arange(H))
    diff = np.arange(T)[None, :] - np.arange(P)[:, None]
    decay = np.where(diff[:, None, :] >= 0, gamma[None, :, None] ** np.maximum(diff, 0)[:, None, :], 0.0)
    decay = np.concatenate([decay, decay[:, :, 0:P]], 2) * HD ** -0.5
    group = np.kron(np.eye(H), np.full((HD, HD), 1.0 / HD))
    w = 1.0 / 10000.0 ** (np.arange(0, C, 2) / C)
    ang = w[:, None] * np.arange(T)[None, :]
    pe = np.concatenate([np.sin(ang), np.cos(ang)], 0)
    turn = np.stack([np.tile(np.cos(ang), (2, 1)), np.concatenate([np.sin(ang), -np.sin(ang)], 0)], 1)
    f = lambda v: np.ascontiguousarray(v, np.float32)
    return {"cst": f(cst), "rope": f(rope), "decay": f(decay), "group": f(group), "pe": f(pe), "turn": f(turn)}


def layouts(v):
    v = {n: np.asarray(a) for n, a in v.items()}
    swap = np.arange(C) ^ 1
    dh = np.arange(C).reshape(H, HD).T.reshape(-1)
    qkv0 = v["L0_attn_w_qkv"].reshape(3, C, C)
    qkv1 = v["L1_attn_w_qkv"].reshape(3, C, C)
    col = lambda a: a.reshape(-1, P).T
    out = {
        "x": v["L0_attn_x"],
        "rW1": v["L0_ffn_rW1"], "rb1": col(v["L0_ffn_rb1"]),
        "rW2": v["L0_ffn_rW2"].reshape(KH, P, HID).transpose(1, 0, 2), "rb2": col(v["L0_ffn_rb2"]),
        "rW3": v["L0_ffn_rW3"].reshape(KH, P, E0).transpose(1, 0, 2), "rb3": v["L0_ffn_rb3"],
        "eW1": v["L0_ffn_eW1"].transpose(1, 0, 2),
        "eb1": v["L0_ffn_eb1"].reshape(E0, KH, P).transpose(2, 0, 1),
        "eW2": v["L0_ffn_eW2"].reshape(E0, KH, P, C).transpose(2, 0, 1, 3), "eb2": v["L0_ffn_eb2"].T,
        "w0": np.concatenate([qkv0[0][dh].T, qkv0[0][swap][dh].T, qkv0[1][dh].T, qkv0[1][swap][dh].T, v["L0_attn_w_gated"].T,
                              qkv0[2].T], 1),
        "w0p": v["L0_attn_w_proj"].T, "gnw": col(v["L0_attn_gn_weight"]), "gnb": col(v["L0_attn_gn_bias"]),
        "w5": np.concatenate([qkv1[0][dh].T, qkv1[1][dh].T, qkv1[2].T], 1), "w5p": v["L1_attn_w_proj"].T,
        "b5p": v["L1_attn_b_proj"],
        "w4": np.concatenate([v["L1_ffn_wq"][:, dh], v["L1_ffn_wk"][:, dh], v["L1_ffn_wv"]], 1), "w4p": v["L1_ffn_wo"],
        "wp": np.stack([v["L1_ffn_wp"].T[dh], np.roll(v["L1_ffn_wp"], C // 2, 0).T[dh]], 1),
        "ln": np.stack([v["L1_ffn_ln1_g"], v["L1_ffn_ln1_b"], v["L1_ffn_ln2_g"], v["L1_ffn_ln2_b"]], 1),
        "selw": v["L1_ffn_sel_w"], "keys": v["L1_ffn_keys"].transpose(1, 0, 2),
        "values": v["L1_ffn_values"].transpose(1, 0, 2),
    }
    return out


def kernel(**inputs):
    import concourse.bacc as _bacc
    from concourse.bass_utils import run_bass_kernel_spmd as _run

    nc = _bacc.Bacc("TRN2", target_bir_lowering=False, num_devices=1)
    arrays, io = {}, {}
    for name, a in {**layouts(inputs), **shape_tables()}.items():
        arrays[f"in_{name}"] = np.ascontiguousarray(a)
        io[name] = nc.dram_tensor(f"in_{name}", a.shape, mybir.dt.from_np(a.dtype), kind="ExternalInput").ap()
    io["out"] = nc.dram_tensor("out", (B, T, C), F32, kind="ExternalOutput").ap()
    program(nc, io)
    return _run(nc, [arrays], core_ids=[0]).results[0]["out"]
```
